# Optimizing a Trainium2 kernel written in Bass

```python
import numpy as np
import jax
import jax.numpy as jnp

def _softmax(x, axis=-1):
    return jax.nn.softmax(x, axis=axis)

def _gelu(x):
    return jax.nn.gelu(x, approximate=True)

def _silu(x):
    return jax.nn.silu(x)

def _sigmoid(x):
    return jax.nn.sigmoid(x)

def _layernorm(x, axis=-1, eps=1e-05):
    m = jnp.mean(x, axis=axis, keepdims=True)
    v = jnp.var(x, axis=axis, keepdims=True)
    return (x - m) / jnp.sqrt(v + eps)

def _scatter_add(tgt, idx, src, axis=0):
    return tgt.at[idx].add(src)

def _segment_sum(src, seg, n):
    return jax.ops.segment_sum(src, seg, n)
kernel_name = 'mk_gnn_resnorm_d4_gnn_r8_075bfc'

def setup_inputs(seed: int=0):
    np.random.seed(seed)
    _w = jnp.asarray

    def _rec_inputs():
        import jax
        import jax.numpy as jnp
        _gk = jax.random.key(seed)
        x = -0.000202 + 1 * jax.random.normal(jax.random.fold_in(_gk, 1), (12500, 64), jnp.float32)
        src = jax.random.randint(jax.random.fold_in(_gk, 2), (400000,), 0, 12500, jnp.int32)
        dst = jnp.minimum((12500 * jax.random.uniform(jax.random.fold_in(_gk, 3), (400000,)) ** 2.0).astype(jnp.int32), 99999)
        _o = jnp.argsort(dst, stable=True)
        src = src[_o]
        dst = dst[_o]
        edge_type_65 = jax.random.randint(jax.random.fold_in(_gk, 14), (400000,), 0, 65, jnp.int32)
        return (x, src, dst, edge_type_65)
    x, src, dst, edge_type_65 = _rec_inputs()

    def _L0_gnn_setup():
        import jax, jax.numpy as jnp
        import numpy as np
        N_NODES = 12500
        N_EDGES = 200000
        D_IN = 64
        D_OUT = 64
        key = jax.random.key(seed)
        k_x, k_e, k_w, k_b = jax.random.split(key, 4)
        x = jax.random.normal(k_x, (N_NODES, D_IN), dtype=jnp.float32)
        edge_index = jax.random.randint(k_e, (2, N_EDGES), 0, N_NODES, dtype=jnp.int64)
        std = 0.02 * np.sqrt(2.0 / (2 * D_IN + D_OUT))
        weight = jax.random.normal(k_w, (2 * D_IN, D_OUT), dtype=jnp.float32) * std
        bias = jnp.zeros((1, D_OUT), dtype=jnp.float32)
        return {'x': x, 'weight': weight, 'bias': bias, 'edge_index': edge_index}
    _L0_gnn_all = _L0_gnn_setup()
    _L0_gnn_in = {k: v for k, v in _L0_gnn_all.items() if k in ('weight', 'bias')}
    del _L0_gnn_all

    def _L1_gnn_setup():
        import jax, jax.numpy as jnp
        import numpy as np
        N = 6250
        D = 64
        E = 100000
        key = jax.random.key(seed)
        k1, k2, k3, k4 = jax.random.split(key, 4)
        f = jax.random.normal(k1, (N, D), dtype=jnp.float32)
        norm = jax.random.uniform(k2, (N, 1), dtype=jnp.float32)
        src = jax.random.randint(k3, (E,), 0, N, dtype=jnp.int64)
        dst = jax.random.randint(k4, (E,), 0, N, dtype=jnp.int64)
        return {'f': f, 'norm': norm, 'src': src, 'dst': dst, 'num_nodes': N}
    _L1_gnn_all = _L1_gnn_setup()
    _L1_gnn_in = {k: v for k, v in _L1_gnn_all.items() if k in ()}
    del _L1_gnn_all

    def _L2_gnn_setup():
        import jax, jax.numpy as jnp
        import numpy as np
        N, E, D, R, L = (6250, 75000, 64, 65, 2)

        def _rgcn_conv(x, src, dst, edge_type, W_r, W_root, b):
            n, d = x.shape
            r = W_r.shape[0]
            seg = dst * r + edge_type
            msg = x[src]
            agg = jax.ops.segment_sum(msg, seg, num_segments=n * r).reshape(n, r, d)
            cnt = jax.ops.segment_sum(jnp.ones((msg.shape[0],), x.dtype), seg, num_segments=n * r).reshape(n, r, 1)
            mean = agg / jnp.maximum(cnt, 1.0)
            out = jnp.einsum('nrd,rdk->nk', mean, W_r)
            return out + x @ W_root + b
        key = jax.random.key(seed)
        ks = jax.random.split(key, 10)
        x = jax.random.normal(ks[0], (N, D), dtype=jnp.float32)
        edge_index = jax.random.randint(ks[1], (2, E), 0, N, dtype=jnp.int64)
        edge_type = jax.random.randint(ks[2], (E,), 0, R, dtype=jnp.int64)
        s = 1.0 / np.sqrt(D)
        W = jax.random.normal(ks[3], (L, R, D, D), dtype=jnp.float32) * s
        root = jax.random.normal(ks[4], (L, D, D), dtype=jnp.float32) * s
        bias = jax.random.normal(ks[5], (L, D), dtype=jnp.float32) * 0.01
        res_W = jax.random.normal(ks[6], (L, D, D), dtype=jnp.float32) * s
        res_b = jax.random.normal(ks[7], (L, D), dtype=jnp.float32) * 0.01
        return {'x': x, 'edge_index': edge_index, 'edge_type': edge_type, 'W': W, 'root': root, 'bias': bias, 'res_W': res_W, 'res_b': res_b}
    _L2_gnn_all = _L2_gnn_setup()
    _L2_gnn_in = {k: v for k, v in _L2_gnn_all.items() if k in ('W', 'root', 'bias', 'res_W', 'res_b')}
    del _L2_gnn_all

    def _L3_gnn_setup():
        import jax, jax.numpy as jnp
        import numpy as np
        EPS = 1e-12

        def _l2_normalize(x):
            n = jnp.linalg.norm(x, axis=-1, keepdims=True)
            return x / jnp.maximum(n, EPS)
        key = jax.random.key(seed)
        k1, k2, k3 = jax.random.split(key, 3)
        N, E, D = (12500, 150000, 64)
        feat = jax.random.normal(k1, (N, D), dtype=jnp.float32)
        beta = jnp.ones((1,), dtype=jnp.float32)
        src = jax.random.randint(k2, (E,), 0, N, dtype=jnp.int32)
        dst = jax.random.randint(k3, (E,), 0, N, dtype=jnp.int32)
        return {'feat': feat, 'beta': beta, 'src': src, 'dst': dst}
    _L3_gnn_all = _L3_gnn_setup()
    _L3_gnn_in = {k: v for k, v in _L3_gnn_all.items() if k in ('beta',)}
    del _L3_gnn_all
    return {'x': x, 'src': src, 'dst': dst, 'edge_type_65': edge_type_65, 'L0_gnn_weight': _L0_gnn_in['weight'], 'L0_gnn_bias': _L0_gnn_in['bias'], 'L2_gnn_W': _L2_gnn_in['W'], 'L2_gnn_root': _L2_gnn_in['root'], 'L2_gnn_bias': _L2_gnn_in['bias'], 'L2_gnn_res_W': _L2_gnn_in['res_W'], 'L2_gnn_res_b': _L2_gnn_in['res_b'], 'L3_gnn_beta': _L3_gnn_in['beta']}

def reference(x, src, dst, edge_type_65, L0_gnn_weight, L0_gnn_bias, L2_gnn_W, L2_gnn_root, L2_gnn_bias, L2_gnn_res_W, L2_gnn_res_b, L3_gnn_beta):
    import jax
    import jax.numpy as jnp

    def _L0_gnn_ref(x, weight, bias, edge_index):
        import jax, jax.numpy as jnp
        import numpy as np
        N_NODES = 12500
        N_EDGES = 200000
        D_IN = 64
        D_OUT = 64
        row = edge_index[0]
        col = edge_index[1]
        n = x.shape[0]
        support = jax.ops.segment_sum(x[col], row, num_segments=n)
        deg = jax.ops.segment_sum(jnp.ones(row.shape[0], dtype=x.dtype), row, num_segments=n)
        support = support / jnp.maximum(deg, 1.0)[:, None]
        h = jnp.concatenate([x, support], axis=1)
        out = h @ weight + bias
        return out

    def _L1_gnn_ref(f, norm, src, dst, num_nodes):
        import jax, jax.numpy as jnp
        import numpy as np
        N = 6250
        D = 64
        E = 100000
        w = norm[src] * norm[dst]
        h = f[src] * w
        s = jax.ops.segment_max(h, dst, num_segments=num_nodes)
        has_in = jax.ops.segment_sum(jnp.ones_like(dst, dtype=jnp.float32), dst, num_segments=num_nodes) > 0
        return jnp.where(has_in[:, None], s, 0.0)

    def _L2_gnn_ref(x, edge_index, edge_type, W, root, bias, res_W, res_b):
        import jax, jax.numpy as jnp
        import numpy as np
        N, E, D, R, L = (6250, 75000, 64, 65, 2)

        def _rgcn_conv(x, src, dst, edge_type, W_r, W_root, b):
            n, d = x.shape
            r = W_r.shape[0]
            seg = dst * r + edge_type
            msg = x[src]
            agg = jax.ops.segment_sum(msg, seg, num_segments=n * r).reshape(n, r, d)
            cnt = jax.ops.segment_sum(jnp.ones((msg.shape[0],), x.dtype), seg, num_segments=n * r).reshape(n, r, 1)
            mean = agg / jnp.maximum(cnt, 1.0)
            out = jnp.einsum('nrd,rdk->nk', mean, W_r)
            return out + x @ W_root + b
        src, dst = (edge_index[0], edge_index[1])
        h = x
        for l in range(W.shape[0]):
            conv = _rgcn_conv(h, src, dst, edge_type, W[l], root[l], bias[l])
            conv = jax.nn.relu(conv)
            res = jax.nn.relu(h @ res_W[l] + res_b[l])
            h = conv + res
        return h

    def _L3_gnn_ref(feat, beta, src, dst):
        import jax, jax.numpy as jnp
        import numpy as np
        EPS = 1e-12

        def _l2_normalize(x):
            n = jnp.linalg.norm(x, axis=-1, keepdims=True)
            return x / jnp.maximum(n, EPS)
        N = feat.shape[0]
        nh = _l2_normalize(feat)
        e = beta[0] * jnp.sum(nh[src] * nh[dst], axis=-1)
        emax = jax.ops.segment_max(e, dst, num_segments=N)
        emax = jnp.where(jnp.isfinite(emax), emax, 0.0)
        p = jnp.exp(e - emax[dst])
        psum = jax.ops.segment_sum(p, dst, num_segments=N)
        p = p / jnp.maximum(psum[dst], EPS)
        msg = feat[src] * p[:, None]
        out = jax.ops.segment_sum(msg, dst, num_segments=N)
        return out
    edge_index = jnp.stack([src, dst])
    deg = jnp.maximum(jax.ops.segment_sum(jnp.ones(dst.shape, jnp.float32), dst, num_segments=12500), 1.0)
    deg_isqrt = deg ** (-0.5)
    x = _layernorm(x + _L0_gnn_ref(x, L0_gnn_weight, L0_gnn_bias, edge_index), axis=-1)
    x = _layernorm(x + _L1_gnn_ref(x, deg_isqrt[:, None], src, dst, 12500), axis=-1)
    x = _layernorm(x + _L2_gnn_ref(x, edge_index, edge_type_65, L2_gnn_W, L2_gnn_root, L2_gnn_bias, L2_gnn_res_W, L2_gnn_res_b), axis=-1)
    x = _layernorm(x + _L3_gnn_ref(x, L3_gnn_beta, src, dst), axis=-1)
    return x

_drawn_inputs = setup_inputs


def setup_inputs(seed=0):
    import zlib

    import numpy as np

    out = dict(_drawn_inputs(seed))
    spreads = {'L0_gnn_bias': (0.0, 0.1)}
    factors = {'L0_gnn_weight': 3.547, 'L2_gnn_bias': 8.0, 'L2_gnn_res_b': 8.0}
    for name, (base, spread) in spreads.items():
        noise = np.random.default_rng([zlib.crc32(name.encode()), seed]).standard_normal(out[name].shape)
        drawn = base * np.exp(spread * noise) if base else spread * noise
        out[name] = jnp.asarray(drawn.astype(out[name].dtype))
    for name, factor in factors.items():
        out[name] = (out[name] * factor).astype(out[name].dtype)
    return out
```

```python
from contextlib import ExitStack

import numpy as np

import concourse.bass as bass
import concourse.mybir as mybir
from concourse.alu_op_type import AluOpType as ALU

F32 = mybir.dt.float32
BF16 = mybir.dt.bfloat16
I32 = mybir.dt.int32
ACT = mybir.ActivationFunctionType
AX = mybir.AxisListType
DVE_ONLY = [mybir.EngineType.DVE]
PE_ONLY = [mybir.EngineType.PE]

P = 128
NODES, EDGES, DIM, TYPES = 12500, 400000, 64, 65
BLOCKS = -(-NODES // P)
PADDED = BLOCKS * P
TILES = EDGES // P
U = 8
HALF = U // 2
ITEM_TURNS = -(-(TILES + BLOCKS - 1) // U)
ITEMS = ITEM_TURNS * U
CHUNKS = -(-ITEMS // P)
ITEMS_PAD = CHUNKS * P
TILE_TURNS = -(-TILES // U)
TILES_RUN = TILE_TURNS * U
TCHUNKS = -(-TILES // P)
TILES_PAD = TCHUNKS * P
FLAT = EDGES // 125
TROW = TILES // 125
G = 7
BLOCK_TURNS = BLOCKS // G
W65 = DIM + 1
TRASH = PADDED
ACC_ROWS = PADDED + P
BIG = 1e30
LN_EPS = 1e-5
TINY = 1e-12
SPAN = TYPES * DIM
BROW = 66

assert EDGES % P == 0 and TILES % 125 == 0 and BLOCKS % G == 0


def hold(engine, c):
    engine.sem_inc(c.held, 1)


def link_on(engine, sem):
    done = [0]

    def link(instruction):
        done[0] += 1
        instruction.then_inc(sem, 1)
        engine.wait_ge(sem, done[0])
        return instruction
    return link


class Stage:

    made = 0

    def __init__(self, nc):
        self.nc, self.stack = nc, ExitStack()
        Stage.made += 1
        self.tag = f"_{Stage.made}"
        self.semaphores = []

    def __enter__(self):
        self.stack.__enter__()
        return self

    def __exit__(self, *error):
        self.stack.__exit__(*error)
        if self.semaphores:
            self.nc.clear_and_free_semaphores(self.semaphores)
            self.nc.all_engine_barrier(sem_only=True)

    def sb(self, name, shape, dt):
        return self.stack.enter_context(self.nc.sbuf_tensor(name + self.tag, shape, dt))

    def ps(self, name, shape, dt):
        return self.stack.enter_context(self.nc.psum_tensor(name + self.tag, shape, dt))

    def sem(self, name):
        self.semaphores.append(self.nc.alloc_semaphore(name=name + self.tag))
        return self.semaphores[-1]

    def sems(self, *names):
        return [self.sem(name) for name in names]

    def block(self):
        return self.stack.enter_context(self.nc.Block())


class TurnCount:

    def __init__(self, engine, sem, turn, each):
        self.engine, self.sem, self.base, self.each, self.n = engine, sem, turn * each, each, 0

    def mark(self, instruction):
        self.n += 1
        instruction.then_inc(self.sem, 1)
        return self.n

    def wait(self, n):
        self.engine.wait_ge(self.sem, self.base + n)

    def close(self):
        assert self.n == self.each, (self.n, self.each)


def node_view(table, width):
    return table.rearrange("(p b) d -> p b d", p=P)


class Scratch:

    def __init__(self, nc):
        def dram(name, shape, dt):
            return nc.dram_tensor(name, shape, dt, kind="Internal").ap()

        self.e_src = dram("e_src", [EDGES], I32)
        self.e_dst = dram("e_dst", [EDGES], I32)
        self.e_type = dram("e_type", [EDGES], I32)
        self.e_prev = dram("e_prev", [EDGES + 1], I32)
        self.block_x65 = dram("block_x65", [CHUNKS, P], I32)
        self.block_x128 = dram("block_x128", [CHUNKS, P], I32)
        self.i_rel = dram("i_rel", [P, ITEMS_PAD], F32)
        self.i_row = dram("i_row", [P, ITEMS_PAD], F32)
        self.i_type = dram("i_type", [P, ITEMS_PAD], F32)
        self.i_rel_row = dram("i_rel_row", [P, ITEMS_PAD], F32)
        self.i_cut = dram("i_cut", [ITEMS_PAD * P + 1], F32)
        self.i_off = dram("i_off", [ITEMS_PAD, P], F32)
        self.i_srcrow = dram("i_srcrow", [ITEMS_PAD, P], F32)
        self.t_row = dram("t_row", [P, TILES_PAD], F32)
        self.t_cut = dram("t_cut", [TILES_RUN * P], F32)
        self.acc = [dram(f"acc{k}", [ACC_ROWS, W65], F32) for k in range(U)]
        self.x = dram("x_state", [PADDED, DIM], F32)
        self.h = dram("h_state", [PADDED, DIM], F32)
        self.res = dram("res_state", [PADDED, DIM], F32)
        self.out_rel = dram("out_rel", [PADDED, W65], F32)
        self.counts = dram("counts", [P, BLOCKS * W65], F32)
        self.degree = dram("degree", [P, BLOCKS], F32)
        self.scanned = dram("scanned", [P * TILES_RUN, DIM], F32)
        self.g = dram("g_table", [PADDED, DIM], F32)
        self.i_weight = dram("i_weight", [P, ITEMS_PAD], F32)
        self.rel_table = dram("rel_table", [PADDED * TYPES, DIM], F32)
        self.nx = dram("nx_table", [PADDED, 2 * DIM], F32)
        self.rows_kept = dram("rows_kept", [P, ITEMS * DIM], F32)
        self.i_score = dram("i_score", [P, ITEMS_PAD], F32)


class Consts:

    def __init__(self, nc, ctx):
        def sb(name, shape, dt):
            return ctx.enter_context(nc.sbuf_tensor(name, shape, dt))

        self.held = ctx.enter_context(nc.semaphore("held"))
        self.iota_i = sb("iota_i", [P, P], I32)
        self.lane_i = sb("lane_i", [P, 1], I32)
        self.iota = sb("iota", [P, P], F32)
        self.iota_b = sb("iota_b", [P, P], BF16)
        self.lane = sb("lane", [P, 1], F32)
        self.ident = sb("ident", [P, P], F32)
        self.ident_b = sb("ident_b", [P, P], BF16)
        self.before = sb("before", [P, P], BF16)
        self.above = sb("above", [P, P], F32)
        self.upto = sb("upto", [P, P], F32)
        self.ones = sb("ones", [P, P], F32)
        self.eps = sb("eps", [P, 1], F32)
        self.block_row = sb("block_row", [1, ITEMS_PAD], I32)


def make_consts(nc, c):
    with Stage(nc) as st:
        iota_done, const_done = st.sems("iota_done", "const_done")
        block = st.block()
        @block.gpsimd
        def _(pool):
            nc.gpsimd.iota(c.iota_i[:, :], pattern=[[1, P]], base=0, channel_multiplier=0).then_inc(iota_done, 1)
            nc.gpsimd.iota(c.lane_i[:, :], pattern=[[0, 1]], base=0, channel_multiplier=1).then_inc(iota_done, 1)

        @block.vector
        def _(dve):
            link = link_on(dve, const_done)
            dve.wait_ge(iota_done, 2)
            link(nc.vector.tensor_copy(c.iota[:, :], c.iota_i[:, :]))
            link(nc.vector.tensor_copy(c.iota_b[:, :], c.iota_i[:, :]))
            link(nc.vector.tensor_copy(c.lane[:, :], c.lane_i[:, :]))
            for out, op in ((c.ident, ALU.is_equal), (c.ident_b, ALU.is_equal), (c.before, ALU.is_lt),
                            (c.above, ALU.is_gt), (c.upto, ALU.is_ge)):
                link(nc.vector.tensor_scalar(out[:, :], c.iota[:, :], c.lane[:, 0:1], None, op))
            link(nc.vector.memset(c.ones[:, :], 1.0))
            link(nc.vector.memset(c.eps[:, :], LN_EPS))


def copy_edges(nc, s, src, dst, edge_type):
    with Stage(nc) as st:
        minus = st.sb("minus", [1, 1], I32)
        minus_set, edges_in = st.sems("minus_set", "edges_in")
        block = st.block()
        @block.vector
        def _(dve):
            nc.vector.memset(minus[:, :], -1).then_inc(minus_set, 1)

        @block.sync
        def _(sp):
            def rows(t):
                return t.rearrange("(p k) -> p k", p=125)
            sp.dma_start(rows(s.e_src), rows(src)).then_inc(edges_in, 16)
            sp.dma_start(rows(s.e_dst), rows(dst)).then_inc(edges_in, 16)
            sp.dma_start(rows(s.e_type), rows(edge_type)).then_inc(edges_in, 16)
            sp.dma_start(rows(s.e_prev[1:EDGES + 1]), rows(dst)).then_inc(edges_in, 16)
            sp.wait_ge(minus_set, 1)
            sp.dma_start(s.e_prev[0:1].rearrange("(p k) -> p k", p=1), minus[:, :]).then_inc(edges_in, 16)
            sp.wait_ge(edges_in, 80)


def map_items(nc, s, c, tile_of, rel_of):
    with Stage(nc) as st:
        last_dst = st.sb("last_dst", [125, TROW], I32)
        tile_id = st.sb("tile_id", [125, TROW], I32)
        key = st.sb("key", [125, TROW], I32)
        key_part = st.sb("key_part", [125, TROW], I32)
        key_hi = st.sb("key_hi", [125, TROW], F32)
        key_lo = st.sb("key_lo", [125, TROW], F32)
        hot_hi = st.sb("hot_hi", [125, TROW, CHUNKS], BF16)
        hot_lo = st.sb("hot_lo", [125, TROW, P], BF16)
        marks = st.sb("marks", [CHUNKS, P], F32)
        upto_here = st.sb("upto_here", [CHUNKS, P], F32)
        tiles_before = st.sb("tiles_before", [CHUNKS, P], F32)
        item_id_i = st.sb("item_id_i", [P, CHUNKS], I32)
        item_id = st.sb("item_id", [P, CHUNKS], F32)
        tiles_t = st.sb("tiles_t", [P, CHUNKS], F32)
        past_end = st.sb("past_end", [P, CHUNKS], F32)
        block_f = st.sb("block_f", [P, CHUNKS], F32)
        block_i = st.sb("block_i", [CHUNKS, 2, P], I32)
        ps_marks = st.ps("ps_marks", [CHUNKS, P], F32)
        ps_sum = st.ps("ps_sum", [CHUNKS, 1], F32)
        ps_t = st.ps("ps_t", [P, CHUNKS], F32)
        ps_b = st.ps("ps_b", [CHUNKS, P], F32)
        last_in, ids_set, map_dve, hot_set, marked, scan_set, summed, before_set, turned, blocks_set, blocks_turned, row_set, row_out = st.sems("last_in", "ids_set", "map_dve", "hot_set", "marked", "scan_set", "summed", "before_set", "turned", "blocks_set", "blocks_turned", "row_set", "row_out")
        block = st.block()

        @block.sync
        def _(sp):
            last = s.e_dst.rearrange("(p j e) -> p j e", j=TROW, e=P)[:, :, P - 1]
            with nc.allow_non_contiguous_dma(reason="one value of each tile"):
                sp.dma_start(last_dst[:, :], last).then_inc(last_in, 16)
            sp.wait_ge(row_set, 1)
            sp.dma_start(s.block_x65, block_i[:, 0, :]).then_inc(row_out, 16)
            sp.dma_start(s.block_x128, block_i[:, 1, :]).then_inc(row_out, 16)
            sp.wait_ge(row_out, 32)
            sp.dma_start(c.block_row[:, :], s.block_x65.rearrange("(o a) b -> o (a b)", o=1)).then_inc(row_out, 16)
            sp.wait_ge(row_out, 48)

        @block.gpsimd
        def _(pool):
            nc.gpsimd.iota(tile_id[:, :], pattern=[[1, TROW]], base=0, channel_multiplier=TROW).then_inc(ids_set, 1)
            nc.gpsimd.iota(item_id_i[:, :], pattern=[[P, CHUNKS]], base=0, channel_multiplier=1).then_inc(ids_set, 1)

        @block.vector
        def _(dve):
            link = link_on(dve, map_dve)
            dve.wait_ge(last_in, 16)
            dve.wait_ge(ids_set, 2)
            link(nc.vector.tensor_scalar(key[:, :], last_dst[:, :], 7, None, ALU.logical_shift_right))
            link(nc.vector.tensor_tensor(key[:, :], key[:, :], tile_id[:, :], ALU.add))
            link(nc.vector.tensor_scalar(key_part[:, :], key[:, :], 7, None, ALU.logical_shift_right))
            link(nc.vector.tensor_copy(key_hi[:, :], key_part[:, :]))
            link(nc.vector.tensor_scalar(key_part[:, :], key[:, :], P - 1, None, ALU.bitwise_and))
            link(nc.vector.tensor_copy(key_lo[:, :], key_part[:, :]))
            link(nc.vector.tensor_tensor(hot_hi[:, :, :], key_hi[:, :, None].to_broadcast([125, TROW, CHUNKS]),
                                         c.iota[0:125, None, 0:CHUNKS].to_broadcast([125, TROW, CHUNKS]), ALU.is_equal))
            nc.vector.tensor_tensor(hot_lo[:, :, :], key_lo[:, :, None].to_broadcast([125, TROW, P]),
                                    c.iota[0:125, None, :].to_broadcast([125, TROW, P]), ALU.is_equal).then_inc(hot_set, 1)
            dve.wait_ge(marked, 1)
            link(nc.vector.tensor_copy(marks[:, :], ps_marks[:, :]))
            nc.vector.tensor_tensor_scan(upto_here[:, :], c.ones[0:CHUNKS, :], marks[:, :], 0.0,
                                         ALU.mult, ALU.add).then_inc(scan_set, 1)
            dve.wait_ge(scan_set, 1)
            dve.wait_ge(summed, 1)
            link(nc.vector.tensor_tensor(tiles_before[:, :], upto_here[:, :], marks[:, :], ALU.subtract))
            nc.vector.tensor_scalar(tiles_before[:, :], tiles_before[:, :], ps_sum[:, 0:1], None,
                                    ALU.add).then_inc(before_set, 1)
            dve.wait_ge(turned, 1)
            link(nc.vector.tensor_copy(tiles_t[:, :], ps_t[:, :]))
            link(nc.vector.tensor_copy(item_id[:, :], item_id_i[:, :]))
            link(nc.vector.tensor_tensor(block_f[:, :], item_id[:, :], tiles_t[:, :], ALU.subtract))
            link(nc.vector.tensor_scalar(past_end[:, :], tiles_t[:, :], float(TILES), 1000.0, ALU.is_ge, ALU.mult))
            link(nc.vector.tensor_tensor(rel_of[:, :], block_f[:, :], past_end[:, :], ALU.add))
            link(nc.vector.tensor_scalar(rel_of[:, :], rel_of[:, :], float(P), None, ALU.mult))
            link(nc.vector.tensor_scalar(tile_of[:, :], tiles_t[:, :], float(TILES - 1), None, ALU.min))
            nc.vector.tensor_scalar(block_f[:, :], block_f[:, :], float(BLOCKS - 1), None, ALU.min).then_inc(blocks_set, 1)
            dve.wait_ge(blocks_turned, 1)
            nc.vector.tensor_scalar(block_i[:, 0, :], ps_b[:, :], float(W65), None, ALU.mult)
            nc.vector.tensor_scalar(block_i[:, 1, :], ps_b[:, :], float(P), None, ALU.mult).then_inc(row_set, 1)

        @block.tensor
        def _(pe):
            pe.wait_ge(hot_set, 1)
            for j in range(TROW):
                last = nc.tensor.matmul(ps_marks[:, :], hot_hi[:, j, :], hot_lo[:, j, :],
                                        start=(j == 0), stop=(j == TROW - 1))
            last.then_inc(marked, 1)
            pe.wait_ge(scan_set, 1)
            nc.tensor.matmul(ps_sum[:, :], c.above[0:CHUNKS, 0:CHUNKS], upto_here[:, P - 1:P],
                             start=True, stop=True).then_inc(summed, 1)
            pe.wait_ge(before_set, 1)
            nc.tensor.transpose(ps_t[:, :], tiles_before[:, :], c.ident[0:CHUNKS, 0:CHUNKS]).then_inc(turned, 1)
            pe.wait_ge(blocks_set, 1)
            nc.tensor.transpose(ps_b[:, :], block_f[:, :], c.ident[:, :]).then_inc(blocks_turned, 1)


def turn_chunks(nc, c, source, out, chunks):
    with Stage(nc) as st:
        ps = st.ps("ps_turn", [P, 2, 4 * P], F32)
        turned, kept = st.sems("turned", "kept")
        block = st.block()
        groups = [range(a, min(a + 4, chunks)) for a in range(0, chunks, 4)]

        @block.tensor
        def _(pe):
            for n, group in enumerate(groups):
                if n >= 2:
                    pe.wait_ge(kept, n - 1)
                for k, chunk in enumerate(group):
                    last = nc.tensor.transpose(ps[:, n % 2, k * P:(k + 1) * P], source[:, chunk, :], c.ident[:, :])
                last.then_inc(turned, 1)

        @block.vector
        def _(dve):
            for n, group in enumerate(groups):
                dve.wait_ge(turned, n + 1)
                nc.vector.tensor_copy(out[:, group[0] * P:(group[-1] + 1) * P],
                                      ps[:, n % 2, 0:len(group) * P]).then_inc(kept, 1)


def item_tables(nc, s, c):
    with Stage(nc) as st:
        tile_of = st.sb("tile_of", [P, CHUNKS], I32)
        rel_of = st.sb("rel_of", [P, CHUNKS], F32)
        map_items(nc, s, c, tile_of, rel_of)
        shape = [P, CHUNKS, P]
        flat = "p c e -> p (c e)"
        with Stage(nc) as st:
            raw = st.sb("raw", [P, 2, CHUNKS, P], I32)
            val = st.sb("val", [P, CHUNKS, P], F32)
            off = st.sb("off", [P, CHUNKS, P], F32)
            other = st.sb("other", [P, CHUNKS, P], F32)
            table = st.sb("table", [P, ITEMS_PAD], F32)
            end = st.sb("end", [1, 1], F32)
            with Stage(nc) as st:
                dst_in, prev_in, dst_dve, cut_set, cut_out = st.sems("dst_in", "prev_in", "dst_dve", "cut_set", "cut_out")
                block = st.block()
                @block.gpsimd
                def _(pool):
                    for which, table_, sem in ((0, s.e_dst, dst_in), (1, s.e_prev[0:EDGES], prev_in)):
                        rows = table_.rearrange("(t e) -> t e", e=P)
                        for k in range(CHUNKS):
                            pool.indirect_dma_start(raw[:, which, k, :], None, rows,
                                                    bass.IndirectOffsetOnAxis(ap=tile_of[:, k:k + 1], axis=0)).then_inc(sem, 16)

                @block.vector
                def _(dve):
                    link = link_on(dve, dst_dve)
                    link(nc.vector.memset(end[:, :], 0.0))
                    dve.wait_ge(dst_in, 16 * CHUNKS)
                    dve.wait_ge(prev_in, 16 * CHUNKS)
                    link(nc.vector.tensor_copy(val[:, :, :], raw[:, 0, :, :]))
                    link(nc.vector.tensor_copy(other[:, :, :], raw[:, 1, :, :]))
                    link(nc.vector.tensor_tensor(other[:, :, :], other[:, :, :], val[:, :, :], ALU.not_equal))
                    link(nc.vector.tensor_tensor(val[:, :, :], val[:, :, :], rel_of[:, :, None].to_broadcast(shape),
                                                 ALU.subtract))
                    link(nc.vector.tensor_scalar(off[:, :, :], val[:, :, :], 0.0, None, ALU.is_ge))
                    link(nc.vector.scalar_tensor_tensor(off[:, :, :].rearrange(flat), val[:, :, :].rearrange(flat), float(P),
                                                        off[:, :, :].rearrange(flat), ALU.is_lt, ALU.mult))
                    link(nc.vector.scalar_tensor_tensor(other[:, :, :].rearrange(flat), other[:, :, :].rearrange(flat), -BIG,
                                                        off[:, :, :].rearrange(flat), ALU.mult, ALU.mult))
                    link(nc.vector.tensor_scalar(off[:, :, :], off[:, :, :], 1.0, BIG, ALU.subtract, ALU.mult))
                    nc.vector.tensor_scalar(val[:, :, :], val[:, :, :], -1.0, float(P), ALU.max, ALU.min).then_inc(cut_set, 1)

                @block.sync
                def _(sp):
                    sp.wait_ge(cut_set, 1)
                    sp.dma_start(s.i_cut[0:ITEMS_PAD * P].rearrange("(c p e) -> p c e", p=P, e=P), other[:, :, :]).then_inc(cut_out, 16)
                    sp.dma_start(s.i_off.rearrange("(c p) e -> p c e", p=P), off[:, :, :]).then_inc(cut_out, 16)
                    sp.dma_start(s.i_cut[ITEMS_PAD * P:].rearrange("(p k) -> p k", p=1), end[:, :]).then_inc(cut_out, 16)
                    sp.wait_ge(cut_out, 48)
            turn_chunks(nc, c, val, table, CHUNKS)
            with Stage(nc) as st:
                rel_out, src_in, type_in, src_dve, srow_set, srow_out = st.sems("rel_out", "src_in", "type_in", "src_dve", "srow_set", "srow_out")
                block = st.block()
                @block.gpsimd
                def _(pool):
                    for which, table_, sem in ((0, s.e_src, src_in), (1, s.e_type, type_in)):
                        rows = table_.rearrange("(t e) -> t e", e=P)
                        for k in range(CHUNKS):
                            pool.indirect_dma_start(raw[:, which, k, :], None, rows,
                                                    bass.IndirectOffsetOnAxis(ap=tile_of[:, k:k + 1], axis=0)).then_inc(sem, 16)

                @block.vector
                def _(dve):
                    link = link_on(dve, src_dve)
                    dve.wait_ge(src_in, 16 * CHUNKS)
                    node_rows(nc, link, val[:, :, :], other[:, :, :], raw[:, 0, :, :], off[:, :, :].bitcast(I32))
                    dve.wait_ge(type_in, 16 * CHUNKS)
                    link(nc.vector.tensor_copy(other[:, :, :], raw[:, 1, :, :]))
                    nc.vector.scalar_tensor_tensor(off[:, :, :].rearrange(flat), val[:, :, :].rearrange(flat), float(TYPES),
                                                   other[:, :, :].rearrange(flat), ALU.mult, ALU.add).then_inc(srow_set, 1)

                @block.sync
                def _(sp):
                    sp.dma_start(s.i_rel, table[:, :]).then_inc(rel_out, 16)
                    sp.wait_ge(srow_set, 1)
                    sp.dma_start(s.i_srcrow.rearrange("(c p) e -> p c e", p=P), val[:, :, :]).then_inc(srow_out, 16)
                    sp.wait_ge(rel_out, 16)
                    sp.wait_ge(srow_out, 16)
            for source, dest in ((val, s.i_row), (other, s.i_type), (off, s.i_rel_row)):
                turn_chunks(nc, c, source, table, CHUNKS)
                store(nc, dest, table[:, :])


def node_rows(nc, link, out, spare, ids, spare_i):
    link(nc.vector.tensor_scalar(spare_i, ids, P - 1, None, ALU.bitwise_and))
    link(nc.vector.tensor_copy(out, spare_i))
    link(nc.vector.tensor_scalar(out, out, float(BLOCKS), None, ALU.mult))
    link(nc.vector.tensor_scalar(spare_i, ids, 7, None, ALU.logical_shift_right))
    link(nc.vector.tensor_copy(spare, spare_i))
    link(nc.vector.tensor_tensor(out, out, spare, ALU.add))


def store(nc, dest, source):
    with Stage(nc) as st:
        stored = st.sem("stored")
        block = st.block()
        @block.sync
        def _(sp):
            sp.dma_start(dest, source).then_inc(stored, 16)
            sp.wait_ge(stored, 16)


def tile_tables(nc, s, c):
    with Stage(nc) as st:
        raw = st.sb("t_raw", [P, TCHUNKS, P], I32)
        val = st.sb("t_val", [P, TCHUNKS, P], F32)
        spare = st.sb("t_spare", [P, TCHUNKS, P], F32)
        spare_i = st.sb("t_spare_i", [P, TCHUNKS, P], I32)
        table = st.sb("t_table", [P, TILES_PAD], F32)
        full = TILES // P
        rest = TILES - full * P
        with Stage(nc) as st:
            raw_set, raw_in, dve_done = st.sems("traw_set", "traw_in", "tsrc_dve")
            block = st.block()
            @block.gpsimd
            def _(pool):
                nc.gpsimd.memset(raw[:, full, :], 0).then_inc(raw_set, 1)

            @block.sync
            def _(sp):
                rows = s.e_src.rearrange("(t e) -> t e", e=P)
                sp.dma_start(raw[:, 0:full, :], rows[0:full * P, :].rearrange("(c p) e -> p c e", p=P)).then_inc(raw_in, 16)
                sp.wait_ge(raw_set, 1)
                sp.dma_start(raw[0:rest, full, :], rows[full * P:TILES, :]).then_inc(raw_in, 16)

            @block.vector
            def _(dve):
                dve.wait_ge(raw_in, 32)
                node_rows(nc, link_on(dve, dve_done), val[:, :, :], spare[:, :, :], raw[:, :, :], spare_i[:, :, :])
        turn_chunks(nc, c, val, table, TCHUNKS)
        store(nc, s.t_row, table[:, :])
        with Stage(nc) as st:
            cut_raw = st.sb("cut_raw", [125, FLAT], I32)
            cut_prev = st.sb("cut_prev", [125, FLAT], I32)
            cut = st.sb("cut", [125, FLAT], F32)
            pad = st.sb("cut_pad", [1, (TILES_RUN - TILES) * P], F32)
            cutraw_in, cutd_dve, cutd_set, cutd_out = st.sems("cutraw_in", "cutd_dve", "cutd_set", "cutd_out")
            block = st.block()
            @block.sync
            def _(sp):
                sp.dma_start(cut_raw[:, :], s.e_dst.rearrange("(p k) -> p k", p=125)).then_inc(cutraw_in, 16)
                sp.dma_start(cut_prev[:, :], s.e_prev[0:EDGES].rearrange("(p k) -> p k", p=125)).then_inc(cutraw_in, 16)
                sp.wait_ge(cutd_set, 2)
                sp.dma_start(s.t_cut[0:EDGES].rearrange("(p k) -> p k", p=125), cut[:, :]).then_inc(cutd_out, 16)
                sp.dma_start(s.t_cut[EDGES:TILES_RUN * P].rearrange("(p k) -> p k", p=1), pad[:, :]).then_inc(cutd_out, 16)
                sp.wait_ge(cutd_out, 32)

            @block.vector
            def _(dve):
                link = link_on(dve, cutd_dve)
                nc.vector.memset(pad[:, :], 0.0).then_inc(cutd_set, 1)
                dve.wait_ge(cutraw_in, 32)
                link(nc.vector.tensor_tensor(cut[:, :], cut_raw[:, :], cut_prev[:, :], ALU.not_equal))
                nc.vector.tensor_scalar(cut[:, :], cut[:, :], -BIG, None, ALU.mult).then_inc(cutd_set, 1)


def load_nodes(nc, x, x_in):
    with Stage(nc) as st:
        cleared, rows_in = st.sems("cleared", "rows_in")
        block = st.block()
        full = NODES // P

        @block.vector
        def _(dve):
            nc.vector.memset(x[:, full, :], 0.0).then_inc(cleared, 1)

        @block.sync
        def _(sp):
            sp.dma_start(x[:, 0:full, :], x_in[0:full * P, :].rearrange("(b p) d -> p b d", p=P)).then_inc(rows_in, 16)
            sp.wait_ge(cleared, 1)
            sp.dma_start(x[0:NODES - full * P, full, :], x_in[full * P:NODES, :]).then_inc(rows_in, 16)
            sp.wait_ge(rows_in, 32)


def clear_accumulators(nc, s):
    with Stage(nc) as st:
        zero = st.sb("zero", [P, ACC_ROWS // P * W65], F32)
        cleared, zero_out = st.sems("cleared", "zero_out")
        block = st.block()

        @block.vector
        def _(dve):
            nc.vector.memset(zero[:, :], 0.0).then_inc(cleared, 1)

        @block.sync
        def _(sp):
            sp.wait_ge(cleared, 1)
            for acc in s.acc:
                sp.dma_start(acc.rearrange("(p b) d -> p (b d)", p=P), zero[:, :]).then_inc(zero_out, 16)
            sp.wait_ge(zero_out, 16 * U)


def mean_loop(nc, s, c, x, counts):
    with Stage(nc) as st:
        x1 = st.sb("x1", [P, BLOCKS, W65], F32)
        rel = st.sb("rel", [P, ITEMS_PAD], F32)
        row = st.sb("row", [P, ITEMS_PAD], F32)
        typ = st.sb("typ", [P, ITEMS_PAD], F32)
        trash = st.sb("trash", [P, 1], F32)
        src_rows = st.sb("src_rows", [P, U, P], F32)
        same = st.sb("same", [P, U, P], BF16)
        hot_dst = st.sb("hot_dst", [P, U, P], BF16)
        hot_type = st.sb("hot_type", [P, U, TYPES], BF16)
        scrap = st.sb("scrap", [P, P], BF16)
        earlier = st.sb("earlier", [P, U], F32)
        shift = st.sb("shift", [P, U], F32)
        target = st.sb("target", [P, U], I32)
        goes = st.sb("goes", [P, U, P], F32)
        sums = st.sb("sums", [P, U, W65], F32)
        ps_goes = st.ps("ps_goes", [P, 2, 512], F32)
        ps_count = st.ps("ps_count", [P, 2, 512], F32)
        ps_sums = st.ps("ps_sums", [P, 2, 512], F32)
        tables_in, setup, chain, rows_used, hot_ready = st.sems("tables_in", "setup", "chain", "rows_used", "hot_ready")
        rows_in = st.sems("rows_in_a", "rows_in_b")
        goes_done, count_done, sums_done = st.sems("goes_done", "count_done", "sums_done")
        goes_kept, sums_kept, count_added, target_set = st.sems("goes_kept", "sums_kept", "count_added", "target_set")
        added = [st.sem(f"added{k}") for k in range(U)]
        block = st.block()

        @block.sync
        def _(sp):
            for t, source in ((rel, s.i_rel), (row, s.i_row), (typ, s.i_type)):
                sp.dma_start(t[:, :], source).then_inc(tables_in, 16)
            rows = s.i_srcrow.rearrange("(o i) e -> o (i e)", o=1)

            def load(first, h):
                span = rows[:, bass.ds(first * P, HALF * P)].to_broadcast([P, HALF * P])
                sp.dma_start(src_rows[:, h * HALF:(h + 1) * HALF, :].rearrange("p i e -> p (i e)"),
                             span).then_inc(rows_in[h], 16)

            for h in range(2):
                load(h * HALF, h)
            with sp.Fori(0, ITEM_TURNS - 1) as turn:
                for h in range(2):
                    sp.wait_ge(rows_used, turn * U + (h + 1) * HALF)
                    load((turn + 1) * U + h * HALF, h)

        @block.vector
        def _(dve):
            link = link_on(dve, setup)
            link(nc.vector.tensor_copy(x1[:, :, 0:DIM], x[:, :, :]))
            link(nc.vector.memset(x1[:, :, DIM:W65], 1.0))
            link(nc.vector.tensor_scalar(trash[:, :], c.lane[:, :], float(TRASH), None, ALU.add))
            link(nc.vector.memset(counts[:, :], 0.0))
            dve.wait_ge(tables_in, 48)
            with dve.Fori(0, ITEM_TURNS) as turn:
                _, at = nc.values_load_multi_w_load_instructions(
                    c.block_row[0:1, bass.ds(turn * U, U)], engines=DVE_ONLY, min_val=0, max_val=(BLOCKS - 1) * W65,
                    skip_runtime_bounds_check_because="the item map clamps the block")
                steps = TurnCount(dve, chain, turn, 4)

                def add_counts(u):
                    dve.wait_ge(count_done, turn * U + u + 1)
                    here = counts[:, bass.ds(at[u], TYPES)]
                    dve.wait_ge(count_added, turn * U + u)
                    nc.vector.tensor_tensor(here, here, ps_count[:, u % 2, 0:TYPES], ALU.add).then_inc(count_added, 1)

                for u in range(U):
                    col = bass.ds(turn * U + u, 1)
                    h = u // HALF
                    if u % HALF == 0:
                        dve.wait_ge(rows_in[h], (turn + 1) * 16)
                    nc.vector.tensor_scalar(same[:, u, :], src_rows[:, u, :], row[:, col], None,
                                            ALU.is_equal).then_inc(rows_used, 1)
                    nc.vector.tensor_scalar(hot_dst[:, u, :], c.iota_b[:, :], rel[:, col], None, ALU.is_equal)
                    nc.vector.tensor_scalar(hot_type[:, u, :], c.iota_b[:, 0:TYPES], typ[:, col], None,
                                            ALU.is_equal).then_inc(hot_ready, 1)
                    dve.wait_ge(rows_used, turn * U + u + 1)
                    nc.vector.tensor_tensor_reduce(out=scrap[:, :], in0=same[:, u, :], in1=c.before[:, :], scale=1.0,
                                                   scalar=0.0, op0=ALU.mult, op1=ALU.add,
                                                   accum_out=earlier[:, u:u + 1])
                    if u >= 2:
                        add_counts(u - 2)
                    if u % HALF == HALF - 1:
                        part = slice(h * HALF, (h + 1) * HALF)
                        cols = bass.ds(turn * U + h * HALF, HALF)
                        far = steps.mark(nc.vector.tensor_scalar(shift[:, part], row[:, cols], -1.0, trash[:, 0:1],
                                                                 ALU.mult, ALU.add))
                        steps.wait(far)
                        moved = steps.mark(nc.vector.scalar_tensor_tensor(shift[:, part], earlier[:, part], 1.0,
                                                                          shift[:, part], ALU.min, ALU.mult))
                        steps.wait(moved)
                        for k in range(h * HALF, (h + 1) * HALF):
                            dve.wait_ge(added[k], turn * 16)
                        nc.vector.tensor_tensor(target[:, part], shift[:, part], row[:, cols], ALU.add).then_inc(target_set, 1)
                add_counts(U - 2)
                add_counts(U - 1)
                steps.close()

        @block.tensor
        def _(pe):
            pe.wait_ge(setup, 4)
            with pe.Fori(0, ITEM_TURNS) as turn:
                _, at = nc.values_load_multi_w_load_instructions(
                    c.block_row[0:1, bass.ds(turn * U, U)], engines=PE_ONLY, min_val=0, max_val=(BLOCKS - 1) * W65,
                    skip_runtime_bounds_check_because="the item map clamps the block")
                x_rows = x1[:, :, :].rearrange("p b d -> p (b d)")

                def pick_sums(u):
                    pe.wait_ge(goes_kept, turn * U + u + 1)
                    pe.wait_ge(sums_kept, turn * U + max(u - 1, 0))
                    nc.tensor.matmul(ps_sums[:, u % 2, 0:W65], goes[:, u, :], x_rows[:, bass.ds(at[u], W65)],
                                     start=True, stop=True).then_inc(sums_done, 1)

                for u in range(U):
                    pe.wait_ge(hot_ready, turn * U + u + 1)
                    nc.tensor.matmul(ps_goes[:, u % 2, 0:P], hot_dst[:, u, :], same[:, u, :],
                                     start=True, stop=True).then_inc(goes_done, 1)
                    pe.wait_ge(count_added, turn * U + max(u - 1, 0))
                    nc.tensor.matmul(ps_count[:, u % 2, 0:TYPES], hot_dst[:, u, :], hot_type[:, u, :],
                                     start=True, stop=True).then_inc(count_done, 1)
                    if u >= 1:
                        pick_sums(u - 1)
                pick_sums(U - 1)

        @block.scalar
        def _(act):
            with act.Fori(0, ITEM_TURNS) as turn:
                def keep_sums(u):
                    act.wait_ge(sums_done, turn * U + u + 1)
                    act.wait_ge(added[u], turn * 16)
                    nc.scalar.copy(sums[:, u, :], ps_sums[:, u % 2, 0:W65]).then_inc(sums_kept, 1)

                for u in range(U):
                    act.wait_ge(goes_done, turn * U + u + 1)
                    nc.scalar.copy(goes[:, u, :], ps_goes[:, u % 2, 0:P]).then_inc(goes_kept, 1)
                    if u >= 1:
                        keep_sums(u - 1)
                keep_sums(U - 1)

        @block.gpsimd
        def _(pool):
            with pool.Fori(0, ITEM_TURNS) as turn:
                for u in range(U):
                    pool.wait_ge(sums_kept, turn * U + u + 1)
                    if u % HALF == 0:
                        pool.wait_ge(target_set, turn * 2 + u // HALF + 1)
                    pool.wait_ge(added[u], turn * 16)
                    hold(pool, c)
                    pool.indirect_dma_start(s.acc[u], bass.IndirectOffsetOnAxis(ap=target[:, u:u + 1], axis=0),
                                            sums[:, u, :], None, compute_op=ALU.add).then_inc(added[u], 16)
            for k in range(U):
                pool.wait_ge(added[k], ITEM_TURNS * 16)


def layer_norm(nc, c, h, x):
    with Stage(nc) as st:
        square = st.sb("square", [P, BLOCKS, DIM], F32)
        stat = st.sb("stat", [P, BLOCKS], F32)
        root = st.sb("root", [P, BLOCKS], F32)
        dve_done, var_set, root_set = st.sems("dve_done", "var_set", "root_set")
        block = st.block()
        shape = [P, BLOCKS, DIM]

        @block.vector
        def _(dve):
            link = link_on(dve, dve_done)
            link(nc.vector.tensor_reduce(stat[:, :], h[:, :, :], AX.X, ALU.add))
            link(nc.vector.tensor_scalar(stat[:, :], stat[:, :], 1.0 / DIM, None, ALU.mult))
            link(nc.vector.tensor_tensor(h[:, :, :], h[:, :, :], stat[:, :, None].to_broadcast(shape), ALU.subtract))
            link(nc.vector.tensor_tensor(square[:, :, :], h[:, :, :], h[:, :, :], ALU.mult))
            nc.vector.tensor_reduce(root[:, :], square[:, :, :], AX.X, ALU.add).then_inc(var_set, 1)
            dve.wait_ge(root_set, 1)
            link(nc.vector.reciprocal(root[:, :], root[:, :]))
            link(nc.vector.tensor_tensor(x[:, :, :], h[:, :, :], root[:, :, None].to_broadcast(shape), ALU.mult))

        @block.scalar
        def _(act):
            act.wait_ge(var_set, 1)
            nc.scalar.activation(root[:, :], root[:, :], ACT.Sqrt, bias=c.eps[:, 0:1], scale=1.0 / DIM).then_inc(root_set, 1)


def sum_accumulators(nc, s, total):
    with Stage(nc) as st:
        part = st.sb("part", [P, 2, BLOCKS * W65], F32)
        part_in = st.sems("part_in_a", "part_in_b")
        first_in, summed = st.sems("first_in", "summed")
        block = st.block()
        flat = total[:, :, :].rearrange("p b d -> p (b d)")

        @block.sync
        def _(sp):
            for k, acc in enumerate(s.acc):
                rows = acc[0:PADDED, :].rearrange("(p b) d -> p (b d)", p=P)
                if k == 0:
                    sp.dma_start(flat, rows).then_inc(first_in, 16)
                    continue
                if k >= 3:
                    sp.wait_ge(summed, k - 2)
                sp.dma_start(part[:, k % 2, :], rows).then_inc(part_in[k % 2], 16)

        @block.vector
        def _(dve):
            dve.wait_ge(first_in, 16)
            for k in range(1, U):
                dve.wait_ge(part_in[k % 2], 16 * ((k + 1) // 2))
                if k >= 2:
                    dve.wait_ge(summed, k - 1)
                nc.vector.tensor_tensor(flat, flat, part[:, k % 2, :], ALU.add).then_inc(summed, 1)


def mean_layer(nc, s, c, x, weight, bias):
    with Stage(nc) as st:
        counts = st.sb("counts", [P, BLOCKS * W65], F32)
        clear_accumulators(nc, s)
        mean_loop(nc, s, c, x, counts)
        finish_counts(nc, s, counts)
    with Stage(nc) as st:
        total = st.sb("total", [P, BLOCKS, W65], F32)
        h = st.sb("h", [P, BLOCKS, DIM], F32)
        sum_accumulators(nc, s, total)
        mean_update(nc, s, c, x, total, h, weight, bias)
        layer_norm(nc, c, h, x)


def finish_counts(nc, s, counts):
    with Stage(nc) as st:
        degree = st.sb("degree", [P, BLOCKS], F32)
        dve_done, ready, out = st.sems("dve_done", "ready", "out")
        block = st.block()

        @block.vector
        def _(dve):
            link = link_on(dve, dve_done)
            link(nc.vector.tensor_reduce(degree[:, :], counts[:, :].rearrange("p (b r) -> p b r", r=W65), AX.X, ALU.add))
            link(nc.vector.tensor_scalar(counts[:, :], counts[:, :], 1.0, None, ALU.max))
            nc.vector.reciprocal(counts[:, :], counts[:, :]).then_inc(ready, 1)

        @block.sync
        def _(sp):
            sp.wait_ge(ready, 1)
            sp.dma_start(s.counts, counts[:, :]).then_inc(out, 16)
            sp.dma_start(s.degree, degree[:, :]).then_inc(out, 16)
            sp.wait_ge(out, 32)


def mean_update(nc, s, c, x, total, h, weight, bias):
    with Stage(nc) as st:
        w = st.sb("w", [2 * DIM, DIM], F32)
        b = st.sb("b", [P, DIM], F32)
        recip = st.sb("recip", [P, BLOCKS], F32)
        both = st.sb("both", [P, G, 2 * DIM], F32)
        both_t = st.sb("both_t", [P, G * P], F32)
        ps_t = st.ps("ps_t", [P, G * P], F32)
        ps_out = st.ps("ps_out", [P, G, DIM], F32)
        w_in, setup, both_set, turned, kept, out_done, chain = st.sems(
            "w_in", "setup", "both_set", "turned", "kept", "out_done", "chain")
        block = st.block()

        @block.sync
        def _(sp):
            sp.dma_start(w[:, :], weight).then_inc(w_in, 16)
            sp.dma_start(b[:, :], bias.to_broadcast([P, DIM])).then_inc(w_in, 16)

        @block.vector
        def _(dve):
            link = link_on(dve, setup)
            link(nc.vector.tensor_scalar(recip[:, :], total[:, :, DIM], 1.0, None, ALU.max))
            link(nc.vector.reciprocal(recip[:, :], recip[:, :]))
            dve.wait_ge(w_in, 32)
            with dve.Fori(0, BLOCK_TURNS) as turn:
                blocks = bass.ds(turn * G, G)
                nc.vector.tensor_copy(both[:, :, 0:DIM], x[:, blocks, :])
                nc.vector.tensor_tensor(both[:, :, DIM:2 * DIM], total[:, blocks, 0:DIM],
                                        recip[:, blocks][:, :, None].to_broadcast([P, G, DIM]), ALU.mult).then_inc(both_set, 1)
                dve.wait_ge(out_done, turn + 1)
                nc.vector.tensor_tensor(h[:, blocks, :], ps_out[:, :, :], x[:, blocks, :], ALU.add).then_inc(chain, 1)
            dve.wait_ge(chain, BLOCK_TURNS)
            link(nc.vector.tensor_tensor(h[:, :, :], h[:, :, :], b[:, None, :].to_broadcast([P, BLOCKS, DIM]), ALU.add))

        @block.tensor
        def _(pe):
            pe.wait_ge(w_in, 32)
            with pe.Fori(0, BLOCK_TURNS) as turn:
                pe.wait_ge(both_set, turn + 1)
                for g in range(G):
                    last = nc.tensor.transpose(ps_t[:, g * P:(g + 1) * P], both[:, g, :], c.ident[:, :])
                last.then_inc(turned, 1)
                pe.wait_ge(kept, turn + 1)
                pe.wait_ge(chain, turn)
                for g in range(G):
                    last = nc.tensor.matmul(ps_out[:, g, :], both_t[:, g * P:(g + 1) * P], w[:, :], start=True, stop=True)
                last.then_inc(out_done, 1)

        @block.scalar
        def _(act):
            with act.Fori(0, BLOCK_TURNS) as turn:
                act.wait_ge(turned, turn + 1)
                nc.scalar.copy(both_t[:, :], ps_t[:, :]).then_inc(kept, 1)


def max_layer(nc, s, c, x):
    with Stage(nc) as st:
        scale = st.sb("scale", [P, BLOCKS], F32)
        end_row = st.sb("end_row", [P, BLOCKS], I32)
        max_prepare(nc, s, c, x, scale, end_row)
        max_loop(nc, s, c)
        with Stage(nc) as inner:
            h = inner.sb("h", [P, BLOCKS, DIM], F32)
            max_update(nc, s, c, x, scale, end_row, h)
            layer_norm(nc, c, h, x)


def max_prepare(nc, s, c, x, scale, end_row):
    with Stage(nc) as st:
        degree = st.sb("degree", [P, BLOCKS], F32)
        w = st.sb("w", [P, BLOCKS], F32)
        g = st.sb("g", [P, BLOCKS, DIM], F32)
        total = st.sb("total", [P, BLOCKS], F32)
        upto = st.sb("upto", [P, BLOCKS], F32)
        end = st.sb("end", [P, BLOCKS], I32)
        spare = st.sb("spare", [P, BLOCKS], I32)
        ps_in = st.ps("ps_in", [P, BLOCKS], F32)
        ps_total = st.ps("ps_total", [P, BLOCKS], F32)
        degree_in, dve_done, clamped, rooted, summed, g_set, g_out = st.sems(
            "degree_in", "dve_done", "clamped", "rooted", "summed", "g_set", "g_out")
        block = st.block()

        @block.sync
        def _(sp):
            sp.dma_start(degree[:, :], s.degree).then_inc(degree_in, 16)
            sp.wait_ge(g_set, 1)
            sp.dma_start(node_view(s.g, DIM), g[:, :, :]).then_inc(g_out, 16)
            sp.wait_ge(g_out, 16)

        @block.tensor
        def _(pe):
            pe.wait_ge(degree_in, 16)
            nc.tensor.matmul(ps_in[:, :], c.upto[:, :], degree[:, :], start=True, stop=True)
            nc.tensor.matmul(ps_total[:, :], c.ones[:, :], degree[:, :], start=True, stop=True).then_inc(summed, 1)

        @block.scalar
        def _(act):
            act.wait_ge(clamped, 1)
            nc.scalar.activation(w[:, :], w[:, :], ACT.Sqrt).then_inc(rooted, 1)

        @block.vector
        def _(dve):
            link = link_on(dve, dve_done)
            dve.wait_ge(degree_in, 16)
            nc.vector.tensor_scalar(w[:, :], degree[:, :], 1.0, None, ALU.max).then_inc(clamped, 1)
            dve.wait_ge(summed, 1)
            link(nc.vector.tensor_copy(total[:, :], ps_total[:, :]))
            link(nc.vector.tensor_tensor_scan(upto[:, :], c.ones[:, 0:BLOCKS], total[:, :], 0.0, ALU.mult, ALU.add))
            link(nc.vector.tensor_tensor(upto[:, :], upto[:, :], total[:, :], ALU.subtract))
            link(nc.vector.tensor_tensor(upto[:, :], upto[:, :], ps_in[:, :], ALU.add))
            link(nc.vector.tensor_scalar(upto[:, :], upto[:, :], -1.0, 0.0, ALU.add, ALU.max))
            link(nc.vector.tensor_copy(end[:, :], upto[:, :]))
            link(nc.vector.tensor_scalar(spare[:, :], end[:, :], P - 1, None, ALU.bitwise_and))
            link(nc.vector.tensor_copy(upto[:, :], spare[:, :]))
            link(nc.vector.tensor_scalar(spare[:, :], end[:, :], 7, None, ALU.logical_shift_right))
            link(nc.vector.tensor_copy(total[:, :], spare[:, :]))
            link(nc.vector.scalar_tensor_tensor(end_row[:, :], upto[:, :], float(TILES_RUN), total[:, :],
                                                ALU.mult, ALU.add))
            dve.wait_ge(rooted, 1)
            link(nc.vector.reciprocal(w[:, :], w[:, :]))
            nc.vector.tensor_tensor(g[:, :, :], x[:, :, :], w[:, :, None].to_broadcast([P, BLOCKS, DIM]),
                                    ALU.mult).then_inc(g_set, 1)
            link(nc.vector.scalar_tensor_tensor(scale[:, :], degree[:, :], 1.0, w[:, :], ALU.min, ALU.mult))


def max_loop(nc, s, c):
    with Stage(nc) as st:
        table = st.sb("table", [P, TILES_PAD], F32)
        index = st.sb("index", [P, U], I32)
        rows = st.sb("rows", [P, U, DIM], F32)
        cut = st.sb("cut", [DIM, 2, HALF * P], F32)
        running = st.sb("running", [DIM, 2, HALF * P], F32)
        back = st.sb("back", [P, 2, HALF * DIM], F32)
        ps_turned = st.ps("ps_turned", [DIM, 2, HALF * P], F32)
        ps_back = st.ps("ps_back", [P, 2, 512], F32)
        table_in, start_set, index_set, turned, scan_done, back_done, back_kept = st.sems(
            "table_in", "start_set", "index_set", "turned", "scan_done", "back_done", "back_kept")
        got = [st.sem(f"got{u}") for u in range(U)]
        cut_in = st.sems("cut_in_a", "cut_in_b")
        stored = st.sems("stored_a", "stored_b")
        block = st.block()

        @block.sync
        def _(sp):
            sp.dma_start(table[:, :], s.t_row).then_inc(table_in, 16)
            cuts = s.t_cut.rearrange("(o k) -> o k", o=1)
            out = s.scanned.rearrange("(p t) d -> p (t d)", p=P)

            def load(first_tile, h):
                sp.dma_start(cut[:, h, :], cuts[:, bass.ds(first_tile * P, HALF * P)].to_broadcast([DIM, HALF * P])
                             ).then_inc(cut_in[h], 16)

            def keep(turn, h):
                sp.wait_ge(back_kept, turn * 2 + h + 1)
                sp.dma_start(out[:, bass.ds((turn * U + h * HALF) * DIM, HALF * DIM)], back[:, h, :]
                             ).then_inc(stored[h], 16)

            for h in range(2):
                load(h * HALF, h)
            with sp.Fori(0, TILE_TURNS - 1) as turn:
                for h in range(2):
                    sp.wait_ge(scan_done, turn * 2 + h + 1)
                    load((turn + 1) * U + h * HALF, h)
                for h in range(2):
                    keep(turn, h)
            for h in range(2):
                keep(TILE_TURNS - 1, h)
                sp.wait_ge(stored[h], 16 * TILE_TURNS)

        @block.gpsimd
        def _(pool):
            with pool.Fori(0, TILE_TURNS) as turn:
                for u in range(U):
                    if u % HALF == 0:
                        pool.wait_ge(index_set, turn * 2 + u // HALF + 1)
                        hold(pool, c)
                    pool.indirect_dma_start(rows[:, u, :], None, s.g,
                                            bass.IndirectOffsetOnAxis(ap=index[:, u:u + 1], axis=0)).then_inc(got[u], 16)

        @block.tensor
        def _(pe):
            with pe.Fori(0, TILE_TURNS) as turn:
                for h in range(2):
                    for k in range(HALF):
                        u = h * HALF + k
                        pe.wait_ge(got[u], (turn + 1) * 16)
                        hold(pe, c)
                        last = nc.tensor.transpose(ps_turned[:, h, k * P:(k + 1) * P], rows[:, u, :], c.ident[:, :])
                    last.then_inc(turned, 1)
                pe.wait_ge(back_kept, turn * 2)
                for h in range(2):
                    pe.wait_ge(scan_done, turn * 2 + h + 1)
                    hold(pe, c)
                    for k in range(HALF):
                        last = nc.tensor.transpose(ps_back[:, h, k * DIM:(k + 1) * DIM], running[:, h, k * P:(k + 1) * P],
                                                   c.ident[0:DIM, 0:DIM])
                    last.then_inc(back_done, 1)

        @block.vector
        def _(dve):
            nc.vector.memset(running[:, 1, HALF * P - 1:HALF * P], -BIG).then_inc(start_set, 1)
            dve.wait_ge(table_in, 16)
            for h in range(2):
                nc.vector.tensor_copy(index[:, h * HALF:(h + 1) * HALF], table[:, h * HALF:(h + 1) * HALF]).then_inc(index_set, 1)
            dve.wait_ge(start_set, 1)
            with dve.Fori(0, TILE_TURNS) as turn:
                dve.wait_ge(back_done, turn * 2)
                for h in range(2):
                    dve.wait_ge(cut_in[h], (turn + 1) * 16)
                    dve.wait_ge(turned, turn * 2 + h + 1)
                    dve.wait_ge(scan_done, turn * 2 + h)
                    nc.vector.tensor_tensor_scan(running[:, h, :], cut[:, h, :], ps_turned[:, h, :],
                                                 running[:, 1 - h, HALF * P - 1:HALF * P], ALU.add, ALU.max
                                                 ).then_inc(scan_done, 1)
                    nc.vector.tensor_copy(index[:, h * HALF:(h + 1) * HALF],
                                          table[:, bass.ds((turn + 1) * U + h * HALF, HALF)]).then_inc(index_set, 1)

        @block.scalar
        def _(act):
            with act.Fori(0, TILE_TURNS) as turn:
                for h in range(2):
                    act.wait_ge(back_done, turn * 2 + h + 1)
                    act.wait_ge(stored[h], turn * 16)
                    nc.scalar.copy(back[:, h, :], ps_back[:, h, 0:HALF * DIM]).then_inc(back_kept, 1)


def max_update(nc, s, c, x, scale, end_row, h):
    with Stage(nc) as st:
        index = st.sb("index", [P, G], I32)
        rows = st.sb("rows", [P, G, DIM], F32)
        index_set, scaled, h_set = st.sems("index_set", "scaled", "h_set")
        got = [st.sem(f"got{g}") for g in range(G)]
        block = st.block()

        @block.gpsimd
        def _(pool):
            with pool.Fori(0, BLOCK_TURNS) as turn:
                pool.wait_ge(index_set, turn + 1)
                hold(pool, c)
                for g in range(G):
                    pool.indirect_dma_start(rows[:, g, :], None, s.scanned,
                                            bass.IndirectOffsetOnAxis(ap=index[:, g:g + 1], axis=0)).then_inc(got[g], 16)

        @block.vector
        def _(dve):
            with dve.Fori(0, BLOCK_TURNS) as turn:
                blocks = bass.ds(turn * G, G)
                nc.vector.tensor_copy(index[:, :], end_row[:, blocks]).then_inc(index_set, 1)
                for g in range(G):
                    dve.wait_ge(got[g], (turn + 1) * 16)
                nc.vector.tensor_tensor(rows[:, :, :], rows[:, :, :], scale[:, blocks][:, :, None].to_broadcast([P, G, DIM]),
                                        ALU.mult).then_inc(scaled, 1)
                dve.wait_ge(scaled, turn + 1)
                nc.vector.tensor_tensor(h[:, blocks, :], rows[:, :, :], x[:, blocks, :], ALU.add).then_inc(h_set, 1)


def relational_layer(nc, s, c, x, weights, root, bias, res_weight, res_bias):
    for layer in range(2):
        with Stage(nc) as st:
            acc = st.sb("acc", [P, BLOCKS, W65], F32)
            with Stage(nc) as inner:
                h = x
                if layer:
                    h = inner.sb("h", [P, BLOCKS, DIM], F32)
                    store(nc, h[:, :, :], node_view(s.h, DIM))
                relational_table(nc, s, c, h, acc, weights[layer], root[layer], bias[layer:layer + 1, :],
                                 res_weight[layer], res_bias[layer:layer + 1, :])
            relational_loop(nc, s, c, acc, first=(layer == 0))
            with Stage(nc) as inner:
                h = inner.sb("h", [P, BLOCKS, DIM], F32)
                relational_update(nc, s, acc, h, x if layer else None)
                if layer:
                    layer_norm(nc, c, h, x)
                else:
                    store(nc, node_view(s.h, DIM), h[:, :, :])


def relational_table(nc, s, c, h, acc, weights, root, bias, res_weight, res_bias):
    tail = SPAN + 2 * DIM
    pieces = -(-tail // 512)
    banks = 6
    slots = 3
    total = G * pieces
    dve_share = (total + 1) // 2
    act_share = total // 2
    with Stage(nc) as st:
        w = st.sb("w", [W65, tail], F32)
        h_t = st.sb("h_t", [W65, G * P], F32)
        stage = st.sb("stage", [P, G, DIM], F32)
        res = st.sb("res", [P, BLOCKS, DIM], F32)
        out = st.sb("out", [P, slots, SPAN], F32)
        ps_t = st.ps("ps_t", [DIM, G * P], F32)
        ps = st.ps("ps", [P, banks, 512], F32)
        w_set, w_in, staged, turned, turned_kept, made, by_dve, by_act, res_out = st.sems(
            "w_set", "w_in", "staged", "turned", "turned_kept", "made", "by_dve", "by_act", "res_out")
        sent = [st.sem(f"sent{k}") for k in range(slots)]
        block = st.block()
        uses = [len(range(k, G, slots)) for k in range(slots)]

        @block.sync
        def _(sp):
            sp.dma_start(w[0:DIM, 0:SPAN].rearrange("d (r k) -> d r k", r=TYPES), weights.rearrange("r d k -> d r k")
                         ).then_inc(w_in, 16)
            sp.dma_start(w[0:DIM, SPAN:SPAN + DIM], root).then_inc(w_in, 16)
            sp.dma_start(w[0:DIM, SPAN + DIM:tail], res_weight).then_inc(w_in, 16)
            sp.wait_ge(w_set, 1)
            sp.dma_start(w[DIM:W65, SPAN:SPAN + DIM], bias).then_inc(w_in, 16)
            sp.dma_start(w[DIM:W65, SPAN + DIM:tail], res_bias).then_inc(w_in, 16)
            rows = s.rel_table.rearrange("(p b r) d -> p b (r d)", p=P, r=TYPES)
            with sp.Fori(0, BLOCK_TURNS) as turn:
                for g in range(G):
                    upto = (g + 1) * pieces
                    sp.wait_ge(by_dve, turn * dve_share + (upto + 1) // 2)
                    hold(sp, c)
                    sp.wait_ge(by_act, turn * act_share + upto // 2)
                    hold(sp, c)
                    sp.dma_start(rows[:, bass.ds(turn * G + g, 1), :], out[:, g % slots:g % slots + 1, :]
                                 ).then_inc(sent[g % slots], 16)
            sp.dma_start(node_view(s.res, DIM), res[:, :, :]).then_inc(res_out, 16)
            sp.wait_ge(res_out, 16)
            for k in range(slots):
                sp.wait_ge(sent[k], 16 * BLOCK_TURNS * uses[k])

        @block.tensor
        def _(pe):
            pe.wait_ge(w_in, 80)
            with pe.Fori(0, BLOCK_TURNS) as turn:
                pe.wait_ge(staged, turn + 1)
                hold(pe, c)
                for g in range(G):
                    last = nc.tensor.transpose(ps_t[:, g * P:(g + 1) * P], stage[:, g, :], c.ident[:, :])
                last.then_inc(turned, 1)
                pe.wait_ge(turned_kept, turn + 1)
                for q in range(total):
                    g, piece = divmod(q, pieces)
                    sem, share = ((by_dve, dve_share), (by_act, act_share))[q % 2]
                    if q < 2:
                        pe.wait_ge(sem, turn * share)
                    elif q >= banks:
                        pe.wait_ge(sem, turn * share + (q - banks) // 2 + 1)
                    a, b = piece * 512, min(tail, (piece + 1) * 512)
                    nc.tensor.matmul(ps[:, q % banks, 0:b - a], h_t[:, g * P:(g + 1) * P], w[:, a:b],
                                     start=True, stop=True).then_inc(made, 1)

        def copy_pieces(engine, turn, parity, copy, relu, sem):
            for q in range(parity, total, 2):
                g, piece = divmod(q, pieces)
                slot = g % slots
                if q - 2 < g * pieces:
                    engine.wait_ge(sent[slot], (turn * uses[slot] + g // slots) * 16)
                engine.wait_ge(made, turn * total + q + 1)
                a, b = piece * 512, min(SPAN, (piece + 1) * 512)
                last = copy(out[:, slot, a:b], ps[:, q % banks, 0:b - a])
                if piece == pieces - 1:
                    here = bass.ds(turn * G + g, 1)
                    copy(acc[:, here, 0:DIM], ps[:, q % banks, b - a:b - a + DIM][:, None, :])
                    last = relu(res[:, here, :], ps[:, q % banks, b - a + DIM:b - a + 2 * DIM][:, None, :])
                last.then_inc(sem, 1)

        @block.vector
        def _(dve):
            nc.vector.memset(h_t[DIM:W65, :], 1.0)
            nc.vector.memset(w[DIM:W65, :], 0.0).then_inc(w_set, 1)
            with dve.Fori(0, BLOCK_TURNS) as turn:
                dve.wait_ge(turned, turn)
                nc.vector.tensor_copy(stage[:, :, :], h[:, bass.ds(turn * G, G), :]).then_inc(staged, 1)
                copy_pieces(dve, turn, 0, nc.vector.tensor_copy, nc.vector.tensor_relu, by_dve)

        @block.scalar
        def _(act):
            with act.Fori(0, BLOCK_TURNS) as turn:
                act.wait_ge(turned, turn + 1)
                nc.scalar.copy(h_t[0:DIM, :], ps_t[:, :]).then_inc(turned_kept, 1)
                copy_pieces(act, turn, 1, nc.scalar.copy,
                            lambda o, i: nc.scalar.activation(o, i, ACT.Relu), by_act)


def relational_loop(nc, s, c, acc, first):
    with Stage(nc) as st:
        rel = st.sb("rel", [P, ITEMS_PAD], F32)
        table = st.sb("table", [P, ITEMS_PAD], F32)
        weight = st.sb("weight", [P, ITEMS_PAD], F32)
        index = st.sb("index", [P, U], I32)
        rows = st.sb("rows", [P, U, DIM], F32)
        share = st.sb("share", [P, U, P], F32)
        ps_sum = st.ps("ps_sum", [P, 2, 512], F32)
        tables_in, setup, index_set, share_set, sum_done, sum_added = st.sems(
            "tables_in", "setup", "index_set", "share_set", "sum_done", "sum_added")
        got = [st.sem(f"got{u}") for u in range(U)]
        if first:
            typ = st.sb("typ", [P, ITEMS_PAD], F32)
            counts = st.sb("counts", [P, BLOCKS * W65], F32)
            hot_dst = st.sb("hot_dst", [P, U, P], BF16)
            hot_type = st.sb("hot_type", [P, U, TYPES], BF16)
            hot_t = st.sb("hot_t", [P, U, P], F32)
            scrap = st.sb("scrap", [P, TYPES], F32)
            picked = st.sb("picked", [P, U], F32)
            ps_hot = st.ps("ps_hot", [P, 2, 1024], BF16)
            ps_weight = st.ps("ps_weight", [P, 2, 512], F32)
            hot_set, hot_turned, hot_kept, weight_done, weight_kept, weight_out = st.sems(
                "hot_set", "hot_turned", "hot_kept", "weight_done", "weight_kept", "weight_out")
        block = st.block()
        loads = [(rel, s.i_rel), (table, s.i_rel_row)] + ([(typ, s.i_type), (counts, s.counts)] if first
                                                          else [(weight, s.i_weight)])

        @block.sync
        def _(sp):
            for t, source in loads:
                sp.dma_start(t[:, :], source).then_inc(tables_in, 16)
            if first:
                sp.wait_ge(weight_kept, ITEM_TURNS + 1)
                sp.dma_start(s.i_weight, weight[:, :]).then_inc(weight_out, 16)
                sp.wait_ge(weight_out, 16)

        @block.gpsimd
        def _(pool):
            with pool.Fori(0, ITEM_TURNS) as turn:
                for u in range(U):
                    if u % HALF == 0:
                        pool.wait_ge(index_set, turn * 2 + u // HALF + 1)
                        hold(pool, c)
                    pool.indirect_dma_start(rows[:, u, :], None, s.rel_table,
                                            bass.IndirectOffsetOnAxis(ap=index[:, u:u + 1], axis=0)).then_inc(got[u], 16)

        @block.vector
        def _(dve):
            if first:
                nc.vector.memset(weight[:, ITEMS:ITEMS_PAD], 0.0).then_inc(weight_kept, 1)
            dve.wait_ge(tables_in, 16 * len(loads))
            for h in range(2):
                part = slice(h * HALF, (h + 1) * HALF)
                nc.vector.tensor_copy(index[:, part], table[:, part]).then_inc(index_set, 1)
            with dve.Fori(0, ITEM_TURNS) as turn:
                _, at = nc.values_load_multi_w_load_instructions(
                    c.block_row[0:1, bass.ds(turn * U, U)], engines=DVE_ONLY, min_val=0, max_val=(BLOCKS - 1) * W65,
                    skip_runtime_bounds_check_because="the item map clamps the block")
                acc_rows = acc[:, :, :].rearrange("p b d -> p (b d)")

                def build(u):
                    col = bass.ds(turn * U + u, 1)
                    nc.vector.tensor_scalar(hot_dst[:, u, :], c.iota_b[:, :], rel[:, col], None, ALU.is_equal)
                    nc.vector.tensor_scalar(hot_type[:, u, :], c.iota_b[:, 0:TYPES], typ[:, col], None,
                                            ALU.is_equal).then_inc(hot_set, 1)

                def pick_weight(u):
                    dve.wait_ge(weight_done, turn * U + u + 1)
                    nc.vector.tensor_tensor_reduce(out=scrap[:, :], in0=ps_weight[:, u % 2, 0:TYPES],
                                                   in1=hot_type[:, u, :], scale=1.0, scalar=0.0, op0=ALU.mult,
                                                   op1=ALU.add, accum_out=picked[:, u:u + 1]).then_inc(setup, 1)
                    dve.wait_ge(setup, turn * U + u + 1)
                    make_share(u, picked[:, u:u + 1])

                def make_share(u, by):
                    nc.vector.tensor_scalar(share[:, u, :], c.iota_b[:, :], rel[:, bass.ds(turn * U + u, 1)], by,
                                            ALU.is_equal, ALU.mult).then_inc(share_set, 1)

                def add_sum(u):
                    dve.wait_ge(sum_done, turn * U + u + 1)
                    dve.wait_ge(sum_added, turn * U + u)
                    here = acc_rows[:, bass.ds(at[u], DIM)]
                    nc.vector.tensor_tensor(here, here, ps_sum[:, u % 2, 0:DIM], ALU.add).then_inc(sum_added, 1)
                    if u % HALF == HALF - 1:
                        h = u // HALF
                        nc.vector.tensor_copy(index[:, h * HALF:(h + 1) * HALF],
                                              table[:, bass.ds((turn + 1) * U + h * HALF, HALF)]).then_inc(index_set, 1)

                for u in range(U + 2):
                    if first:
                        if u < U:
                            build(u)
                        if 1 <= u <= U:
                            pick_weight(u - 1)
                    elif u < U:
                        make_share(u, weight[:, bass.ds(turn * U + u, 1)])
                    if u >= 2:
                        add_sum(u - 2)
                if first:
                    nc.vector.tensor_copy(weight[:, bass.ds(turn * U, U)], picked[:, :]).then_inc(weight_kept, 1)

        @block.tensor
        def _(pe):
            if first:
                pe.wait_ge(tables_in, 16 * len(loads))
            with pe.Fori(0, ITEM_TURNS) as turn:
                if first:
                    _, at = nc.values_load_multi_w_load_instructions(
                        c.block_row[0:1, bass.ds(turn * U, U)], engines=PE_ONLY, min_val=0, max_val=(BLOCKS - 1) * W65,
                        skip_runtime_bounds_check_because="the item map clamps the block")

                def turn_hot(u):
                    pe.wait_ge(hot_set, turn * U + u + 1)
                    nc.tensor.transpose(ps_hot[:, u % 2, 0:P], hot_dst[:, u, :], c.ident_b[:, :]).then_inc(hot_turned, 1)

                def find_weights(u):
                    pe.wait_ge(hot_kept, turn * U + u + 1)
                    nc.tensor.matmul(ps_weight[:, u % 2, 0:TYPES], hot_t[:, u, :], counts[:, bass.ds(at[u], TYPES)],
                                     start=True, stop=True).then_inc(weight_done, 1)

                def sum_rows(u):
                    pe.wait_ge(share_set, turn * U + u + 1)
                    pe.wait_ge(got[u], (turn + 1) * 16)
                    pe.wait_ge(sum_added, turn * U + max(u - 1, 0))
                    nc.tensor.matmul(ps_sum[:, u % 2, 0:DIM], share[:, u, :], rows[:, u, :],
                                     start=True, stop=True).then_inc(sum_done, 1)

                if first:
                    for u in range(U + 2):
                        if u < U:
                            turn_hot(u)
                        if 1 <= u <= U:
                            find_weights(u - 1)
                        if u >= 2:
                            sum_rows(u - 2)
                else:
                    for u in range(U):
                        sum_rows(u)

        if first:
            @block.scalar
            def _(act):
                with act.Fori(0, ITEM_TURNS) as turn:
                    for u in range(U):
                        act.wait_ge(hot_turned, turn * U + u + 1)
                        nc.scalar.copy(hot_t[:, u, :], ps_hot[:, u % 2, 0:P]).then_inc(hot_kept, 1)


def relational_update(nc, s, acc, h, x):
    with Stage(nc) as st:
        res = st.sb("res", [P, BLOCKS, DIM], F32)
        res_in, dve_done = st.sems("res_in", "dve_done")
        block = st.block()

        @block.sync
        def _(sp):
            sp.dma_start(res[:, :, :], node_view(s.res, DIM)).then_inc(res_in, 16)

        @block.vector
        def _(dve):
            link = link_on(dve, dve_done)
            dve.wait_ge(res_in, 16)
            link(nc.vector.scalar_tensor_tensor(h[:, :, :], acc[:, :, 0:DIM], 0.0, res[:, :, :], ALU.max, ALU.add))
            if x is not None:
                link(nc.vector.tensor_tensor(h[:, :, :], h[:, :, :], x[:, :, :], ALU.add))


SPAN_ITEMS = 13
assert ITEMS % (2 * SPAN_ITEMS) == 0


def attention_layer(nc, s, c, x, beta):
    with Stage(nc) as st:
        nx_t = st.sb("nx_t", [DIM, BLOCKS, P], F32)
        attention_prepare(nc, s, c, x, nx_t)
        score_loop(nc, s, c, nx_t)
    with Stage(nc) as st:
        prob = st.sb("prob", [P, ITEMS_PAD], F32)
        softmax_shift(nc, s, c, prob, beta)
        acc = st.sb("acc", [P, BLOCKS, W65], F32)
        weighted_loop(nc, s, c, prob, acc)
        with Stage(nc) as inner:
            h = inner.sb("h", [P, BLOCKS, DIM], F32)
            attention_update(nc, x, acc, h)
            layer_norm(nc, c, h, x)


def attention_prepare(nc, s, c, x, nx_t):
    with Stage(nc) as st:
        both = st.sb("both", [P, BLOCKS, 2 * DIM], F32)
        length = st.sb("length", [P, BLOCKS], F32)
        stage = st.sb("stage", [P, G, DIM], F32)
        ps_t = st.ps("ps_t", [DIM, G, P], F32)
        dve_done, squared, rooted, both_set, staged, turned, kept, out = st.sems(
            "dve_done", "squared", "rooted", "both_set", "staged", "turned", "kept", "out")
        block = st.block()
        shape = [P, BLOCKS, DIM]

        @block.vector
        def _(dve):
            link = link_on(dve, dve_done)
            link(nc.vector.tensor_tensor(both[:, :, 0:DIM], x[:, :, :], x[:, :, :], ALU.mult))
            nc.vector.tensor_reduce(length[:, :], both[:, :, 0:DIM], AX.X, ALU.add).then_inc(squared, 1)
            dve.wait_ge(rooted, 1)
            link(nc.vector.tensor_scalar(length[:, :], length[:, :], TINY, None, ALU.max))
            link(nc.vector.reciprocal(length[:, :], length[:, :]))
            link(nc.vector.tensor_copy(both[:, :, DIM:2 * DIM], x[:, :, :]))
            nc.vector.tensor_tensor(both[:, :, 0:DIM], x[:, :, :], length[:, :, None].to_broadcast(shape),
                                    ALU.mult).then_inc(both_set, 1)
            dve.wait_ge(both_set, 1)
            with dve.Fori(0, BLOCK_TURNS) as turn:
                dve.wait_ge(turned, turn)
                nc.vector.tensor_copy(stage[:, :, :], both[:, bass.ds(turn * G, G), 0:DIM]).then_inc(staged, 1)

        @block.scalar
        def _(act):
            act.wait_ge(squared, 1)
            nc.scalar.activation(length[:, :], length[:, :], ACT.Sqrt).then_inc(rooted, 1)
            with act.Fori(0, BLOCK_TURNS) as turn:
                act.wait_ge(turned, turn + 1)
                nc.scalar.copy(nx_t[:, bass.ds(turn * G, G), :], ps_t[:, :, :]).then_inc(kept, 1)

        @block.tensor
        def _(pe):
            with pe.Fori(0, BLOCK_TURNS) as turn:
                pe.wait_ge(staged, turn + 1)
                pe.wait_ge(kept, turn)
                hold(pe, c)
                for g in range(G):
                    last = nc.tensor.transpose(ps_t[:, g, :], stage[:, g, :], c.ident[:, :])
                last.then_inc(turned, 1)

        @block.sync
        def _(sp):
            sp.wait_ge(both_set, 1)
            sp.dma_start(node_view(s.nx, 2 * DIM), both[:, :, :]).then_inc(out, 16)
            sp.wait_ge(out, 16)


def score_loop(nc, s, c, nx_t):
    with Stage(nc) as st:
        rel = st.sb("rel", [P, ITEMS_PAD], F32)
        table = st.sb("table", [P, ITEMS_PAD], F32)
        score = st.sb("score", [P, ITEMS_PAD], F32)
        block_row = st.sb("block_row", [1, ITEMS_PAD], I32)
        index = st.sb("index", [P, U], I32)
        rows = st.sb("rows", [P, U, 2 * DIM], F32)
        rows_t = st.sb("rows_t", [DIM, U, P], F32)
        hot_dst = st.sb("hot_dst", [P, 2, P], BF16)
        scrap = st.sb("scrap", [P, P], F32)
        picked = st.sb("picked", [P, U], F32)
        ps_t = st.ps("ps_t", [DIM, 2, 512], F32)
        ps_all = st.ps("ps_all", [P, 2, 512], F32)
        tables_in, hot_set, index_set, turned, turned_kept, all_done, picks, score_set, score_out = st.sems(
            "tables_in", "hot_set", "index_set", "turned", "turned_kept", "all_done", "picks", "score_set", "score_out")
        got = [st.sem(f"got{u}") for u in range(U)]
        kept = st.sems("kept_a", "kept_b")
        block = st.block()

        @block.sync
        def _(sp):
            for t, source in ((rel, s.i_rel), (table, s.i_row), (block_row, s.block_x128.rearrange("(o a) b -> o (a b)", o=1))):
                sp.dma_start(t[:, :], source).then_inc(tables_in, 16)
            with sp.Fori(0, ITEM_TURNS) as turn:
                for h in range(2):
                    for u in range(h * HALF, (h + 1) * HALF):
                        sp.wait_ge(got[u], (turn + 1) * 16)
                    sp.dma_start(s.rows_kept[:, bass.ds((turn * U + h * HALF) * DIM, HALF * DIM)].rearrange("p (i d) -> p i d", d=DIM),
                                 rows[:, h * HALF:(h + 1) * HALF, DIM:2 * DIM]).then_inc(kept[h], 16)
            sp.wait_ge(score_set, ITEM_TURNS + 1)
            sp.dma_start(s.i_score, score[:, :]).then_inc(score_out, 16)
            sp.wait_ge(score_out, 16)
            for h in range(2):
                sp.wait_ge(kept[h], ITEM_TURNS * 16)

        @block.gpsimd
        def _(pool):
            with pool.Fori(0, ITEM_TURNS) as turn:
                for u in range(U):
                    if u % HALF == 0:
                        pool.wait_ge(index_set, turn * 2 + u // HALF + 1)
                        pool.wait_ge(kept[u // HALF], turn * 16)
                        hold(pool, c)
                    pool.indirect_dma_start(rows[:, u, :], None, s.nx,
                                            bass.IndirectOffsetOnAxis(ap=index[:, u:u + 1], axis=0)).then_inc(got[u], 16)

        @block.tensor
        def _(pe):
            pe.wait_ge(tables_in, 48)
            with pe.Fori(0, ITEM_TURNS) as turn:
                _, at = nc.values_load_multi_w_load_instructions(
                    block_row[0:1, bass.ds(turn * U, U)], engines=PE_ONLY, min_val=0, max_val=(BLOCKS - 1) * P,
                    skip_runtime_bounds_check_because="the item map clamps the block")
                nodes = nx_t[:, :, :].rearrange("d b n -> d (b n)")

                def multiply(u):
                    pe.wait_ge(turned_kept, turn * U + u + 1)
                    pe.wait_ge(picks, turn * U + max(u - 1, 0))
                    nc.tensor.matmul(ps_all[:, u % 2, 0:P], rows_t[:, u, :], nodes[:, bass.ds(at[u], P)],
                                     start=True, stop=True).then_inc(all_done, 1)

                for u in range(U):
                    pe.wait_ge(got[u], (turn + 1) * 16)
                    hold(pe, c)
                    nc.tensor.transpose(ps_t[:, u % 2, 0:P], rows[:, u, 0:DIM], c.ident[:, :]).then_inc(turned, 1)
                    if u >= 1:
                        multiply(u - 1)
                multiply(U - 1)

        @block.scalar
        def _(act):
            with act.Fori(0, ITEM_TURNS) as turn:
                for u in range(U):
                    act.wait_ge(turned, turn * U + u + 1)
                    nc.scalar.copy(rows_t[:, u, :], ps_t[:, u % 2, 0:P]).then_inc(turned_kept, 1)

        @block.vector
        def _(dve):
            nc.vector.memset(score[:, ITEMS:ITEMS_PAD], 0.0).then_inc(score_set, 1)
            dve.wait_ge(tables_in, 48)
            for h in range(2):
                part = slice(h * HALF, (h + 1) * HALF)
                nc.vector.tensor_copy(index[:, part], table[:, part]).then_inc(index_set, 1)
            with dve.Fori(0, ITEM_TURNS) as turn:
                for u in range(U):
                    nc.vector.tensor_scalar(hot_dst[:, u % 2, :], c.iota_b[:, :], rel[:, bass.ds(turn * U + u, 1)], None,
                                            ALU.is_equal).then_inc(hot_set, 1)
                    dve.wait_ge(hot_set, turn * U + u + 1)
                    dve.wait_ge(all_done, turn * U + u + 1)
                    nc.vector.tensor_tensor_reduce(out=scrap[:, :], in0=ps_all[:, u % 2, 0:P], in1=hot_dst[:, u % 2, :],
                                                   scale=1.0, scalar=0.0, op0=ALU.mult, op1=ALU.add,
                                                   accum_out=picked[:, u:u + 1]).then_inc(picks, 1)
                    if u % HALF == HALF - 1:
                        h = u // HALF
                        nc.vector.tensor_copy(index[:, h * HALF:(h + 1) * HALF],
                                              table[:, bass.ds((turn + 1) * U + h * HALF, HALF)]).then_inc(index_set, 1)
                dve.wait_ge(picks, (turn + 1) * U)
                nc.vector.tensor_copy(score[:, bass.ds(turn * U, U)], picked[:, :]).then_inc(score_set, 1)


def softmax_shift(nc, s, c, prob, beta):
    with Stage(nc) as st:
        score = st.sb("score", [P, CHUNKS, P], F32)
        val = st.sb("val", [P, CHUNKS * P], F32)
        cut = st.sb("cut", [P, CHUNKS * P], F32)
        cut_next = st.sb("cut_next", [P, CHUNKS * P], F32)
        off = st.sb("off", [P, CHUNKS * P], F32)
        run = st.sb("run", [P, CHUNKS * P], F32)
        beta_all = st.sb("beta_all", [P, 1], F32)
        edge = st.sb("edge", [P, 2], F32)
        edge_row = st.sb("edge_row", [1, 2, P], F32)
        carry_row = st.sb("carry_row", [1, P + 1], F32)
        carry = st.sb("carry", [P, 1], F32)
        ps = st.ps("ps", [P, 2, 4 * P], F32)
        ps_row = st.ps("ps_row", [1, 2, P], F32)
        ps_carry = st.ps("ps_carry", [P, 1], F32)
        loaded, chunks_turned, chunks_kept, dve_done = st.sems("loaded", "chunks_turned", "chunks_kept", "dve_done")
        edge_set, edge_turned, row_set, row_turned, exp_ready, exp_done = st.sems(
            "edge_set", "edge_turned", "row_set", "row_turned", "exp_ready", "exp_done")
        block = st.block()
        groups = [range(a, min(a + 4, CHUNKS)) for a in range(0, CHUNKS, 4)]
        N = len(groups)
        size = CHUNKS * P

        @block.sync
        def _(sp):
            sp.dma_start(score[:, :, :].rearrange("e c p -> e (c p)"), s.i_score).then_inc(loaded, 16)
            sp.dma_start(cut[:, :], s.i_cut[0:P * size].rearrange("(p k) -> p k", p=P)).then_inc(loaded, 16)
            sp.dma_start(cut_next[:, :], s.i_cut[1:P * size + 1].rearrange("(p k) -> p k", p=P)).then_inc(loaded, 16)
            sp.dma_start(off[:, :], s.i_off.rearrange("(p j) e -> p (j e)", p=P)).then_inc(loaded, 16)
            sp.dma_start(beta_all[:, :], beta.rearrange("(o k) -> o k", o=1).to_broadcast([P, 1])).then_inc(loaded, 16)

        @block.tensor
        def _(pe):
            pe.wait_ge(loaded, 80)
            by_item = score[:, :, :].rearrange("e c p -> e (c p)").rearrange("e (p j) -> e j p", j=CHUNKS)
            for n, group in enumerate(groups):
                if n >= 2:
                    pe.wait_ge(chunks_kept, n - 1)
                for k, j in enumerate(group):
                    last = nc.tensor.transpose(ps[:, n % 2, k * P:(k + 1) * P], by_item[:, j, :], c.ident[:, :])
                last.then_inc(chunks_turned, 1)
            for k in range(2):
                pe.wait_ge(edge_set, k + 1)
                for q in range(2):
                    last = nc.tensor.transpose(ps_row[0:1, q, :], edge[:, q:q + 1], c.ident[:, :])
                last.then_inc(edge_turned, 1)
                pe.wait_ge(row_set, k + 1)
                nc.tensor.transpose(ps_carry[:, :], carry_row[0:1, k:k + P], c.ident[0:1, 0:1]).then_inc(row_turned, 1)
            pe.wait_ge(exp_done, 1)
            for n, group in enumerate(groups):
                pe.wait_ge(chunks_kept, N + max(n - 1, 0))
                for k, j in enumerate(group):
                    last = nc.tensor.transpose(ps[:, n % 2, k * P:(k + 1) * P], val[:, j * P:(j + 1) * P], c.ident[:, :])
                last.then_inc(chunks_turned, 1)

        @block.scalar
        def _(act):
            act.wait_ge(exp_ready, 1)
            nc.scalar.activation(val[:, :], val[:, :], ACT.Exp).then_inc(exp_done, 1)

        @block.vector
        def _(dve):
            link = link_on(dve, dve_done)
            dve.wait_ge(loaded, 80)
            for n, group in enumerate(groups):
                dve.wait_ge(chunks_turned, n + 1)
                nc.vector.tensor_copy(val[:, group[0] * P:(group[-1] + 1) * P], ps[:, n % 2, 0:len(group) * P]
                                      ).then_inc(chunks_kept, 1)
            dve.wait_ge(chunks_kept, N)
            link(nc.vector.scalar_tensor_tensor(val[:, :], val[:, :], beta_all[:, 0:1], off[:, :], ALU.mult, ALU.add))

            def scan(out, cuts, values, start, back):
                step = slice(None, None, -1) if back else slice(None)
                link(nc.vector.tensor_tensor_scan(out[:, step], cuts[:, step], values[:, step], start, ALU.add, ALU.max))

            def carried(k, out, cuts, end):
                link(nc.vector.tensor_copy(edge[:, 0:1], out[:, end:end + 1]))
                nc.vector.tensor_reduce(edge[:, 1:2], cuts[:, :], AX.X, ALU.min).then_inc(edge_set, 1)
                dve.wait_ge(edge_turned, k + 1)
                link(nc.vector.tensor_copy(edge_row[:, :, :], ps_row[:, :, :]))
                link(nc.vector.memset(carry_row[:, :], -BIG))
                lanes = slice(None, None, -1) if k else slice(None)
                goes = carry_row[0:1, 1 - k:1 - k + P]
                nc.vector.tensor_tensor_scan(goes[:, lanes], edge_row[0:1, 1, :][:, lanes], edge_row[0:1, 0, :][:, lanes],
                                             -BIG, ALU.add, ALU.max).then_inc(row_set, 1)
                dve.wait_ge(row_turned, k + 1)
                link(nc.vector.tensor_copy(carry[:, :], ps_carry[:, :]))

            scan(run, cut, val, -BIG, back=False)
            carried(0, run, cut, size - 1)
            scan(run, cut, val, carry[:, 0:1], back=False)
            scan(off, cut_next, run, -BIG, back=True)
            carried(1, off, cut_next, 0)
            scan(off, cut_next, run, carry[:, 0:1], back=True)
            nc.vector.tensor_tensor(val[:, :], val[:, :], off[:, :], ALU.subtract).then_inc(exp_ready, 1)
            by_item = prob[:, :].rearrange("e (p j) -> e j p", j=CHUNKS)
            for n, group in enumerate(groups):
                dve.wait_ge(chunks_turned, N + n + 1)
                nc.vector.tensor_copy(by_item[:, group[0]:group[-1] + 1, :],
                                      ps[:, n % 2, 0:len(group) * P].rearrange("e (j p) -> e j p", p=P)).then_inc(chunks_kept, 1)


def weighted_loop(nc, s, c, prob, acc):
    V = 2 * SPAN_ITEMS
    with Stage(nc) as st:
        rel = st.sb("rel", [P, ITEMS_PAD], F32)
        rows = st.sb("rows", [P, V, W65], F32)
        share = st.sb("share", [P, 4, P], F32)
        ps_sum = st.ps("ps_sum", [P, 4, 512], F32)
        tables_in, ones_set, share_set, sum_done, sum_added = st.sems(
            "tables_in", "ones_set", "share_set", "sum_done", "sum_added")
        rows_in = st.sems("rows_in_a", "rows_in_b")
        block = st.block()

        @block.sync
        def _(sp):
            sp.dma_start(rel[:, :], s.i_rel).then_inc(tables_in, 16)

            def load(item, h):
                part = slice(h * SPAN_ITEMS, (h + 1) * SPAN_ITEMS)
                source = s.rows_kept[:, bass.ds(item * DIM, SPAN_ITEMS * DIM)].rearrange("p (i d) -> p i d", d=DIM)
                sp.dma_start(rows[:, part, 0:DIM], source).then_inc(rows_in[h], 16)

            for h in range(2):
                load(h * SPAN_ITEMS, h)
            with sp.Fori(0, ITEMS // V - 1) as turn:
                for h in range(2):
                    sp.wait_ge(sum_done, turn * V + (h + 1) * SPAN_ITEMS)
                    load((turn + 1) * V + h * SPAN_ITEMS, h)

        @block.vector
        def _(dve):
            nc.vector.memset(rows[:, :, DIM:W65], 1.0).then_inc(ones_set, 1)
            nc.vector.memset(acc[:, :, :], 0.0).then_inc(ones_set, 1)
            dve.wait_ge(tables_in, 16)
            dve.wait_ge(ones_set, 2)
            with dve.Fori(0, ITEMS // V) as turn:
                _, at = nc.values_load_multi_w_load_instructions(
                    c.block_row[0:1, bass.ds(turn * V, V)], engines=DVE_ONLY, min_val=0, max_val=(BLOCKS - 1) * W65,
                    skip_runtime_bounds_check_because="the item map clamps the block")
                acc_rows = acc[:, :, :].rearrange("p b d -> p (b d)")

                def add_sum(u):
                    dve.wait_ge(sum_done, turn * V + u + 1)
                    dve.wait_ge(sum_added, turn * V + u)
                    here = acc_rows[:, bass.ds(at[u], W65)]
                    nc.vector.tensor_tensor(here, here, ps_sum[:, u % 4, 0:W65], ALU.add).then_inc(sum_added, 1)

                for u in range(V + 2):
                    if u < V:
                        col = bass.ds(turn * V + u, 1)
                        nc.vector.tensor_scalar(share[:, u % 4, :], c.iota_b[:, :], rel[:, col], prob[:, col],
                                                ALU.is_equal, ALU.mult).then_inc(share_set, 1)
                    if u >= 2:
                        add_sum(u - 2)

        @block.tensor
        def _(pe):
            pe.wait_ge(ones_set, 1)
            with pe.Fori(0, ITEMS // V) as turn:
                for u in range(V):
                    if u % SPAN_ITEMS == 0:
                        pe.wait_ge(rows_in[u // SPAN_ITEMS], (turn + 1) * 16)
                    pe.wait_ge(share_set, turn * V + u + 1)
                    nc.tensor.matmul(ps_sum[:, u % 4, 0:W65], share[:, u % 4, :], rows[:, u, :],
                                     start=True, stop=True).then_inc(sum_done, 1)


def attention_update(nc, x, acc, h):
    with Stage(nc) as st:
        recip = st.sb("recip", [P, BLOCKS], F32)
        dve_done = st.sem("dve_done")
        block = st.block()

        @block.vector
        def _(dve):
            link = link_on(dve, dve_done)
            link(nc.vector.tensor_scalar(recip[:, :], acc[:, :, DIM], TINY, None, ALU.max))
            link(nc.vector.reciprocal(recip[:, :], recip[:, :]))
            link(nc.vector.tensor_tensor(h[:, :, :], acc[:, :, 0:DIM], recip[:, :, None].to_broadcast([P, BLOCKS, DIM]),
                                         ALU.mult))
            link(nc.vector.tensor_tensor(h[:, :, :], h[:, :, :], x[:, :, :], ALU.add))


def store_nodes(nc, x, out):
    with Stage(nc) as st:
        stored = st.sem("stored")
        block = st.block()
        full = NODES // P

        @block.sync
        def _(sp):
            sp.dma_start(out[0:full * P, :].rearrange("(b p) d -> p b d", p=P), x[:, 0:full, :]).then_inc(stored, 16)
            sp.dma_start(out[full * P:NODES, :], x[0:NODES - full * P, full, :]).then_inc(stored, 16)
            sp.wait_ge(stored, 32)


def graph_layers(nc, x_in, src, dst, edge_type, mean_weight, mean_bias, rel_weight, rel_root, rel_bias,
                 res_weight, res_bias, beta, out):
    with ExitStack() as ctx:
        Stage.made = 0
        c = Consts(nc, ctx)
        s = Scratch(nc)
        x = ctx.enter_context(nc.sbuf_tensor("x", [P, BLOCKS, DIM], F32))
        make_consts(nc, c)
        copy_edges(nc, s, src, dst, edge_type)
        item_tables(nc, s, c)
        tile_tables(nc, s, c)
        load_nodes(nc, x, x_in)
        mean_layer(nc, s, c, x, mean_weight, mean_bias)
        max_layer(nc, s, c, x)
        relational_layer(nc, s, c, x, rel_weight, rel_root, rel_bias, res_weight, res_bias)
        attention_layer(nc, s, c, x, beta)
        store_nodes(nc, x, out)


_INS = ["x", "src", "dst", "edge_type_65", "L0_gnn_weight", "L0_gnn_bias", "L2_gnn_W", "L2_gnn_root", "L2_gnn_bias",
        "L2_gnn_res_W", "L2_gnn_res_b", "L3_gnn_beta"]


def kernel(**inputs):
    import concourse.bacc as bacc
    from concourse.bass_utils import run_bass_kernel_spmd

    nc = bacc.Bacc("TRN2", target_bir_lowering=False, num_devices=1)
    arrays, args = {}, []
    for name in _INS:
        a = np.ascontiguousarray(inputs[name])
        arrays[f"in_{name}"] = a
        args.append(nc.dram_tensor(f"in_{name}", a.shape, mybir.dt.from_np(a.dtype), kind="ExternalInput").ap())
    out = nc.dram_tensor("out_x", (NODES, DIM), F32, kind="ExternalOutput").ap()
    graph_layers(nc, *args, out)
    return run_bass_kernel_spmd(nc, [arrays], core_ids=[0]).results[0]["out_x"]
```

```python
from contextlib import ExitStack

import numpy as np

import concourse.bass as bass
import concourse.mybir as mybir
from concourse.alu_op_type import AluOpType as ALU

F32 = mybir.dt.float32
BF16 = mybir.dt.bfloat16
I32 = mybir.dt.int32
ACT = mybir.ActivationFunctionType
AX = mybir.AxisListType
DVE_ONLY = [mybir.EngineType.DVE]
PE_ONLY = [mybir.EngineType.PE]

P = 128
NODES, EDGES, DIM, TYPES = 12500, 400000, 64, 65
BLOCKS = -(-NODES // P)
PADDED = BLOCKS * P
TILES = EDGES // P
U = 26
HALF = U // 2
ACCS = HALF
RING = 4
TU = 8
THALF = TU // 2
ITEM_TURNS = -(-(TILES + BLOCKS - 1) // U)
ITEMS = ITEM_TURNS * U
CHUNKS = -(-ITEMS // P)
ITEMS_PAD = CHUNKS * P
TILE_TURNS = -(-TILES // TU)
TILES_RUN = TILE_TURNS * TU
TCHUNKS = -(-TILES // P)
TILES_PAD = TCHUNKS * P
FLAT = EDGES // 125
TROW = TILES // 125
G = 7
BLOCK_TURNS = BLOCKS // G
W65 = DIM + 1
TRASH = PADDED
ACC_ROWS = PADDED + P
BANK = 512
BIG = 1e30
LN_EPS = 1e-5
TINY = 1e-12
SPAN = TYPES * DIM
BROW = 66

assert EDGES % P == 0 and TILES % 125 == 0 and BLOCKS % G == 0


def hold(engine, c):
    engine.sem_inc(c.held, 1)


def link_on(engine, sem):
    done = [0]

    def link(instruction):
        done[0] += 1
        instruction.then_inc(sem, 1)
        engine.wait_ge(sem, done[0])
        return instruction
    return link


class Stage:

    made = 0

    def __init__(self, nc):
        self.nc, self.stack = nc, ExitStack()
        Stage.made += 1
        self.tag = f"_{Stage.made}"
        self.semaphores = []

    def __enter__(self):
        self.stack.__enter__()
        return self

    def __exit__(self, *error):
        self.stack.__exit__(*error)
        if self.semaphores:
            self.nc.clear_and_free_semaphores(self.semaphores)
            self.nc.all_engine_barrier(sem_only=True)

    def sb(self, name, shape, dt):
        return self.stack.enter_context(self.nc.sbuf_tensor(name + self.tag, shape, dt))

    def ps(self, name, shape, dt):
        return self.stack.enter_context(self.nc.psum_tensor(name + self.tag, shape, dt))

    def sem(self, name):
        self.semaphores.append(self.nc.alloc_semaphore(name=name + self.tag))
        return self.semaphores[-1]

    def sems(self, *names):
        return [self.sem(name) for name in names]

    def block(self):
        return self.stack.enter_context(self.nc.Block())


class TurnCount:

    def __init__(self, engine, sem, turn, each):
        self.engine, self.sem, self.base, self.each, self.n = engine, sem, turn * each, each, 0

    def mark(self, instruction):
        self.n += 1
        instruction.then_inc(self.sem, 1)
        return self.n

    def wait(self, n):
        self.engine.wait_ge(self.sem, self.base + n)

    def close(self):
        assert self.n == self.each, (self.n, self.each)


def node_view(table, width):
    return table.rearrange("(p b) d -> p b d", p=P)


class Scratch:

    def __init__(self, nc):
        def dram(name, shape, dt):
            return nc.dram_tensor(name, shape, dt, kind="Internal").ap()

        self.e_src = dram("e_src", [EDGES], I32)
        self.e_dst = dram("e_dst", [EDGES], I32)
        self.e_type = dram("e_type", [EDGES], I32)
        self.e_prev = dram("e_prev", [EDGES + 1], I32)
        self.block_x65 = dram("block_x65", [CHUNKS, P], I32)
        self.block_x64 = dram("block_x64", [CHUNKS, P], I32)
        self.i_rel = dram("i_rel", [P, ITEMS_PAD], F32)
        self.i_row = dram("i_row", [P, ITEMS_PAD], F32)
        self.i_type = dram("i_type", [P, ITEMS_PAD], F32)
        self.i_rel_row = dram("i_rel_row", [P, ITEMS_PAD], F32)
        self.i_cut = dram("i_cut", [ITEMS_PAD * P + 1], F32)
        self.i_off = dram("i_off", [ITEMS_PAD, P], F32)
        self.i_srcrow = dram("i_srcrow", [ITEMS_PAD, P], F32)
        self.t_row = dram("t_row", [P, TILES_PAD], F32)
        self.t_cut = dram("t_cut", [TILES_RUN * P], F32)
        self.acc = [dram(f"acc{k}", [ACC_ROWS, W65], F32) for k in range(ACCS)]
        self.x = dram("x_state", [PADDED, DIM], F32)
        self.h = dram("h_state", [PADDED, DIM], F32)
        self.res = dram("res_state", [PADDED, DIM], F32)
        self.out_rel = dram("out_rel", [PADDED, W65], F32)
        self.counts = dram("counts", [P, BLOCKS * W65], F32)
        self.degree = dram("degree", [P, BLOCKS], F32)
        self.scanned = dram("scanned", [P * TILES_RUN, DIM], F32)
        self.g = dram("g_table", [PADDED, DIM], F32)
        self.i_weight = dram("i_weight", [P, ITEMS_PAD], F32)
        self.rel_table = dram("rel_table", [PADDED * TYPES, DIM], F32)
        self.nx = dram("nx_table", [PADDED, 2 * DIM], F32)


class Consts:

    def __init__(self, nc, ctx):
        def sb(name, shape, dt):
            return ctx.enter_context(nc.sbuf_tensor(name, shape, dt))

        self.held = ctx.enter_context(nc.semaphore("held"))
        self.iota_i = sb("iota_i", [P, P], I32)
        self.lane_i = sb("lane_i", [P, 1], I32)
        self.iota = sb("iota", [P, P], F32)
        self.iota_b = sb("iota_b", [P, P], BF16)
        self.lane = sb("lane", [P, 1], F32)
        self.ident = sb("ident", [P, P], F32)
        self.ident_b = sb("ident_b", [P, P], BF16)
        self.before = sb("before", [P, P], BF16)
        self.above = sb("above", [P, P], F32)
        self.upto = sb("upto", [P, P], F32)
        self.ones = sb("ones", [P, P], F32)
        self.eps = sb("eps", [P, 1], F32)
        self.block_row = sb("block_row", [1, ITEMS_PAD], I32)


def make_consts(nc, c):
    with Stage(nc) as st:
        iota_done, const_done = st.sems("iota_done", "const_done")
        block = st.block()
        @block.gpsimd
        def _(pool):
            nc.gpsimd.iota(c.iota_i[:, :], pattern=[[1, P]], base=0, channel_multiplier=0).then_inc(iota_done, 1)
            nc.gpsimd.iota(c.lane_i[:, :], pattern=[[0, 1]], base=0, channel_multiplier=1).then_inc(iota_done, 1)

        @block.vector
        def _(dve):
            link = link_on(dve, const_done)
            dve.wait_ge(iota_done, 2)
            link(nc.vector.tensor_copy(c.iota[:, :], c.iota_i[:, :]))
            link(nc.vector.tensor_copy(c.iota_b[:, :], c.iota_i[:, :]))
            link(nc.vector.tensor_copy(c.lane[:, :], c.lane_i[:, :]))
            for out, op in ((c.ident, ALU.is_equal), (c.ident_b, ALU.is_equal), (c.before, ALU.is_lt),
                            (c.above, ALU.is_gt), (c.upto, ALU.is_ge)):
                link(nc.vector.tensor_scalar(out[:, :], c.iota[:, :], c.lane[:, 0:1], None, op))
            link(nc.vector.memset(c.ones[:, :], 1.0))
            link(nc.vector.memset(c.eps[:, :], LN_EPS))


def copy_edges(nc, s, src, dst, edge_type):
    with Stage(nc) as st:
        minus = st.sb("minus", [1, 1], I32)
        minus_set, edges_in = st.sems("minus_set", "edges_in")
        block = st.block()
        @block.vector
        def _(dve):
            nc.vector.memset(minus[:, :], -1).then_inc(minus_set, 1)

        @block.sync
        def _(sp):
            def rows(t):
                return t.rearrange("(p k) -> p k", p=125)
            sp.dma_start(rows(s.e_src), rows(src)).then_inc(edges_in, 16)
            sp.dma_start(rows(s.e_dst), rows(dst)).then_inc(edges_in, 16)
            sp.dma_start(rows(s.e_type), rows(edge_type)).then_inc(edges_in, 16)
            sp.dma_start(rows(s.e_prev[1:EDGES + 1]), rows(dst)).then_inc(edges_in, 16)
            sp.wait_ge(minus_set, 1)
            sp.dma_start(s.e_prev[0:1].rearrange("(p k) -> p k", p=1), minus[:, :]).then_inc(edges_in, 16)
            sp.wait_ge(edges_in, 80)


def sort_edges(nc, s, c, src, dst, edge_type):
    with Stage(nc) as st:
        flag = st.sb("flag", [1, 1], I32)
        find_disorder(nc, s, c, flag)
        with Stage(nc) as inner:
            free = inner.sb("free", [P, BLOCKS], F32)
            sort_loop(nc, s, c, flag, dst, free)
            place_edges(nc, s, c, flag, src, dst, edge_type, free)
    with Stage(nc) as st:
        prev_in = st.sem("prev_in")
        block = st.block()

        @block.sync
        def _(sp):
            sp.dma_start(s.e_prev[1:EDGES + 1].rearrange("(p k) -> p k", p=125), s.e_dst.rearrange("(p k) -> p k", p=125)
                         ).then_inc(prev_in, 16)
            sp.wait_ge(prev_in, 16)


def find_disorder(nc, s, c, flag):
    with Stage(nc) as st:
        here = st.sb("here", [125, FLAT], I32)
        prev = st.sb("prev", [125, FLAT], I32)
        less = st.sb("less", [125, FLAT], F32)
        number = st.sb("number", [125, 1], F32)
        ps = st.ps("ps", [1, 1], F32)
        loaded, dve_done, counted, summed = st.sems("loaded", "dve_done", "counted", "summed")
        block = st.block()

        @block.sync
        def _(sp):
            sp.dma_start(here[:, :], s.e_dst.rearrange("(p k) -> p k", p=125)).then_inc(loaded, 16)
            sp.dma_start(prev[:, :], s.e_prev[0:EDGES].rearrange("(p k) -> p k", p=125)).then_inc(loaded, 16)

        @block.vector
        def _(dve):
            link = link_on(dve, dve_done)
            dve.wait_ge(loaded, 32)
            link(nc.vector.tensor_tensor(less[:, :], here[:, :], prev[:, :], ALU.is_lt))
            nc.vector.tensor_reduce(number[:, :], less[:, :], AX.X, ALU.add).then_inc(counted, 1)
            dve.wait_ge(summed, 1)
            link(nc.vector.tensor_copy(flag[:, :], ps[:, :]))

        @block.tensor
        def _(pe):
            pe.wait_ge(counted, 1)
            nc.tensor.matmul(ps[:, :], number[:, :], c.ones[0:125, 0:1], start=True, stop=True).then_inc(summed, 1)


def read_flag(engine, flag):
    return engine.value_load(flag[0:1, 0:1], min_val=0, max_val=EDGES)


def hot_node(nc, step, c, ids, parts_i, parts, hot_lane, hot_block):
    step(nc.vector.tensor_scalar(parts_i[:, 0:1], ids, P - 1, None, ALU.bitwise_and))
    step(nc.vector.tensor_scalar(parts_i[:, 1:2], ids, 7, None, ALU.logical_shift_right))
    step(nc.vector.tensor_copy(parts[:, :], parts_i[:, :]))
    step(nc.vector.tensor_scalar(hot_lane[:, :], c.iota[:, :], parts[:, 0:1], None, ALU.is_equal))
    step(nc.vector.tensor_scalar(hot_block[:, :], c.iota[:, 0:BLOCKS], parts[:, 1:2], None, ALU.is_equal))


def sort_loop(nc, s, c, flag, dst, free):
    with Stage(nc) as st:
        ids = st.sb("ids", [P, 1], I32)
        parts_i = st.sb("parts_i", [P, 2], I32)
        parts = st.sb("parts", [P, 2], F32)
        hot_lane = st.sb("hot_lane", [P, P], F32)
        hot_block = st.sb("hot_block", [P, BLOCKS], F32)
        total = st.sb("total", [P, BLOCKS], F32)
        upto = st.sb("upto", [P, BLOCKS], F32)
        ps_count = st.ps("ps_count", [P, BLOCKS], F32)
        ps_in = st.ps("ps_in", [P, BLOCKS], F32)
        ps_total = st.ps("ps_total", [P, BLOCKS], F32)
        cleared, ids_in, chain, hot_set, counted, added, summed, dve_done = st.sems(
            "cleared", "ids_in", "chain", "hot_set", "counted", "added", "summed", "dve_done")
        block = st.block()

        @block.sync
        def _(sp):
            disorder = read_flag(sp, flag)
            with sp.If(disorder != 0):
                with sp.Fori(0, TILES) as tile:
                    sp.wait_ge(added, tile)
                    sp.dma_start(ids[:, :], dst[bass.ds(tile * P, P)].rearrange("(p k) -> p k", k=1)).then_inc(ids_in, 16)

        @block.tensor
        def _(pe):
            disorder = read_flag(pe, flag)
            with pe.If(disorder != 0):
                with pe.Fori(0, TILES) as tile:
                    pe.wait_ge(hot_set, tile + 1)
                    nc.tensor.matmul(ps_count[:, :], hot_lane[:, :], hot_block[:, :], start=True, stop=True).then_inc(counted, 1)
                pe.wait_ge(added, TILES)
                nc.tensor.matmul(ps_in[:, :], c.above[:, :], free[:, :], start=True, stop=True)
                nc.tensor.matmul(ps_total[:, :], c.ones[:, :], free[:, :], start=True, stop=True).then_inc(summed, 1)

        @block.vector
        def _(dve):
            nc.vector.memset(free[:, :], 0.0).then_inc(cleared, 1)
            dve.wait_ge(cleared, 1)
            disorder = read_flag(dve, flag)
            with dve.If(disorder != 0):
                with dve.Fori(0, TILES) as tile:
                    steps = TurnCount(dve, chain, tile, 5)
                    dve.wait_ge(ids_in, (tile + 1) * 16)
                    hot_node(nc, lambda i: steps.wait(steps.mark(i)), c, ids[:, :], parts_i, parts, hot_lane, hot_block)
                    steps.close()
                    dve.sem_inc(hot_set, 1)
                    dve.wait_ge(counted, tile + 1)
                    nc.vector.tensor_tensor(free[:, :], free[:, :], ps_count[:, :], ALU.add).then_inc(added, 1)
                link = link_on(dve, dve_done)
                dve.wait_ge(summed, 1)
                link(nc.vector.tensor_copy(total[:, :], ps_total[:, :]))
                link(nc.vector.tensor_tensor_scan(upto[:, :], c.ones[:, 0:BLOCKS], total[:, :], 0.0, ALU.mult, ALU.add))
                link(nc.vector.tensor_tensor(upto[:, :], upto[:, :], total[:, :], ALU.subtract))
                link(nc.vector.tensor_tensor(free[:, :], upto[:, :], ps_in[:, :], ALU.add))


def place_edges(nc, s, c, flag, src, dst, edge_type, free):
    with Stage(nc) as st:
        edge = st.sb("edge", [P, 3], I32)
        row = st.sb("row", [P, P], I32)
        parts_i = st.sb("parts_i", [P, 2], I32)
        parts = st.sb("parts", [P, 2], F32)
        ids = st.sb("ids", [P, 1], F32)
        hot_lane = st.sb("hot_lane", [P, P], F32)
        hot_block = st.sb("hot_block", [P, BLOCKS], F32)
        hot_t = st.sb("hot_t", [P, P], F32)
        same = st.sb("same", [P, P], F32)
        scrap = st.sb("scrap", [P, P], F32)
        earlier = st.sb("earlier", [P, 1], F32)
        first = st.sb("first", [P, 1], F32)
        place = st.sb("place", [P, 1], I32)
        ps_t = st.ps("ps_t", [P, P], F32)
        ps_free = st.ps("ps_free", [P, BLOCKS], F32)
        ps_count = st.ps("ps_count", [P, BLOCKS], F32)
        edge_in, chain, hot_set, turned, kept, looked_up, counted, placed, tile_done = st.sems(
            "edge_in", "chain", "hot_set", "turned", "kept", "looked_up", "counted", "placed", "tile_done")
        block = st.block()

        @block.sync
        def _(sp):
            disorder = read_flag(sp, flag)
            with sp.If(disorder != 0):
                with sp.Fori(0, TILES) as tile:
                    sp.wait_ge(tile_done, tile)
                    for k, t in enumerate((src, dst, edge_type)):
                        sp.dma_start(edge[:, k:k + 1], t[bass.ds(tile * P, P)].rearrange("(p k) -> p k", k=1)
                                     ).then_inc(edge_in, 16)
                    sp.dma_start(row[:, :], dst.rearrange("(o k) -> o k", o=1)[:, bass.ds(tile * P, P)].to_broadcast([P, P])
                                 ).then_inc(edge_in, 16)

        @block.tensor
        def _(pe):
            disorder = read_flag(pe, flag)
            with pe.If(disorder != 0):
                with pe.Fori(0, TILES) as tile:
                    pe.wait_ge(hot_set, tile + 1)
                    nc.tensor.matmul(ps_count[:, :], hot_lane[:, :], hot_block[:, :], start=True, stop=True)
                    nc.tensor.transpose(ps_t[:, :], hot_lane[:, :], c.ident[:, :]).then_inc(turned, 1)
                    pe.wait_ge(kept, tile + 1)
                    nc.tensor.matmul(ps_free[:, :], hot_t[:, :], free[:, :], start=True, stop=True).then_inc(looked_up, 1)

        @block.vector
        def _(dve):
            disorder = read_flag(dve, flag)
            with dve.If(disorder != 0):
                with dve.Fori(0, TILES) as tile:
                    steps = TurnCount(dve, chain, tile, 10)

                    def step(i):
                        steps.wait(steps.mark(i))
                    dve.wait_ge(edge_in, (tile + 1) * 64)
                    hot_node(nc, step, c, edge[:, 1:2], parts_i, parts, hot_lane, hot_block)
                    dve.sem_inc(hot_set, 1)
                    step(nc.vector.tensor_copy(ids[:, :], edge[:, 1:2]))
                    step(nc.vector.tensor_scalar(same[:, :], row[:, :], ids[:, 0:1], None, ALU.is_equal))
                    step(nc.vector.tensor_tensor_reduce(out=scrap[:, :], in0=same[:, :], in1=c.before[:, :], scale=1.0,
                                                        scalar=0.0, op0=ALU.mult, op1=ALU.add, accum_out=earlier[:, :]))
                    dve.wait_ge(turned, tile + 1)
                    nc.vector.tensor_copy(hot_t[:, :], ps_t[:, :]).then_inc(kept, 1)
                    dve.wait_ge(looked_up, tile + 1)
                    step(nc.vector.tensor_tensor_reduce(out=scrap[:, 0:BLOCKS], in0=ps_free[:, :], in1=hot_block[:, :],
                                                        scale=1.0, scalar=0.0, op0=ALU.mult, op1=ALU.add,
                                                        accum_out=first[:, :]))
                    step(nc.vector.tensor_tensor(free[:, :], free[:, :], ps_count[:, :], ALU.add))
                    nc.vector.tensor_tensor(place[:, :], first[:, :], earlier[:, :], ALU.add).then_inc(counted, 1)
                    steps.close()

        @block.gpsimd
        def _(pool):
            disorder = read_flag(pool, flag)
            with pool.If(disorder != 0):
                with pool.Fori(0, TILES) as tile:
                    pool.wait_ge(counted, tile + 1)
                    hold(pool, c)
                    for k, t in enumerate((s.e_src, s.e_dst, s.e_type)):
                        pool.indirect_dma_start(t.rearrange("(e k) -> e k", k=1),
                                                bass.IndirectOffsetOnAxis(ap=place[:, 0:1], axis=0),
                                                edge[:, k:k + 1], None).then_inc(placed, 16)
                    pool.wait_ge(placed, (tile + 1) * 48)
                    pool.sem_inc(tile_done, 1)


def map_items(nc, s, c, tile_of, rel_of):
    with Stage(nc) as st:
        last_dst = st.sb("last_dst", [125, TROW], I32)
        tile_id = st.sb("tile_id", [125, TROW], I32)
        key = st.sb("key", [125, TROW], I32)
        key_part = st.sb("key_part", [125, TROW], I32)
        key_hi = st.sb("key_hi", [125, TROW], F32)
        key_lo = st.sb("key_lo", [125, TROW], F32)
        hot_hi = st.sb("hot_hi", [125, TROW, CHUNKS], BF16)
        hot_lo = st.sb("hot_lo", [125, TROW, P], BF16)
        marks = st.sb("marks", [CHUNKS, P], F32)
        upto_here = st.sb("upto_here", [CHUNKS, P], F32)
        tiles_before = st.sb("tiles_before", [CHUNKS, P], F32)
        item_id_i = st.sb("item_id_i", [P, CHUNKS], I32)
        item_id = st.sb("item_id", [P, CHUNKS], F32)
        tiles_t = st.sb("tiles_t", [P, CHUNKS], F32)
        past_end = st.sb("past_end", [P, CHUNKS], F32)
        block_f = st.sb("block_f", [P, CHUNKS], F32)
        block_i = st.sb("block_i", [CHUNKS, 2, P], I32)
        ps_marks = st.ps("ps_marks", [CHUNKS, P], F32)
        ps_sum = st.ps("ps_sum", [CHUNKS, 1], F32)
        ps_t = st.ps("ps_t", [P, CHUNKS], F32)
        ps_b = st.ps("ps_b", [CHUNKS, P], F32)
        last_in, ids_set, map_dve, hot_set, marked, scan_set, summed, before_set, turned, blocks_set, blocks_turned, row_set, row_out = st.sems("last_in", "ids_set", "map_dve", "hot_set", "marked", "scan_set", "summed", "before_set", "turned", "blocks_set", "blocks_turned", "row_set", "row_out")
        block = st.block()

        @block.sync
        def _(sp):
            last = s.e_dst.rearrange("(p j e) -> p j e", j=TROW, e=P)[:, :, P - 1]
            with nc.allow_non_contiguous_dma(reason="one value of each tile"):
                sp.dma_start(last_dst[:, :], last).then_inc(last_in, 16)
            sp.wait_ge(row_set, 1)
            sp.dma_start(s.block_x65, block_i[:, 0, :]).then_inc(row_out, 16)
            sp.dma_start(s.block_x64, block_i[:, 1, :]).then_inc(row_out, 16)
            sp.wait_ge(row_out, 32)
            sp.dma_start(c.block_row[:, :], s.block_x65.rearrange("(o a) b -> o (a b)", o=1)).then_inc(row_out, 16)
            sp.wait_ge(row_out, 48)

        @block.gpsimd
        def _(pool):
            nc.gpsimd.iota(tile_id[:, :], pattern=[[1, TROW]], base=0, channel_multiplier=TROW).then_inc(ids_set, 1)
            nc.gpsimd.iota(item_id_i[:, :], pattern=[[P, CHUNKS]], base=0, channel_multiplier=1).then_inc(ids_set, 1)

        @block.vector
        def _(dve):
            link = link_on(dve, map_dve)
            dve.wait_ge(last_in, 16)
            dve.wait_ge(ids_set, 2)
            link(nc.vector.tensor_scalar(key[:, :], last_dst[:, :], 7, None, ALU.logical_shift_right))
            link(nc.vector.tensor_tensor(key[:, :], key[:, :], tile_id[:, :], ALU.add))
            link(nc.vector.tensor_scalar(key_part[:, :], key[:, :], 7, None, ALU.logical_shift_right))
            link(nc.vector.tensor_copy(key_hi[:, :], key_part[:, :]))
            link(nc.vector.tensor_scalar(key_part[:, :], key[:, :], P - 1, None, ALU.bitwise_and))
            link(nc.vector.tensor_copy(key_lo[:, :], key_part[:, :]))
            link(nc.vector.tensor_tensor(hot_hi[:, :, :], key_hi[:, :, None].to_broadcast([125, TROW, CHUNKS]),
                                         c.iota[0:125, None, 0:CHUNKS].to_broadcast([125, TROW, CHUNKS]), ALU.is_equal))
            nc.vector.tensor_tensor(hot_lo[:, :, :], key_lo[:, :, None].to_broadcast([125, TROW, P]),
                                    c.iota[0:125, None, :].to_broadcast([125, TROW, P]), ALU.is_equal).then_inc(hot_set, 1)
            dve.wait_ge(marked, 1)
            link(nc.vector.tensor_copy(marks[:, :], ps_marks[:, :]))
            nc.vector.tensor_tensor_scan(upto_here[:, :], c.ones[0:CHUNKS, :], marks[:, :], 0.0,
                                         ALU.mult, ALU.add).then_inc(scan_set, 1)
            dve.wait_ge(scan_set, 1)
            dve.wait_ge(summed, 1)
            link(nc.vector.tensor_tensor(tiles_before[:, :], upto_here[:, :], marks[:, :], ALU.subtract))
            nc.vector.tensor_scalar(tiles_before[:, :], tiles_before[:, :], ps_sum[:, 0:1], None,
                                    ALU.add).then_inc(before_set, 1)
            dve.wait_ge(turned, 1)
            link(nc.vector.tensor_copy(tiles_t[:, :], ps_t[:, :]))
            link(nc.vector.tensor_copy(item_id[:, :], item_id_i[:, :]))
            link(nc.vector.tensor_tensor(block_f[:, :], item_id[:, :], tiles_t[:, :], ALU.subtract))
            link(nc.vector.tensor_scalar(past_end[:, :], tiles_t[:, :], float(TILES), 1000.0, ALU.is_ge, ALU.mult))
            link(nc.vector.tensor_tensor(rel_of[:, :], block_f[:, :], past_end[:, :], ALU.add))
            link(nc.vector.tensor_scalar(rel_of[:, :], rel_of[:, :], float(P), None, ALU.mult))
            link(nc.vector.tensor_scalar(tile_of[:, :], tiles_t[:, :], float(TILES - 1), None, ALU.min))
            nc.vector.tensor_scalar(block_f[:, :], block_f[:, :], float(BLOCKS - 1), None, ALU.min).then_inc(blocks_set, 1)
            dve.wait_ge(blocks_turned, 1)
            nc.vector.tensor_scalar(block_i[:, 0, :], ps_b[:, :], float(W65), None, ALU.mult)
            nc.vector.tensor_scalar(block_i[:, 1, :], ps_b[:, :], float(DIM), None, ALU.mult).then_inc(row_set, 1)

        @block.tensor
        def _(pe):
            pe.wait_ge(hot_set, 1)
            for j in range(TROW):
                last = nc.tensor.matmul(ps_marks[:, :], hot_hi[:, j, :], hot_lo[:, j, :],
                                        start=(j == 0), stop=(j == TROW - 1))
            last.then_inc(marked, 1)
            pe.wait_ge(scan_set, 1)
            nc.tensor.matmul(ps_sum[:, :], c.above[0:CHUNKS, 0:CHUNKS], upto_here[:, P - 1:P],
                             start=True, stop=True).then_inc(summed, 1)
            pe.wait_ge(before_set, 1)
            nc.tensor.transpose(ps_t[:, :], tiles_before[:, :], c.ident[0:CHUNKS, 0:CHUNKS]).then_inc(turned, 1)
            pe.wait_ge(blocks_set, 1)
            nc.tensor.transpose(ps_b[:, :], block_f[:, :], c.ident[:, :]).then_inc(blocks_turned, 1)


def turn_chunks(nc, c, source, out, chunks):
    with Stage(nc) as st:
        ps = st.ps("ps_turn", [P, 2, 4 * P], F32)
        turned, kept = st.sems("turned", "kept")
        block = st.block()
        groups = [range(a, min(a + 4, chunks)) for a in range(0, chunks, 4)]

        @block.tensor
        def _(pe):
            for n, group in enumerate(groups):
                if n >= 2:
                    pe.wait_ge(kept, n - 1)
                for k, chunk in enumerate(group):
                    last = nc.tensor.transpose(ps[:, n % 2, k * P:(k + 1) * P], source[:, chunk, :], c.ident[:, :])
                last.then_inc(turned, 1)

        @block.vector
        def _(dve):
            for n, group in enumerate(groups):
                dve.wait_ge(turned, n + 1)
                nc.vector.tensor_copy(out[:, group[0] * P:(group[-1] + 1) * P],
                                      ps[:, n % 2, 0:len(group) * P]).then_inc(kept, 1)


def item_tables(nc, s, c):
    with Stage(nc) as st:
        tile_of = st.sb("tile_of", [P, CHUNKS], I32)
        rel_of = st.sb("rel_of", [P, CHUNKS], F32)
        map_items(nc, s, c, tile_of, rel_of)
        shape = [P, CHUNKS, P]
        flat = "p c e -> p (c e)"
        with Stage(nc) as st:
            raw = st.sb("raw", [P, 2, CHUNKS, P], I32)
            val = st.sb("val", [P, CHUNKS, P], F32)
            off = st.sb("off", [P, CHUNKS, P], F32)
            other = st.sb("other", [P, CHUNKS, P], F32)
            table = st.sb("table", [P, ITEMS_PAD], F32)
            end = st.sb("end", [1, 1], F32)
            with Stage(nc) as st:
                dst_in, prev_in, dst_dve, cut_set, cut_out = st.sems("dst_in", "prev_in", "dst_dve", "cut_set", "cut_out")
                block = st.block()
                @block.gpsimd
                def _(pool):
                    for which, table_, sem in ((0, s.e_dst, dst_in), (1, s.e_prev[0:EDGES], prev_in)):
                        rows = table_.rearrange("(t e) -> t e", e=P)
                        for k in range(CHUNKS):
                            pool.indirect_dma_start(raw[:, which, k, :], None, rows,
                                                    bass.IndirectOffsetOnAxis(ap=tile_of[:, k:k + 1], axis=0)).then_inc(sem, 16)

                @block.vector
                def _(dve):
                    link = link_on(dve, dst_dve)
                    link(nc.vector.memset(end[:, :], 0.0))
                    dve.wait_ge(dst_in, 16 * CHUNKS)
                    dve.wait_ge(prev_in, 16 * CHUNKS)
                    link(nc.vector.tensor_copy(val[:, :, :], raw[:, 0, :, :]))
                    link(nc.vector.tensor_copy(other[:, :, :], raw[:, 1, :, :]))
                    link(nc.vector.tensor_tensor(other[:, :, :], other[:, :, :], val[:, :, :], ALU.not_equal))
                    link(nc.vector.tensor_tensor(val[:, :, :], val[:, :, :], rel_of[:, :, None].to_broadcast(shape),
                                                 ALU.subtract))
                    link(nc.vector.tensor_scalar(off[:, :, :], val[:, :, :], 0.0, None, ALU.is_ge))
                    link(nc.vector.scalar_tensor_tensor(off[:, :, :].rearrange(flat), val[:, :, :].rearrange(flat), float(P),
                                                        off[:, :, :].rearrange(flat), ALU.is_lt, ALU.mult))
                    link(nc.vector.scalar_tensor_tensor(other[:, :, :].rearrange(flat), other[:, :, :].rearrange(flat), -BIG,
                                                        off[:, :, :].rearrange(flat), ALU.mult, ALU.mult))
                    link(nc.vector.tensor_scalar(off[:, :, :], off[:, :, :], 1.0, BIG, ALU.subtract, ALU.mult))
                    nc.vector.tensor_scalar(val[:, :, :], val[:, :, :], -1.0, float(P), ALU.max, ALU.min).then_inc(cut_set, 1)

                @block.sync
                def _(sp):
                    sp.wait_ge(cut_set, 1)
                    sp.dma_start(s.i_cut[0:ITEMS_PAD * P].rearrange("(c p e) -> p c e", p=P, e=P), other[:, :, :]).then_inc(cut_out, 16)
                    sp.dma_start(s.i_off.rearrange("(c p) e -> p c e", p=P), off[:, :, :]).then_inc(cut_out, 16)
                    sp.dma_start(s.i_cut[ITEMS_PAD * P:].rearrange("(p k) -> p k", p=1), end[:, :]).then_inc(cut_out, 16)
                    sp.wait_ge(cut_out, 48)
            turn_chunks(nc, c, val, table, CHUNKS)
            with Stage(nc) as st:
                rel_out, src_in, type_in, src_dve, srow_set, srow_out = st.sems("rel_out", "src_in", "type_in", "src_dve", "srow_set", "srow_out")
                block = st.block()
                @block.gpsimd
                def _(pool):
                    for which, table_, sem in ((0, s.e_src, src_in), (1, s.e_type, type_in)):
                        rows = table_.rearrange("(t e) -> t e", e=P)
                        for k in range(CHUNKS):
                            pool.indirect_dma_start(raw[:, which, k, :], None, rows,
                                                    bass.IndirectOffsetOnAxis(ap=tile_of[:, k:k + 1], axis=0)).then_inc(sem, 16)

                @block.vector
                def _(dve):
                    link = link_on(dve, src_dve)
                    dve.wait_ge(src_in, 16 * CHUNKS)
                    node_rows(nc, link, val[:, :, :], other[:, :, :], raw[:, 0, :, :], off[:, :, :].bitcast(I32))
                    dve.wait_ge(type_in, 16 * CHUNKS)
                    link(nc.vector.tensor_copy(other[:, :, :], raw[:, 1, :, :]))
                    nc.vector.scalar_tensor_tensor(off[:, :, :].rearrange(flat), val[:, :, :].rearrange(flat), float(TYPES),
                                                   other[:, :, :].rearrange(flat), ALU.mult, ALU.add).then_inc(srow_set, 1)

                @block.sync
                def _(sp):
                    sp.dma_start(s.i_rel, table[:, :]).then_inc(rel_out, 16)
                    sp.wait_ge(srow_set, 1)
                    sp.dma_start(s.i_srcrow.rearrange("(c p) e -> p c e", p=P), val[:, :, :]).then_inc(srow_out, 16)
                    sp.wait_ge(rel_out, 16)
                    sp.wait_ge(srow_out, 16)
            for source, dest in ((val, s.i_row), (other, s.i_type), (off, s.i_rel_row)):
                turn_chunks(nc, c, source, table, CHUNKS)
                store(nc, dest, table[:, :])


def node_rows(nc, link, out, spare, ids, spare_i):
    link(nc.vector.tensor_scalar(spare_i, ids, P - 1, None, ALU.bitwise_and))
    link(nc.vector.tensor_copy(out, spare_i))
    link(nc.vector.tensor_scalar(out, out, float(BLOCKS), None, ALU.mult))
    link(nc.vector.tensor_scalar(spare_i, ids, 7, None, ALU.logical_shift_right))
    link(nc.vector.tensor_copy(spare, spare_i))
    link(nc.vector.tensor_tensor(out, out, spare, ALU.add))


def store(nc, dest, source):
    with Stage(nc) as st:
        stored = st.sem("stored")
        block = st.block()
        @block.sync
        def _(sp):
            sp.dma_start(dest, source).then_inc(stored, 16)
            sp.wait_ge(stored, 16)


def tile_tables(nc, s, c):
    with Stage(nc) as st:
        raw = st.sb("t_raw", [P, TCHUNKS, P], I32)
        val = st.sb("t_val", [P, TCHUNKS, P], F32)
        spare = st.sb("t_spare", [P, TCHUNKS, P], F32)
        spare_i = st.sb("t_spare_i", [P, TCHUNKS, P], I32)
        table = st.sb("t_table", [P, TILES_PAD], F32)
        full = TILES // P
        rest = TILES - full * P
        with Stage(nc) as st:
            raw_set, raw_in, dve_done = st.sems("traw_set", "traw_in", "tsrc_dve")
            block = st.block()
            @block.gpsimd
            def _(pool):
                nc.gpsimd.memset(raw[:, full, :], 0).then_inc(raw_set, 1)

            @block.sync
            def _(sp):
                rows = s.e_src.rearrange("(t e) -> t e", e=P)
                sp.dma_start(raw[:, 0:full, :], rows[0:full * P, :].rearrange("(c p) e -> p c e", p=P)).then_inc(raw_in, 16)
                sp.wait_ge(raw_set, 1)
                sp.dma_start(raw[0:rest, full, :], rows[full * P:TILES, :]).then_inc(raw_in, 16)

            @block.vector
            def _(dve):
                dve.wait_ge(raw_in, 32)
                node_rows(nc, link_on(dve, dve_done), val[:, :, :], spare[:, :, :], raw[:, :, :], spare_i[:, :, :])
        turn_chunks(nc, c, val, table, TCHUNKS)
        store(nc, s.t_row, table[:, :])
        with Stage(nc) as st:
            cut_raw = st.sb("cut_raw", [125, FLAT], I32)
            cut_prev = st.sb("cut_prev", [125, FLAT], I32)
            cut = st.sb("cut", [125, FLAT], F32)
            pad = st.sb("cut_pad", [1, (TILES_RUN - TILES) * P], F32)
            cutraw_in, cutd_dve, cutd_set, cutd_out = st.sems("cutraw_in", "cutd_dve", "cutd_set", "cutd_out")
            block = st.block()
            @block.sync
            def _(sp):
                sp.dma_start(cut_raw[:, :], s.e_dst.rearrange("(p k) -> p k", p=125)).then_inc(cutraw_in, 16)
                sp.dma_start(cut_prev[:, :], s.e_prev[0:EDGES].rearrange("(p k) -> p k", p=125)).then_inc(cutraw_in, 16)
                sp.wait_ge(cutd_set, 2)
                sp.dma_start(s.t_cut[0:EDGES].rearrange("(p k) -> p k", p=125), cut[:, :]).then_inc(cutd_out, 16)
                sp.dma_start(s.t_cut[EDGES:TILES_RUN * P].rearrange("(p k) -> p k", p=1), pad[:, :]).then_inc(cutd_out, 16)
                sp.wait_ge(cutd_out, 32)

            @block.vector
            def _(dve):
                link = link_on(dve, cutd_dve)
                nc.vector.memset(pad[:, :], 0.0).then_inc(cutd_set, 1)
                dve.wait_ge(cutraw_in, 32)
                link(nc.vector.tensor_tensor(cut[:, :], cut_raw[:, :], cut_prev[:, :], ALU.not_equal))
                nc.vector.tensor_scalar(cut[:, :], cut[:, :], -BIG, None, ALU.mult).then_inc(cutd_set, 1)


def load_nodes(nc, x, x_in):
    with Stage(nc) as st:
        cleared, rows_in = st.sems("cleared", "rows_in")
        block = st.block()
        full = NODES // P

        @block.vector
        def _(dve):
            nc.vector.memset(x[:, full, :], 0.0).then_inc(cleared, 1)

        @block.sync
        def _(sp):
            sp.dma_start(x[:, 0:full, :], x_in[0:full * P, :].rearrange("(b p) d -> p b d", p=P)).then_inc(rows_in, 16)
            sp.wait_ge(cleared, 1)
            sp.dma_start(x[0:NODES - full * P, full, :], x_in[full * P:NODES, :]).then_inc(rows_in, 16)
            sp.wait_ge(rows_in, 32)


def clear_accumulators(nc, s):
    with Stage(nc) as st:
        zero = st.sb("zero", [P, ACC_ROWS // P * W65], F32)
        cleared, zero_out = st.sems("cleared", "zero_out")
        block = st.block()

        @block.vector
        def _(dve):
            nc.vector.memset(zero[:, :], 0.0).then_inc(cleared, 1)

        @block.sync
        def _(sp):
            sp.wait_ge(cleared, 1)
            for acc in s.acc:
                sp.dma_start(acc.rearrange("(p b) d -> p (b d)", p=P), zero[:, :]).then_inc(zero_out, 16)
            sp.wait_ge(zero_out, 16 * ACCS)


def mean_loop(nc, s, c, x, counts):
    LAG = 3
    with Stage(nc) as st:
        x1 = st.sb("x1", [P, BLOCKS, W65], F32)
        rel = st.sb("rel", [P, ITEMS_PAD], F32)
        row = st.sb("row", [P, ITEMS_PAD], F32)
        typ = st.sb("typ", [P, ITEMS_PAD], F32)
        trash = st.sb("trash", [P, 1], F32)
        src_rows = st.sb("src_rows", [P, U, P], F32)
        same = st.sb("same", [P, 2 * RING, P], BF16)
        hot_dst = st.sb("hot_dst", [P, 2 * RING, P], BF16)
        hot_type = st.sb("hot_type", [P, 2 * RING, TYPES], BF16)
        scrap = st.sb("scrap", [P, P], BF16)
        earlier = st.sb("earlier", [P, U], F32)
        shift = st.sb("shift", [P, U], F32)
        target = st.sb("target", [P, U], I32)
        goes = st.sb("goes", [P, RING, P], F32)
        sums = st.sb("sums", [P, ACCS, W65], F32)
        ps_goes = st.ps("ps_goes", [P, 3, BANK], F32)
        ps_count = st.ps("ps_count", [P, 3, BANK], F32)
        ps_sums = st.ps("ps_sums", [P, 2, BANK], F32)
        tables_in, setup, chain, rows_used, hot_ready = st.sems("tables_in", "setup", "chain", "rows_used", "hot_ready")
        rows_in = st.sems("rows_in_a", "rows_in_b")
        goes_done, count_done, sums_done = st.sems("goes_done", "count_done", "sums_done")
        goes_kept, sums_kept, count_added, target_set = st.sems("goes_kept", "sums_kept", "count_added", "target_set")
        added = [st.sem(f"added{k}") for k in range(ACCS)]
        block = st.block()

        @block.sync
        def _(sp):
            for t, source in ((rel, s.i_rel), (row, s.i_row), (typ, s.i_type)):
                sp.dma_start(t[:, :], source).then_inc(tables_in, 16)
            rows = s.i_srcrow.rearrange("(o i) e -> o (i e)", o=1)

            def load(first, h):
                span = rows[:, bass.ds(first * P, HALF * P)].to_broadcast([P, HALF * P])
                sp.dma_start(src_rows[:, h * HALF:(h + 1) * HALF, :].rearrange("p i e -> p (i e)"),
                             span).then_inc(rows_in[h], 16)

            for h in range(2):
                load(h * HALF, h)
            with sp.Fori(0, ITEM_TURNS - 1) as turn:
                for h in range(2):
                    sp.wait_ge(rows_used, turn * U + (h + 1) * HALF)
                    load((turn + 1) * U + h * HALF, h)

        @block.vector
        def _(dve):
            link = link_on(dve, setup)
            link(nc.vector.tensor_copy(x1[:, :, 0:DIM], x[:, :, :]))
            link(nc.vector.memset(x1[:, :, DIM:W65], 1.0))
            link(nc.vector.tensor_scalar(trash[:, :], c.lane[:, :], float(TRASH), None, ALU.add))
            link(nc.vector.memset(counts[:, :], 0.0))
            dve.wait_ge(tables_in, 48)
            with dve.Fori(0, ITEM_TURNS) as turn:
                _, at = nc.values_load_multi_w_load_instructions(
                    c.block_row[0:1, bass.ds(turn * U, U)], engines=DVE_ONLY, min_val=0, max_val=(BLOCKS - 1) * W65,
                    skip_runtime_bounds_check_because="the item map clamps the block")
                steps = TurnCount(dve, chain, turn, 4)

                def add_counts(u):
                    dve.wait_ge(count_done, turn * U + u + 1)
                    here = counts[:, bass.ds(at[u], TYPES)]
                    dve.wait_ge(count_added, turn * U + u)
                    nc.vector.tensor_tensor(here, here, ps_count[:, u % 3, 0:TYPES], ALU.add).then_inc(count_added, 1)

                for u in range(U):
                    col = bass.ds(turn * U + u, 1)
                    h = u // HALF
                    if u % HALF == 0:
                        dve.wait_ge(rows_in[h], (turn + 1) * 16)
                    nc.vector.tensor_scalar(same[:, u % (2 * RING), :], src_rows[:, u, :], row[:, col], None,
                                            ALU.is_equal).then_inc(rows_used, 1)
                    nc.vector.tensor_scalar(hot_dst[:, u % (2 * RING), :], c.iota_b[:, :], rel[:, col], None, ALU.is_equal)
                    nc.vector.tensor_scalar(hot_type[:, u % (2 * RING), :], c.iota_b[:, 0:TYPES], typ[:, col], None,
                                            ALU.is_equal).then_inc(hot_ready, 1)
                    dve.wait_ge(rows_used, turn * U + u + 1)
                    nc.vector.tensor_tensor_reduce(out=scrap[:, :], in0=same[:, u % (2 * RING), :], in1=c.before[:, :], scale=1.0,
                                                   scalar=0.0, op0=ALU.mult, op1=ALU.add,
                                                   accum_out=earlier[:, u:u + 1])
                    if u >= LAG:
                        add_counts(u - LAG)
                    if u % HALF == HALF - 1:
                        part = slice(h * HALF, (h + 1) * HALF)
                        cols = bass.ds(turn * U + h * HALF, HALF)
                        far = steps.mark(nc.vector.tensor_scalar(shift[:, part], row[:, cols], -1.0, trash[:, 0:1],
                                                                 ALU.mult, ALU.add))
                        steps.wait(far)
                        moved = steps.mark(nc.vector.scalar_tensor_tensor(shift[:, part], earlier[:, part], 1.0,
                                                                          shift[:, part], ALU.min, ALU.mult))
                        steps.wait(moved)
                        dve.wait_ge(sums_kept, turn * U + h * HALF)
                        nc.vector.tensor_tensor(target[:, part], shift[:, part], row[:, cols], ALU.add).then_inc(target_set, 1)
                for u in range(U - LAG, U):
                    add_counts(u)
                steps.close()

        @block.tensor
        def _(pe):
            pe.wait_ge(setup, 4)
            with pe.Fori(0, ITEM_TURNS) as turn:
                _, at = nc.values_load_multi_w_load_instructions(
                    c.block_row[0:1, bass.ds(turn * U, U)], engines=PE_ONLY, min_val=0, max_val=(BLOCKS - 1) * W65,
                    skip_runtime_bounds_check_because="the item map clamps the block")
                x_rows = x1[:, :, :].rearrange("p b d -> p (b d)")

                def pick_sums(u):
                    pe.wait_ge(goes_kept, turn * U + u + 1)
                    pe.wait_ge(sums_kept, turn * U + max(u - 1, 0))
                    nc.tensor.matmul(ps_sums[:, u % 2, 0:W65], goes[:, u % RING, :], x_rows[:, bass.ds(at[u], W65)],
                                     start=True, stop=True).then_inc(sums_done, 1)

                for u in range(U):
                    pe.wait_ge(hot_ready, turn * U + u + 1)
                    nc.tensor.matmul(ps_goes[:, u % 3, 0:P], hot_dst[:, u % (2 * RING), :], same[:, u % (2 * RING), :],
                                     start=True, stop=True).then_inc(goes_done, 1)
                    pe.wait_ge(count_added, turn * U + max(u - 2, 0))
                    nc.tensor.matmul(ps_count[:, u % 3, 0:TYPES], hot_dst[:, u % (2 * RING), :], hot_type[:, u % (2 * RING), :],
                                     start=True, stop=True).then_inc(count_done, 1)
                    if u >= LAG - 1:
                        pick_sums(u - LAG + 1)
                for u in range(U - LAG + 1, U):
                    pick_sums(u)

        @block.scalar
        def _(act):
            with act.Fori(0, ITEM_TURNS) as turn:
                def keep_sums(u):
                    act.wait_ge(sums_done, turn * U + u + 1)
                    act.wait_ge(added[u % ACCS], (turn * 2 + u // ACCS) * 16)
                    nc.scalar.copy(sums[:, u % ACCS, :], ps_sums[:, u % 2, 0:W65]).then_inc(sums_kept, 1)

                for u in range(U):
                    act.wait_ge(goes_done, turn * U + u + 1)
                    nc.scalar.copy(goes[:, u % RING, :], ps_goes[:, u % 3, 0:P]).then_inc(goes_kept, 1)
                    if u >= LAG:
                        keep_sums(u - LAG)
                for u in range(U - LAG, U):
                    keep_sums(u)

        @block.gpsimd
        def _(pool):
            with pool.Fori(0, ITEM_TURNS) as turn:
                for u in range(U):
                    pool.wait_ge(sums_kept, turn * U + u + 1)
                    if u % HALF == 0:
                        pool.wait_ge(target_set, turn * 2 + u // HALF + 1)
                    pool.wait_ge(added[u % ACCS], (turn * 2 + u // ACCS) * 16)
                    hold(pool, c)
                    pool.indirect_dma_start(s.acc[u % ACCS], bass.IndirectOffsetOnAxis(ap=target[:, u:u + 1], axis=0),
                                            sums[:, u % ACCS, :], None, compute_op=ALU.add).then_inc(added[u % ACCS], 16)
            for k in range(ACCS):
                pool.wait_ge(added[k], ITEM_TURNS * 32)


def layer_norm(nc, c, h, x):
    with Stage(nc) as st:
        square = st.sb("square", [P, BLOCKS, DIM], F32)
        stat = st.sb("stat", [P, BLOCKS], F32)
        root = st.sb("root", [P, BLOCKS], F32)
        dve_done, var_set, root_set = st.sems("dve_done", "var_set", "root_set")
        block = st.block()
        shape = [P, BLOCKS, DIM]

        @block.vector
        def _(dve):
            link = link_on(dve, dve_done)
            link(nc.vector.tensor_reduce(stat[:, :], h[:, :, :], AX.X, ALU.add))
            link(nc.vector.tensor_scalar(stat[:, :], stat[:, :], 1.0 / DIM, None, ALU.mult))
            link(nc.vector.tensor_tensor(h[:, :, :], h[:, :, :], stat[:, :, None].to_broadcast(shape), ALU.subtract))
            link(nc.vector.tensor_tensor(square[:, :, :], h[:, :, :], h[:, :, :], ALU.mult))
            nc.vector.tensor_reduce(root[:, :], square[:, :, :], AX.X, ALU.add).then_inc(var_set, 1)
            dve.wait_ge(root_set, 1)
            link(nc.vector.reciprocal(root[:, :], root[:, :]))
            link(nc.vector.tensor_tensor(x[:, :, :], h[:, :, :], root[:, :, None].to_broadcast(shape), ALU.mult))

        @block.scalar
        def _(act):
            act.wait_ge(var_set, 1)
            nc.scalar.activation(root[:, :], root[:, :], ACT.Sqrt, bias=c.eps[:, 0:1], scale=1.0 / DIM).then_inc(root_set, 1)


def sum_accumulators(nc, s, total):
    with Stage(nc) as st:
        part = st.sb("part", [P, 2, BLOCKS * W65], F32)
        part_in = st.sems("part_in_a", "part_in_b")
        first_in, summed = st.sems("first_in", "summed")
        block = st.block()
        flat = total[:, :, :].rearrange("p b d -> p (b d)")

        @block.sync
        def _(sp):
            for k, acc in enumerate(s.acc):
                rows = acc[0:PADDED, :].rearrange("(p b) d -> p (b d)", p=P)
                if k == 0:
                    sp.dma_start(flat, rows).then_inc(first_in, 16)
                    continue
                if k >= 3:
                    sp.wait_ge(summed, k - 2)
                sp.dma_start(part[:, k % 2, :], rows).then_inc(part_in[k % 2], 16)

        @block.vector
        def _(dve):
            dve.wait_ge(first_in, 16)
            for k in range(1, ACCS):
                dve.wait_ge(part_in[k % 2], 16 * ((k + 1) // 2))
                if k >= 2:
                    dve.wait_ge(summed, k - 1)
                nc.vector.tensor_tensor(flat, flat, part[:, k % 2, :], ALU.add).then_inc(summed, 1)


def mean_layer(nc, s, c, x, weight, bias):
    with Stage(nc) as st:
        counts = st.sb("counts", [P, BLOCKS * W65], F32)
        clear_accumulators(nc, s)
        mean_loop(nc, s, c, x, counts)
        finish_counts(nc, s, counts)
    with Stage(nc) as st:
        total = st.sb("total", [P, BLOCKS, W65], F32)
        h = st.sb("h", [P, BLOCKS, DIM], F32)
        sum_accumulators(nc, s, total)
        mean_update(nc, s, c, x, total, h, weight, bias)
        layer_norm(nc, c, h, x)


def finish_counts(nc, s, counts):
    with Stage(nc) as st:
        degree = st.sb("degree", [P, BLOCKS], F32)
        dve_done, ready, out = st.sems("dve_done", "ready", "out")
        block = st.block()

        @block.vector
        def _(dve):
            link = link_on(dve, dve_done)
            link(nc.vector.tensor_reduce(degree[:, :], counts[:, :].rearrange("p (b r) -> p b r", r=W65), AX.X, ALU.add))
            link(nc.vector.tensor_scalar(counts[:, :], counts[:, :], 1.0, None, ALU.max))
            nc.vector.reciprocal(counts[:, :], counts[:, :]).then_inc(ready, 1)

        @block.sync
        def _(sp):
            sp.wait_ge(ready, 1)
            sp.dma_start(s.counts, counts[:, :]).then_inc(out, 16)
            sp.dma_start(s.degree, degree[:, :]).then_inc(out, 16)
            sp.wait_ge(out, 32)


def mean_update(nc, s, c, x, total, h, weight, bias):
    with Stage(nc) as st:
        w = st.sb("w", [2 * DIM, DIM], F32)
        b = st.sb("b", [P, DIM], F32)
        recip = st.sb("recip", [P, BLOCKS], F32)
        both = st.sb("both", [P, G, 2 * DIM], F32)
        both_t = st.sb("both_t", [P, G * P], F32)
        ps_t = st.ps("ps_t", [P, G * P], F32)
        ps_out = st.ps("ps_out", [P, G, DIM], F32)
        w_in, setup, both_set, turned, kept, out_done, chain = st.sems(
            "w_in", "setup", "both_set", "turned", "kept", "out_done", "chain")
        block = st.block()

        @block.sync
        def _(sp):
            sp.dma_start(w[:, :], weight).then_inc(w_in, 16)
            sp.dma_start(b[:, :], bias.to_broadcast([P, DIM])).then_inc(w_in, 16)

        @block.vector
        def _(dve):
            link = link_on(dve, setup)
            link(nc.vector.tensor_scalar(recip[:, :], total[:, :, DIM], 1.0, None, ALU.max))
            link(nc.vector.reciprocal(recip[:, :], recip[:, :]))
            dve.wait_ge(w_in, 32)
            with dve.Fori(0, BLOCK_TURNS) as turn:
                blocks = bass.ds(turn * G, G)
                nc.vector.tensor_copy(both[:, :, 0:DIM], x[:, blocks, :])
                nc.vector.tensor_tensor(both[:, :, DIM:2 * DIM], total[:, blocks, 0:DIM],
                                        recip[:, blocks][:, :, None].to_broadcast([P, G, DIM]), ALU.mult).then_inc(both_set, 1)
                dve.wait_ge(out_done, turn + 1)
                nc.vector.tensor_tensor(h[:, blocks, :], ps_out[:, :, :], x[:, blocks, :], ALU.add).then_inc(chain, 1)
            dve.wait_ge(chain, BLOCK_TURNS)
            link(nc.vector.tensor_tensor(h[:, :, :], h[:, :, :], b[:, None, :].to_broadcast([P, BLOCKS, DIM]), ALU.add))

        @block.tensor
        def _(pe):
            pe.wait_ge(w_in, 32)
            with pe.Fori(0, BLOCK_TURNS) as turn:
                pe.wait_ge(both_set, turn + 1)
                for g in range(G):
                    last = nc.tensor.transpose(ps_t[:, g * P:(g + 1) * P], both[:, g, :], c.ident[:, :])
                last.then_inc(turned, 1)
                pe.wait_ge(kept, turn + 1)
                pe.wait_ge(chain, turn)
                for g in range(G):
                    last = nc.tensor.matmul(ps_out[:, g, :], both_t[:, g * P:(g + 1) * P], w[:, :], start=True, stop=True)
                last.then_inc(out_done, 1)

        @block.scalar
        def _(act):
            with act.Fori(0, BLOCK_TURNS) as turn:
                act.wait_ge(turned, turn + 1)
                nc.scalar.copy(both_t[:, :], ps_t[:, :]).then_inc(kept, 1)


def max_layer(nc, s, c, x):
    with Stage(nc) as st:
        scale = st.sb("scale", [P, BLOCKS], F32)
        end_row = st.sb("end_row", [P, BLOCKS], I32)
        max_prepare(nc, s, c, x, scale, end_row)
        max_loop(nc, s, c)
        with Stage(nc) as inner:
            h = inner.sb("h", [P, BLOCKS, DIM], F32)
            max_update(nc, s, c, x, scale, end_row, h)
            layer_norm(nc, c, h, x)


def max_prepare(nc, s, c, x, scale, end_row):
    with Stage(nc) as st:
        degree = st.sb("degree", [P, BLOCKS], F32)
        w = st.sb("w", [P, BLOCKS], F32)
        g = st.sb("g", [P, BLOCKS, DIM], F32)
        total = st.sb("total", [P, BLOCKS], F32)
        upto = st.sb("upto", [P, BLOCKS], F32)
        end = st.sb("end", [P, BLOCKS], I32)
        spare = st.sb("spare", [P, BLOCKS], I32)
        ps_in = st.ps("ps_in", [P, BLOCKS], F32)
        ps_total = st.ps("ps_total", [P, BLOCKS], F32)
        degree_in, dve_done, clamped, rooted, summed, g_set, g_out = st.sems(
            "degree_in", "dve_done", "clamped", "rooted", "summed", "g_set", "g_out")
        block = st.block()

        @block.sync
        def _(sp):
            sp.dma_start(degree[:, :], s.degree).then_inc(degree_in, 16)
            sp.wait_ge(g_set, 1)
            sp.dma_start(node_view(s.g, DIM), g[:, :, :]).then_inc(g_out, 16)
            sp.wait_ge(g_out, 16)

        @block.tensor
        def _(pe):
            pe.wait_ge(degree_in, 16)
            nc.tensor.matmul(ps_in[:, :], c.upto[:, :], degree[:, :], start=True, stop=True)
            nc.tensor.matmul(ps_total[:, :], c.ones[:, :], degree[:, :], start=True, stop=True).then_inc(summed, 1)

        @block.scalar
        def _(act):
            act.wait_ge(clamped, 1)
            nc.scalar.activation(w[:, :], w[:, :], ACT.Sqrt).then_inc(rooted, 1)

        @block.vector
        def _(dve):
            link = link_on(dve, dve_done)
            dve.wait_ge(degree_in, 16)
            nc.vector.tensor_scalar(w[:, :], degree[:, :], 1.0, None, ALU.max).then_inc(clamped, 1)
            dve.wait_ge(summed, 1)
            link(nc.vector.tensor_copy(total[:, :], ps_total[:, :]))
            link(nc.vector.tensor_tensor_scan(upto[:, :], c.ones[:, 0:BLOCKS], total[:, :], 0.0, ALU.mult, ALU.add))
            link(nc.vector.tensor_tensor(upto[:, :], upto[:, :], total[:, :], ALU.subtract))
            link(nc.vector.tensor_tensor(upto[:, :], upto[:, :], ps_in[:, :], ALU.add))
            link(nc.vector.tensor_scalar(upto[:, :], upto[:, :], -1.0, 0.0, ALU.add, ALU.max))
            link(nc.vector.tensor_copy(end[:, :], upto[:, :]))
            link(nc.vector.tensor_scalar(spare[:, :], end[:, :], P - 1, None, ALU.bitwise_and))
            link(nc.vector.tensor_copy(upto[:, :], spare[:, :]))
            link(nc.vector.tensor_scalar(spare[:, :], end[:, :], 7, None, ALU.logical_shift_right))
            link(nc.vector.tensor_copy(total[:, :], spare[:, :]))
            link(nc.vector.scalar_tensor_tensor(end_row[:, :], upto[:, :], float(TILES_RUN), total[:, :],
                                                ALU.mult, ALU.add))
            dve.wait_ge(rooted, 1)
            link(nc.vector.reciprocal(w[:, :], w[:, :]))
            nc.vector.tensor_tensor(g[:, :, :], x[:, :, :], w[:, :, None].to_broadcast([P, BLOCKS, DIM]),
                                    ALU.mult).then_inc(g_set, 1)
            link(nc.vector.scalar_tensor_tensor(scale[:, :], degree[:, :], 1.0, w[:, :], ALU.min, ALU.mult))


def max_loop(nc, s, c):
    with Stage(nc) as st:
        table = st.sb("table", [P, TILES_PAD], F32)
        index = st.sb("index", [P, TU], I32)
        rows = st.sb("rows", [P, TU, DIM], F32)
        cut = st.sb("cut", [DIM, 2, THALF * P], F32)
        running = st.sb("running", [DIM, 2, THALF * P], F32)
        back = st.sb("back", [P, 2, THALF * DIM], F32)
        ps_turned = st.ps("ps_turned", [DIM, 2, THALF * P], F32)
        ps_back = st.ps("ps_back", [P, 2, 512], F32)
        table_in, start_set, index_set, turned, scan_done, back_done, back_kept = st.sems(
            "table_in", "start_set", "index_set", "turned", "scan_done", "back_done", "back_kept")
        got = [st.sem(f"got{u}") for u in range(TU)]
        cut_in = st.sems("cut_in_a", "cut_in_b")
        stored = st.sems("stored_a", "stored_b")
        block = st.block()

        @block.sync
        def _(sp):
            sp.dma_start(table[:, :], s.t_row).then_inc(table_in, 16)
            cuts = s.t_cut.rearrange("(o k) -> o k", o=1)
            out = s.scanned.rearrange("(p t) d -> p (t d)", p=P)

            def load(first_tile, h):
                sp.dma_start(cut[:, h, :], cuts[:, bass.ds(first_tile * P, THALF * P)].to_broadcast([DIM, THALF * P])
                             ).then_inc(cut_in[h], 16)

            def keep(turn, h):
                sp.wait_ge(back_kept, turn * 2 + h + 1)
                sp.dma_start(out[:, bass.ds((turn * TU + h * THALF) * DIM, THALF * DIM)], back[:, h, :]
                             ).then_inc(stored[h], 16)

            for h in range(2):
                load(h * THALF, h)
            with sp.Fori(0, TILE_TURNS - 1) as turn:
                for h in range(2):
                    sp.wait_ge(scan_done, turn * 2 + h + 1)
                    load((turn + 1) * TU + h * THALF, h)
                for h in range(2):
                    keep(turn, h)
            for h in range(2):
                keep(TILE_TURNS - 1, h)
                sp.wait_ge(stored[h], 16 * TILE_TURNS)

        @block.gpsimd
        def _(pool):
            with pool.Fori(0, TILE_TURNS) as turn:
                for u in range(TU):
                    if u % THALF == 0:
                        pool.wait_ge(index_set, turn * 2 + u // THALF + 1)
                        hold(pool, c)
                    pool.indirect_dma_start(rows[:, u, :], None, s.g,
                                            bass.IndirectOffsetOnAxis(ap=index[:, u:u + 1], axis=0)).then_inc(got[u], 16)

        @block.tensor
        def _(pe):
            with pe.Fori(0, TILE_TURNS) as turn:
                for h in range(2):
                    for k in range(THALF):
                        u = h * THALF + k
                        pe.wait_ge(got[u], (turn + 1) * 16)
                        hold(pe, c)
                        last = nc.tensor.transpose(ps_turned[:, h, k * P:(k + 1) * P], rows[:, u, :], c.ident[:, :])
                    last.then_inc(turned, 1)
                pe.wait_ge(back_kept, turn * 2)
                for h in range(2):
                    pe.wait_ge(scan_done, turn * 2 + h + 1)
                    hold(pe, c)
                    for k in range(THALF):
                        last = nc.tensor.transpose(ps_back[:, h, k * DIM:(k + 1) * DIM], running[:, h, k * P:(k + 1) * P],
                                                   c.ident[0:DIM, 0:DIM])
                    last.then_inc(back_done, 1)

        @block.vector
        def _(dve):
            nc.vector.memset(running[:, 1, THALF * P - 1:THALF * P], -BIG).then_inc(start_set, 1)
            dve.wait_ge(table_in, 16)
            for h in range(2):
                nc.vector.tensor_copy(index[:, h * THALF:(h + 1) * THALF], table[:, h * THALF:(h + 1) * THALF]).then_inc(index_set, 1)
            dve.wait_ge(start_set, 1)
            with dve.Fori(0, TILE_TURNS) as turn:
                dve.wait_ge(back_done, turn * 2)
                for h in range(2):
                    dve.wait_ge(cut_in[h], (turn + 1) * 16)
                    dve.wait_ge(turned, turn * 2 + h + 1)
                    dve.wait_ge(scan_done, turn * 2 + h)
                    nc.vector.tensor_tensor_scan(running[:, h, :], cut[:, h, :], ps_turned[:, h, :],
                                                 running[:, 1 - h, THALF * P - 1:THALF * P], ALU.add, ALU.max
                                                 ).then_inc(scan_done, 1)
                    nc.vector.tensor_copy(index[:, h * THALF:(h + 1) * THALF],
                                          table[:, bass.ds((turn + 1) * TU + h * THALF, THALF)]).then_inc(index_set, 1)

        @block.scalar
        def _(act):
            with act.Fori(0, TILE_TURNS) as turn:
                for h in range(2):
                    act.wait_ge(back_done, turn * 2 + h + 1)
                    act.wait_ge(stored[h], turn * 16)
                    nc.scalar.copy(back[:, h, :], ps_back[:, h, 0:THALF * DIM]).then_inc(back_kept, 1)


def max_update(nc, s, c, x, scale, end_row, h):
    with Stage(nc) as st:
        index = st.sb("index", [P, G], I32)
        rows = st.sb("rows", [P, G, DIM], F32)
        index_set, scaled, h_set = st.sems("index_set", "scaled", "h_set")
        got = [st.sem(f"got{g}") for g in range(G)]
        block = st.block()

        @block.gpsimd
        def _(pool):
            with pool.Fori(0, BLOCK_TURNS) as turn:
                pool.wait_ge(index_set, turn + 1)
                hold(pool, c)
                for g in range(G):
                    pool.indirect_dma_start(rows[:, g, :], None, s.scanned,
                                            bass.IndirectOffsetOnAxis(ap=index[:, g:g + 1], axis=0)).then_inc(got[g], 16)

        @block.vector
        def _(dve):
            with dve.Fori(0, BLOCK_TURNS) as turn:
                blocks = bass.ds(turn * G, G)
                nc.vector.tensor_copy(index[:, :], end_row[:, blocks]).then_inc(index_set, 1)
                for g in range(G):
                    dve.wait_ge(got[g], (turn + 1) * 16)
                nc.vector.tensor_tensor(rows[:, :, :], rows[:, :, :], scale[:, blocks][:, :, None].to_broadcast([P, G, DIM]),
                                        ALU.mult).then_inc(scaled, 1)
                dve.wait_ge(scaled, turn + 1)
                nc.vector.tensor_tensor(h[:, blocks, :], rows[:, :, :], x[:, blocks, :], ALU.add).then_inc(h_set, 1)


def relational_layer(nc, s, c, x, weights, root, bias, res_weight, res_bias):
    for layer in range(2):
        with Stage(nc) as st:
            acc = st.sb("acc", [P, BLOCKS, W65], F32)
            with Stage(nc) as inner:
                h = x
                if layer:
                    h = inner.sb("h", [P, BLOCKS, DIM], F32)
                    store(nc, h[:, :, :], node_view(s.h, DIM))
                relational_table(nc, s, c, h, acc, weights[layer], root[layer], bias[layer:layer + 1, :],
                                 res_weight[layer], res_bias[layer:layer + 1, :])
            relational_loop(nc, s, c, acc, first=(layer == 0))
            with Stage(nc) as inner:
                h = inner.sb("h", [P, BLOCKS, DIM], F32)
                relational_update(nc, s, acc, h, x if layer else None)
                if layer:
                    layer_norm(nc, c, h, x)
                else:
                    store(nc, node_view(s.h, DIM), h[:, :, :])


def relational_table(nc, s, c, h, acc, weights, root, bias, res_weight, res_bias):
    tail = SPAN + 2 * DIM
    pieces = -(-tail // BANK)
    banks = 6
    slots = 3
    total = G * pieces
    dve_share = (total + 1) // 2
    act_share = total // 2
    low, high = slice(0, DIM), slice(DIM, P)
    with Stage(nc) as st:
        w_12 = st.sb("w_12", [P, tail], BF16)
        w_31 = st.sb("w_31", [P, tail], BF16)
        h_11 = st.sb("h_11", [P, G * P], BF16)
        h_22 = st.sb("h_22", [P, G * P], BF16)
        h_13 = st.sb("h_13", [P, G * P], BF16)
        h_rest = st.sb("h_rest", [P, G * P], F32)
        stage = st.sb("stage", [P, G, 2, DIM], F32)
        biases = st.sb("biases", [P, 2, DIM], F32)
        res = st.sb("res", [P, BLOCKS, DIM], F32)
        out = st.sb("out", [P, slots, SPAN], F32)
        w = out[:, :, :].rearrange("p s k -> p (s k)")[:, 0:tail]
        ps_t = st.ps("ps_t", [P, G * P], F32)
        ps = st.ps("ps", [P, banks, BANK], F32)
        w_in, w_split, chain, staged, turned, first_kept, h_split, made, by_dve, by_act, res_set, res_out = st.sems(
            "w_in", "w_split", "chain", "staged", "turned", "first_kept", "h_split", "made", "by_dve", "by_act",
            "res_set", "res_out")
        sent = [st.sem(f"sent{k}") for k in range(slots)]
        block = st.block()
        uses = [len(range(k, G, slots)) for k in range(slots)]

        @block.sync
        def _(sp):
            for half in (low, high):
                sp.dma_start(w[half, 0:SPAN].rearrange("d (r k) -> d r k", r=TYPES), weights.rearrange("r d k -> d r k")
                             ).then_inc(w_in, 16)
                sp.dma_start(w[half, SPAN:SPAN + DIM], root).then_inc(w_in, 16)
                sp.dma_start(w[half, SPAN + DIM:tail], res_weight).then_inc(w_in, 16)
            sp.dma_start(biases[:, 0, :], bias.to_broadcast([P, DIM])).then_inc(w_in, 16)
            sp.dma_start(biases[:, 1, :], res_bias.to_broadcast([P, DIM])).then_inc(w_in, 16)
            rows = s.rel_table.rearrange("(p b r) d -> p b (r d)", p=P, r=TYPES)
            with sp.Fori(0, BLOCK_TURNS) as turn:
                for g in range(G):
                    upto = (g + 1) * pieces
                    sp.wait_ge(by_dve, turn * dve_share + (upto + 1) // 2)
                    hold(sp, c)
                    sp.wait_ge(by_act, turn * act_share + upto // 2)
                    hold(sp, c)
                    sp.dma_start(rows[:, bass.ds(turn * G + g, 1), :], out[:, g % slots:g % slots + 1, :]
                                 ).then_inc(sent[g % slots], 16)
            sp.wait_ge(res_set, 1)
            sp.dma_start(node_view(s.res, DIM), res[:, :, :]).then_inc(res_out, 16)
            sp.wait_ge(res_out, 16)
            for k in range(slots):
                sp.wait_ge(sent[k], 16 * BLOCK_TURNS * uses[k])

        @block.tensor
        def _(pe):
            pe.wait_ge(w_split, 6)
            with pe.Fori(0, BLOCK_TURNS) as turn:
                pe.wait_ge(staged, turn + 1)
                hold(pe, c)
                for g in range(G):
                    last = nc.tensor.transpose(ps_t[:, g * P:(g + 1) * P], stage[:, g, :, :].rearrange("p a d -> p (a d)"),
                                               c.ident[:, :])
                last.then_inc(turned, 1)
                pe.wait_ge(h_split, turn + 1)
                for q in range(total):
                    g, piece = divmod(q, pieces)
                    sem, share = ((by_dve, dve_share), (by_act, act_share))[q % 2]
                    if q < 2:
                        pe.wait_ge(sem, turn * share)
                    elif q >= banks:
                        pe.wait_ge(sem, turn * share + (q - banks) // 2 + 1)
                    a, b = piece * BANK, min(tail, (piece + 1) * BANK)
                    block_cols = slice(g * P, (g + 1) * P)
                    sums = ps[:, q % banks, 0:b - a]
                    nc.tensor.matmul(sums, h_13[:, block_cols], w_31[:, a:b], start=True, stop=False)
                    nc.tensor.matmul(sums, h_22[:, block_cols], w_12[:, a:b], start=False, stop=False)
                    nc.tensor.matmul(sums, h_11[:, block_cols], w_12[:, a:b], start=False, stop=True).then_inc(made, 1)

        def copy_pieces(engine, turn, parity, copy, sem):
            for q in range(parity, total, 2):
                g, piece = divmod(q, pieces)
                slot = g % slots
                if q - 2 < g * pieces:
                    engine.wait_ge(sent[slot], (turn * uses[slot] + g // slots) * 16)
                engine.wait_ge(made, turn * total + q + 1)
                a, b = piece * BANK, min(SPAN, (piece + 1) * BANK)
                last = copy(out[:, slot, a:b], ps[:, q % banks, 0:b - a])
                if piece == pieces - 1:
                    here = bass.ds(turn * G + g, 1)
                    copy(acc[:, here, 0:DIM], ps[:, q % banks, b - a:b - a + DIM][:, None, :])
                    last = copy(res[:, here, :], ps[:, q % banks, b - a + DIM:b - a + 2 * DIM][:, None, :])
                last.then_inc(sem, 1)

        @block.vector
        def _(dve):
            link = link_on(dve, w_split)
            dve.wait_ge(w_in, 16 * 8)
            link(nc.vector.tensor_copy(w_12[:, :], w[:, :]))
            nc.vector.tensor_copy(w_31[high, :], w_12[high, :])
            link(nc.vector.tensor_tensor(w[:, :], w[:, :], w_12[:, :], ALU.subtract))
            link(nc.vector.tensor_copy(w_12[high, :], w[high, :]))
            link(nc.vector.tensor_copy(w_31[low, :], w[low, :]))
            link(nc.vector.tensor_tensor(w[low, :], w[low, :], w_31[low, :], ALU.subtract))
            link(nc.vector.tensor_copy(w_31[low, :], w[low, :]))
            with dve.Fori(0, BLOCK_TURNS) as turn:
                steps = TurnCount(dve, chain, turn, 4)
                dve.wait_ge(turned, turn)
                blocks = h[:, bass.ds(turn * G, G), :]
                nc.vector.tensor_copy(stage[:, :, 0, :], blocks)
                nc.vector.tensor_copy(stage[:, :, 1, :], blocks).then_inc(staged, 1)
                dve.wait_ge(made, turn * total)
                dve.wait_ge(first_kept, turn + 1)
                steps.wait(steps.mark(nc.vector.tensor_tensor(h_rest[:, :], ps_t[:, :], h_11[:, :], ALU.subtract)))
                steps.wait(steps.mark(nc.vector.tensor_copy(h_22[:, :], h_rest[:, :])))
                steps.wait(steps.mark(nc.vector.tensor_tensor(h_rest[high, :], h_rest[high, :], h_22[high, :],
                                                              ALU.subtract)))
                steps.mark(nc.vector.tensor_copy(h_13[low, :], h_11[low, :]))
                nc.vector.tensor_copy(h_13[high, :], h_rest[high, :]).then_inc(h_split, 1)
                steps.close()
                copy_pieces(dve, turn, 0, nc.vector.tensor_copy, by_dve)
            dve.wait_ge(by_dve, BLOCK_TURNS * dve_share)
            dve.wait_ge(by_act, BLOCK_TURNS * act_share)
            shape = [P, BLOCKS, DIM]
            nc.vector.tensor_tensor(acc[:, :, 0:DIM], acc[:, :, 0:DIM], biases[:, 0:1, :].to_broadcast(shape), ALU.add)
            link(nc.vector.tensor_tensor(res[:, :, :], res[:, :, :], biases[:, 1:2, :].to_broadcast(shape), ALU.add))
            nc.vector.tensor_relu(res[:, :, :], res[:, :, :]).then_inc(res_set, 1)

        @block.scalar
        def _(act):
            with act.Fori(0, BLOCK_TURNS) as turn:
                act.wait_ge(turned, turn + 1)
                act.wait_ge(made, turn * total)
                nc.scalar.copy(h_11[:, :], ps_t[:, :]).then_inc(first_kept, 1)
                copy_pieces(act, turn, 1, nc.scalar.copy, by_act)


def relational_loop(nc, s, c, acc, first):
    sums = 2 if first else RING
    with Stage(nc) as st:
        rel = st.sb("rel", [P, ITEMS_PAD], F32)
        table = st.sb("table", [P, ITEMS_PAD], F32)
        weight = st.sb("weight", [P, ITEMS_PAD], F32)
        index = st.sb("index", [P, U], I32)
        rows = st.sb("rows", [P, U, DIM], F32)
        share = st.sb("share", [P, RING, P], F32)
        ps_sum = st.ps("ps_sum", [P, sums, BANK], F32)
        tables_in, setup, index_set, share_set, sum_done, sum_added = st.sems(
            "tables_in", "setup", "index_set", "share_set", "sum_done", "sum_added")
        got = [st.sem(f"got{u}") for u in range(U)]
        if first:
            typ = st.sb("typ", [P, ITEMS_PAD], F32)
            counts = st.sb("counts", [P, BLOCKS * W65], F32)
            hot_dst = st.sb("hot_dst", [P, 2 * RING, P], BF16)
            hot_type = st.sb("hot_type", [P, 2 * RING, TYPES], BF16)
            hot_t = st.sb("hot_t", [P, RING, P], F32)
            scrap = st.sb("scrap", [P, TYPES], F32)
            picked = st.sb("picked", [P, U], F32)
            ps_hot = st.ps("ps_hot", [P, 3, 2 * BANK], BF16)
            ps_weight = st.ps("ps_weight", [P, 3, BANK], F32)
            hot_set, hot_turned, hot_kept, weight_done, weight_kept, weight_out = st.sems(
                "hot_set", "hot_turned", "hot_kept", "weight_done", "weight_kept", "weight_out")
        block = st.block()
        loads = [(rel, s.i_rel), (table, s.i_rel_row)] + ([(typ, s.i_type), (counts, s.counts)] if first
                                                          else [(weight, s.i_weight)])

        @block.sync
        def _(sp):
            for t, source in loads:
                sp.dma_start(t[:, :], source).then_inc(tables_in, 16)
            if first:
                sp.wait_ge(weight_kept, ITEM_TURNS + 1)
                sp.dma_start(s.i_weight, weight[:, :]).then_inc(weight_out, 16)
                sp.wait_ge(weight_out, 16)

        @block.gpsimd
        def _(pool):
            with pool.Fori(0, ITEM_TURNS) as turn:
                for u in range(U):
                    if u % HALF == 0:
                        pool.wait_ge(index_set, turn * 2 + u // HALF + 1)
                        hold(pool, c)
                    pool.indirect_dma_start(rows[:, u, :], None, s.rel_table,
                                            bass.IndirectOffsetOnAxis(ap=index[:, u:u + 1], axis=0)).then_inc(got[u], 16)

        @block.vector
        def _(dve):
            if first:
                nc.vector.memset(weight[:, ITEMS:ITEMS_PAD], 0.0).then_inc(weight_kept, 1)
            dve.wait_ge(tables_in, 16 * len(loads))
            for h in range(2):
                part = slice(h * HALF, (h + 1) * HALF)
                nc.vector.tensor_copy(index[:, part], table[:, part]).then_inc(index_set, 1)
            with dve.Fori(0, ITEM_TURNS) as turn:
                _, at = nc.values_load_multi_w_load_instructions(
                    c.block_row[0:1, bass.ds(turn * U, U)], engines=DVE_ONLY, min_val=0, max_val=(BLOCKS - 1) * W65,
                    skip_runtime_bounds_check_because="the item map clamps the block")
                acc_rows = acc[:, :, :].rearrange("p b d -> p (b d)")

                def build(u):
                    col = bass.ds(turn * U + u, 1)
                    nc.vector.tensor_scalar(hot_dst[:, u % (2 * RING), :], c.iota_b[:, :], rel[:, col], None, ALU.is_equal)
                    nc.vector.tensor_scalar(hot_type[:, u % (2 * RING), :], c.iota_b[:, 0:TYPES], typ[:, col], None,
                                            ALU.is_equal).then_inc(hot_set, 1)

                def pick_weight(u):
                    dve.wait_ge(weight_done, turn * U + u + 1)
                    nc.vector.tensor_tensor_reduce(out=scrap[:, :], in0=ps_weight[:, u % 3, 0:TYPES],
                                                   in1=hot_type[:, u % (2 * RING), :], scale=1.0, scalar=0.0, op0=ALU.mult,
                                                   op1=ALU.add, accum_out=picked[:, u:u + 1]).then_inc(setup, 1)
                    dve.wait_ge(setup, turn * U + u + 1)
                    make_share(u, picked[:, u:u + 1])

                def make_share(u, by):
                    nc.vector.tensor_scalar(share[:, u % RING, :], c.iota_b[:, :], rel[:, bass.ds(turn * U + u, 1)], by,
                                            ALU.is_equal, ALU.mult).then_inc(share_set, 1)

                def add_sum(u):
                    dve.wait_ge(sum_done, turn * U + u + 1)
                    dve.wait_ge(sum_added, turn * U + u)
                    here = acc_rows[:, bass.ds(at[u], DIM)]
                    nc.vector.tensor_tensor(here, here, ps_sum[:, u % sums, 0:DIM], ALU.add).then_inc(sum_added, 1)
                    if u % HALF == HALF - 1:
                        h = u // HALF
                        nc.vector.tensor_copy(index[:, h * HALF:(h + 1) * HALF],
                                              table[:, bass.ds((turn + 1) * U + h * HALF, HALF)]).then_inc(index_set, 1)

                lag = 5 if first else 3
                for u in range(U + lag):
                    if first:
                        if u < U:
                            build(u)
                        if 3 <= u < U + 3:
                            pick_weight(u - 3)
                    elif u < U:
                        make_share(u, weight[:, bass.ds(turn * U + u, 1)])
                    if u >= lag:
                        add_sum(u - lag)
                if first:
                    nc.vector.tensor_copy(weight[:, bass.ds(turn * U, U)], picked[:, :]).then_inc(weight_kept, 1)

        @block.tensor
        def _(pe):
            if first:
                pe.wait_ge(tables_in, 16 * len(loads))
            with pe.Fori(0, ITEM_TURNS) as turn:
                if first:
                    _, at = nc.values_load_multi_w_load_instructions(
                        c.block_row[0:1, bass.ds(turn * U, U)], engines=PE_ONLY, min_val=0, max_val=(BLOCKS - 1) * W65,
                        skip_runtime_bounds_check_because="the item map clamps the block")

                def turn_hot(u):
                    pe.wait_ge(hot_set, turn * U + u + 1)
                    nc.tensor.transpose(ps_hot[:, u % 3, 0:P], hot_dst[:, u % (2 * RING), :], c.ident_b[:, :]).then_inc(hot_turned, 1)

                def find_weights(u):
                    pe.wait_ge(hot_kept, turn * U + u + 1)
                    nc.tensor.matmul(ps_weight[:, u % 3, 0:TYPES], hot_t[:, u % RING, :], counts[:, bass.ds(at[u], TYPES)],
                                     start=True, stop=True).then_inc(weight_done, 1)

                def sum_rows(u):
                    pe.wait_ge(share_set, turn * U + u + 1)
                    pe.wait_ge(got[u], (turn + 1) * 16)
                    pe.wait_ge(sum_added, turn * U + max(u - sums + 1, 0))
                    nc.tensor.matmul(ps_sum[:, u % sums, 0:DIM], share[:, u % RING, :], rows[:, u, :],
                                     start=True, stop=True).then_inc(sum_done, 1)

                if first:
                    for u in range(U + 4):
                        if u < U:
                            turn_hot(u)
                        if 2 <= u < U + 2:
                            find_weights(u - 2)
                        if u >= 4:
                            sum_rows(u - 4)
                else:
                    for u in range(U):
                        sum_rows(u)

        if first:
            @block.scalar
            def _(act):
                with act.Fori(0, ITEM_TURNS) as turn:
                    for u in range(U):
                        act.wait_ge(hot_turned, turn * U + u + 1)
                        nc.scalar.copy(hot_t[:, u % RING, :], ps_hot[:, u % 3, 0:P]).then_inc(hot_kept, 1)


def relational_update(nc, s, acc, h, x):
    with Stage(nc) as st:
        res = st.sb("res", [P, BLOCKS, DIM], F32)
        res_in, dve_done = st.sems("res_in", "dve_done")
        block = st.block()

        @block.sync
        def _(sp):
            sp.dma_start(res[:, :, :], node_view(s.res, DIM)).then_inc(res_in, 16)

        @block.vector
        def _(dve):
            link = link_on(dve, dve_done)
            dve.wait_ge(res_in, 16)
            link(nc.vector.scalar_tensor_tensor(h[:, :, :], acc[:, :, 0:DIM], 0.0, res[:, :, :], ALU.max, ALU.add))
            if x is not None:
                link(nc.vector.tensor_tensor(h[:, :, :], h[:, :, :], x[:, :, :], ALU.add))


def attention_layer(nc, s, c, x, beta):
    with Stage(nc) as st:
        acc = st.sb("acc", [P, BLOCKS, W65], F32)
        with Stage(nc) as inner:
            parts = inner.sb("parts", [P, 3, BLOCKS * DIM], BF16)
            attention_prepare(nc, s, c, x, parts)
            attention_loop(nc, s, c, parts, beta, acc)
        with Stage(nc) as inner:
            h = inner.sb("h", [P, BLOCKS, DIM], F32)
            attention_update(nc, x, acc, h)
            layer_norm(nc, c, h, x)


def attention_prepare(nc, s, c, x, parts):
    with Stage(nc) as st:
        both = st.sb("both", [P, BLOCKS, 2 * DIM], F32)
        rest = st.sb("rest", [P, BLOCKS, DIM], F32)
        length = st.sb("length", [P, BLOCKS], F32)
        dve_done, squared, rooted, both_set, out = st.sems("dve_done", "squared", "rooted", "both_set", "out")
        block = st.block()
        shape = [P, BLOCKS, DIM]

        @block.vector
        def _(dve):
            link = link_on(dve, dve_done)
            unit = both[:, :, 0:DIM]
            link(nc.vector.tensor_tensor(unit, x[:, :, :], x[:, :, :], ALU.mult))
            nc.vector.tensor_reduce(length[:, :], unit, AX.X, ALU.add).then_inc(squared, 1)
            nc.vector.tensor_copy(both[:, :, DIM:2 * DIM], x[:, :, :])
            dve.wait_ge(rooted, 1)
            link(nc.vector.tensor_scalar(length[:, :], length[:, :], TINY, None, ALU.max))
            link(nc.vector.reciprocal(length[:, :], length[:, :]))
            nc.vector.tensor_tensor(unit, x[:, :, :], length[:, :, None].to_broadcast(shape), ALU.mult).then_inc(both_set, 1)
            dve.wait_ge(both_set, 1)
            part = [parts[:, k, :].rearrange("p (b d) -> p b d", d=DIM) for k in range(3)]
            link(nc.vector.tensor_copy(part[0], unit))
            link(nc.vector.tensor_tensor(rest[:, :, :], unit, part[0], ALU.subtract))
            link(nc.vector.tensor_copy(part[1], rest[:, :, :]))
            link(nc.vector.tensor_tensor(rest[:, :, :], rest[:, :, :], part[1], ALU.subtract))
            link(nc.vector.tensor_copy(part[2], rest[:, :, :]))

        @block.scalar
        def _(act):
            act.wait_ge(squared, 1)
            nc.scalar.activation(length[:, :], length[:, :], ACT.Sqrt).then_inc(rooted, 1)

        @block.sync
        def _(sp):
            sp.wait_ge(both_set, 1)
            sp.dma_start(node_view(s.nx, 2 * DIM), both[:, :, :]).then_inc(out, 16)
            sp.wait_ge(out, 16)


def attention_loop(nc, s, c, parts, beta, acc):
    SPANS = -(-(TILES + BLOCKS - 1) // HALF)
    TURNS = -(-SPANS // 3)
    assert (3 * TURNS + 3) * HALF <= ITEMS_PAD
    SCORES, LOWS, ENDS, CARRY, LAST, DELTA, PROBS = 0, 128, 160, 192, 200, 201, 256
    STEPS = 8
    SCRAPS = 4
    GROUPS = [range(0, 3), range(3, 6), range(6, 9), range(9, HALF)]
    MOST = len(GROUPS[-1])
    with Stage(nc) as st:
        rel = st.sb("rel", [P, ITEMS_PAD], F32)
        block_row = st.sb("block_row", [1, ITEMS_PAD], I32)
        table = st.sb("table", [P, 3, HALF], F32)
        index = st.sb("index", [P, 3 * HALF], I32)
        rows = st.sb("rows", [P, 3 * HALF, 2 * DIM], F32)
        hot_t = st.sb("hot_t", [P, 2, MOST * P], BF16)
        hot_dst = st.sb("hot_dst", [P, 3 * HALF, P], F32)
        scaled_rows = st.sb("scaled_rows", [P, 3, HALF, W65], F32)
        scrap = st.sb("scrap", [P, SCRAPS, DIM], F32)
        picked = st.sb("picked", [P, 3, HALF], F32)
        cut = st.sb("cut", [HALF, 3, P], F32)
        cut_next = st.sb("cut_next", [HALF, 3, P], F32)
        off = st.sb("off", [HALF, 3, P], F32)
        val = st.sb("val", [HALF, P], F32)
        ahead = st.sb("ahead", [HALF, P], F32)
        back = st.sb("back", [HALF, P], F32)
        prob = st.sb("prob", [HALF, P], F32)
        lows = st.sb("lows", [HALF, 2], F32)
        carry = st.sb("carry", [HALF, 2], F32)
        beta_all = st.sb("beta_all", [HALF, 1], F32)
        lows_row = st.sb("lows_row", [1, 2, HALF], F32)
        ends_row = st.sb("ends_row", [1, 2, HALF], F32)
        into = st.sb("into", [1, 3, HALF + 1], F32)
        into_back = st.sb("into_back", [1, HALF + 1], F32)
        raised = st.sb("raised", [1, 1], F32)
        delta = st.sb("delta", [1, 1], F32)
        last_lane = st.sb("last_lane", [P, 1], F32)
        log_factor = st.sb("log_factor", [P, 1], F32)
        factor = st.sb("factor", [P, 1], F32)
        ps_t = st.ps("ps_t", [P, 2, BANK], F32)
        ps_dst = st.ps("ps_dst", [P, 2, BANK], F32)
        ps_sum = st.ps("ps_sum", [P, 2, BANK], F32)
        ps = st.ps("ps", [P, BANK], F32)
        tables_in, setup, first_steps, steps_done, index_set, hot_set = st.sems(
            "tables_in", "setup", "first_steps", "steps_done", "index_set", "hot_set")
        turned, turned_kept, looked_up, picks = st.sems("turned", "turned_kept", "looked_up", "picks")
        scaled, sum_done, sum_added = st.sems("scaled", "sum_done", "sum_added")
        scores_turned, ends_set, ends_turned, into_set, into_turned, shifted, exp_done, delta_set, prob_turned = st.sems(
            "scores_turned", "ends_set", "ends_turned", "into_set", "into_turned", "shifted", "exp_done", "delta_set",
            "prob_turned")
        prob_set, log_set, factor_set = st.sems("prob_set", "log_set", "factor_set")
        got = [st.sem(f"got{u}") for u in range(3 * HALF)]
        bits_in = [st.sem(f"bits_in{k}") for k in range(3)]
        table_in = [st.sem(f"table_in{k}") for k in range(3)]
        block = st.block()

        @block.sync
        def _(sp):
            for t, source in ((rel, s.i_rel), (block_row, s.block_x64.rearrange("(o a) b -> o (a b)", o=1))):
                sp.dma_start(t[:, :], source).then_inc(tables_in, 16)
            sp.dma_start(beta_all[:, :], beta.rearrange("(o k) -> o k", o=1).to_broadcast([HALF, 1])).then_inc(tables_in, 16)

            def load_table(n, slot):
                sp.dma_start(table[:, slot, :], s.i_row[:, bass.ds(n * HALF, HALF)]).then_inc(table_in[slot], 16)

            def load_bits(n, slot):
                span = HALF * P
                for t, first in ((cut, n * span), (cut_next, n * span + 1)):
                    sp.dma_start(t[:, slot, :], s.i_cut[bass.ds(first, span)].rearrange("(i e) -> i e", e=P)
                                 ).then_inc(bits_in[slot], 16)
                sp.dma_start(off[:, slot, :], s.i_off[bass.ds(n * HALF, HALF), :]).then_inc(bits_in[slot], 16)

            for slot in range(3):
                load_table(slot, slot)
            for slot in range(3):
                load_bits(slot, slot)
            with sp.Fori(0, TURNS) as turn:
                for slot in range(3):
                    n = turn * 3 + slot
                    sp.wait_ge(index_set, n + 1)
                    load_table(n + 3, slot)
                    sp.wait_ge(prob_set, n + 1)
                    load_bits(n + 3, slot)
            for slot in range(3):
                sp.wait_ge(table_in[slot], (TURNS + 1) * 16)
                sp.wait_ge(bits_in[slot], (TURNS + 1) * 48)

        @block.gpsimd
        def _(pool):
            def gather(n, slot):
                pool.wait_ge(index_set, n + 1)
                hold(pool, c)
                for u in range(slot * HALF, (slot + 1) * HALF):
                    pool.indirect_dma_start(rows[:, u, :], None, s.nx,
                                            bass.IndirectOffsetOnAxis(ap=index[:, u:u + 1], axis=0)).then_inc(got[u], 16)

            with pool.Fori(0, TURNS) as turn:
                for slot in range(3):
                    gather(turn * 3 + slot, slot)
            for slot in range(2):
                gather(3 * TURNS + slot, slot)

        @block.tensor
        def _(pe):
            ident = c.ident[0:HALF, 0:HALF]

            def load_blocks(first, count):
                return nc.values_load_multi_w_load_instructions(
                    block_row[0:1, bass.ds(first, count)], engines=PE_ONLY, min_val=0, max_val=(BLOCKS - 1) * DIM,
                    skip_runtime_bounds_check_because="the item map clamps the block")[1]

            def turn_hot(n, slot, g):
                pe.wait_ge(hot_set, n * HALF + GROUPS[g].stop)
                hold(pe, c)
                for k, i in enumerate(GROUPS[g]):
                    last = nc.tensor.transpose(ps_t[:, g % 2, k * P:(k + 1) * P], hot_dst[:, slot * HALF + i, :], c.ident[:, :])
                last.then_inc(turned, 1)

            def look_up(n, g, at):
                pe.wait_ge(turned_kept, n * len(GROUPS) + g + 1)
                pe.wait_ge(picks, n * HALF + (GROUPS[g - 2].stop if g >= 2 else 0))
                for k, i in enumerate(GROUPS[g]):
                    for part in range(3):
                        last = nc.tensor.matmul(ps_dst[:, g % 2, k * DIM:(k + 1) * DIM], hot_t[:, g % 2, k * P:(k + 1) * P],
                                                parts[:, part, bass.ds(at[i], DIM)], start=part == 0, stop=part == 2)
                last.then_inc(looked_up, 1)

            def sum_rows(n, slot, g):
                pe.wait_ge(scaled, n * HALF + GROUPS[g].stop)
                pe.wait_ge(sum_added, n * HALF + (GROUPS[g - 2].stop if g >= 2 else 0))
                for k, i in enumerate(GROUPS[g]):
                    last = nc.tensor.matmul(ps_sum[:, g % 2, k * W65:(k + 1) * W65], hot_dst[:, slot * HALF + i, :],
                                            scaled_rows[:, slot, i, :], start=True, stop=True)
                last.then_inc(sum_done, 1)

            def turn_scores(n, slot, first):
                pe.wait_ge(picks, (n + 1) * HALF)
                hold(pe, c)
                for k in range(2):
                    nc.tensor.transpose(ps[0:1, LOWS + k * HALF:LOWS + (k + 1) * HALF], lows[:, k:k + 1], ident)
                if not first:
                    nc.tensor.matmul(ps[:, LAST:LAST + 1], hot_dst[:, (slot + 2) % 3 * HALF + HALF - 1, :],
                                     c.ident[:, P - 1:P], start=True, stop=True)
                nc.tensor.transpose(ps[0:HALF, SCORES:SCORES + P], picked[:, slot, :], c.ident[:, :]).then_inc(scores_turned, 1)

            def turn_ends(n, slot, first):
                pe.wait_ge(ends_set, n + 1)
                hold(pe, c)
                nc.tensor.transpose(ps[0:1, ENDS:ENDS + HALF], ahead[:, P - 1:P], ident)
                nc.tensor.transpose(ps[0:1, ENDS + HALF:ENDS + 2 * HALF], back[:, 0:1], ident).then_inc(ends_turned, 1)

            def turn_into(n, slot, first):
                pe.wait_ge(into_set, n + 1)
                hold(pe, c)
                nc.tensor.transpose(ps[0:HALF, CARRY:CARRY + 1], into[0:1, slot, 0:HALF], c.ident[0:1, 0:1])
                nc.tensor.transpose(ps[0:HALF, CARRY + 1:CARRY + 2], into_back[0:1, 1:HALF + 1], c.ident[0:1, 0:1]
                                    ).then_inc(into_turned, 1)

            def turn_probs(n, slot, first):
                if not first:
                    pe.wait_ge(delta_set, n)
                    nc.tensor.matmul(ps[:, DELTA:DELTA + 1], c.ones[0:1, :], delta[0:1, 0:1], start=True, stop=True)
                pe.wait_ge(exp_done, n + 1)
                hold(pe, c)
                nc.tensor.transpose(ps[:, PROBS:PROBS + HALF], prob[:, :], ident).then_inc(prob_turned, 1)

            shift_steps = (turn_scores, turn_ends, turn_into, turn_probs)

            def span(b, slot, at, shift=True, sums=True):
                def shift_step(k):
                    if shift:
                        shift_steps[k](b + 1, (slot + 1) % 3, not sums)

                for g in range(len(GROUPS)):
                    turn_hot(b + 2, (slot + 2) % 3, g)
                    if sums:
                        sum_rows(b, slot, g)
                    shift_step(g)
                    look_up(b + 2, g, at)

            pe.wait_ge(tables_in, 48)
            pe.wait_ge(setup, 3)
            at = load_blocks(0, 2 * HALF)
            span(-2, 1, at[:HALF], shift=False, sums=False)
            span(-1, 2, at[HALF:], sums=False)
            with pe.Fori(0, TURNS) as turn:
                at = load_blocks(turn * (3 * HALF) + 2 * HALF, 2 * HALF) + load_blocks(turn * (3 * HALF) + 4 * HALF, HALF)
                for slot in range(3):
                    span(turn * 3 + slot, slot, at[slot * HALF:(slot + 1) * HALF])

        @block.scalar
        def _(act):
            def scale_rows(slot, items):
                for i in items:
                    nc.scalar.activation(scaled_rows[:, slot, i, 0:DIM], rows[:, slot * HALF + i, DIM:2 * DIM],
                                         ACT.Copy, scale=scaled_rows[:, slot, i, DIM:W65]).then_inc(scaled, 1)

            def span(b, slot, shift=True, sums=True):
                if sums:
                    act.wait_ge(prob_set, b + 1)
                for g, group in enumerate(GROUPS):
                    if sums:
                        scale_rows(slot, (GROUPS[0], range(GROUPS[1].start, GROUPS[2].stop), GROUPS[3], ())[g])
                    act.wait_ge(turned, (b + 2) * len(GROUPS) + g + 1)
                    size = len(group) * P
                    nc.scalar.copy(hot_t[:, g % 2, 0:size], ps_t[:, g % 2, 0:size]).then_inc(turned_kept, 1)
                    if shift and g == 2:
                        act.wait_ge(shifted, b + 2)
                        nc.scalar.activation(prob[:, :], val[:, :], ACT.Exp).then_inc(exp_done, 1)
                if sums:
                    act.wait_ge(log_set, b + 1)
                    nc.scalar.activation(factor[:, :], log_factor[:, :], ACT.Exp).then_inc(factor_set, 1)

            span(-2, 1, shift=False, sums=False)
            span(-1, 2, sums=False)
            with act.Fori(0, TURNS) as turn:
                for slot in range(3):
                    span(turn * 3 + slot, slot)

        @block.vector
        def _(dve):
            acc_rows = acc[:, :, :].rearrange("p b d -> p (b d)")

            def build(n, slot, i):
                nc.vector.tensor_scalar(hot_dst[:, slot * HALF + i, :], c.iota_b[:, :], rel[:, bass.ds(n * HALF + i, 1)],
                                        None, ALU.is_equal).then_inc(hot_set, 1)

            def set_index(n, uses, slot):
                dve.wait_ge(table_in[slot], uses * 16)
                nc.vector.tensor_copy(index[:, slot * HALF:(slot + 1) * HALF], table[:, slot, :]).then_inc(index_set, 1)

            def find_lows(n, uses, slot):
                dve.wait_ge(bits_in[slot], uses * 48)
                nc.vector.tensor_reduce(lows[:, 0:1], cut[:, slot, :], AX.X, ALU.min)
                nc.vector.tensor_reduce(lows[:, 1:2], cut_next[:, slot, :], AX.X, ALU.min)

            def pick(n, uses, slot, g):
                dve.wait_ge(looked_up, n * len(GROUPS) + g + 1)
                for k, i in enumerate(GROUPS[g]):
                    dve.wait_ge(got[slot * HALF + i], uses * 16)
                    if i >= SCRAPS:
                        dve.wait_ge(picks, n * HALF + i - SCRAPS + 1)
                    nc.vector.tensor_tensor_reduce(out=scrap[:, i % SCRAPS, :], in0=ps_dst[:, g % 2, k * DIM:(k + 1) * DIM],
                                                   in1=rows[:, slot * HALF + i, 0:DIM], scale=1.0, scalar=0.0, op0=ALU.mult,
                                                   op1=ALU.add, accum_out=picked[:, slot, i:i + 1]).then_inc(picks, 1)

            def add_sums(n, slot, g, at):
                dve.wait_ge(sum_done, n * len(GROUPS) + g + 1)
                for k, i in enumerate(GROUPS[g]):
                    dve.wait_ge(sum_added, n * HALF + i)
                    here = acc_rows[:, bass.ds(at[i], W65)]
                    nc.vector.tensor_tensor(here, here, ps_sum[:, g % 2, k * W65:(k + 1) * W65], ALU.add).then_inc(sum_added, 1)
                    build(n + 3, slot, i)

            def scan(out, cuts, values, start, reverse):
                step = slice(None, None, -1) if reverse else slice(None)
                return nc.vector.tensor_tensor_scan(out[:, step], cuts[:, step], values[:, step], start, ALU.add, ALU.max)

            def scan_items(n, slot, link, first):
                dve.wait_ge(scores_turned, n + 1)
                link(nc.vector.scalar_tensor_tensor(val[:, :], ps[0:HALF, SCORES:SCORES + P], beta_all[:, 0:1], off[:, slot, :],
                                                    ALU.mult, ALU.add))
                nc.vector.tensor_copy(lows_row[:, :, :], ps[0:1, LOWS:LOWS + 2 * HALF].rearrange("o (k i) -> o k i", k=2))
                if not first:
                    nc.vector.tensor_copy(last_lane[:, :], ps[:, LAST:LAST + 1])
                scan(ahead, cut[:, slot, :], val, -BIG, False)
                scan(back, cut_next[:, slot, :], val, -BIG, True).then_inc(ends_set, 1)

            def scan_ends(n, slot, link, first):
                dve.wait_ge(ends_turned, n + 1)
                link(nc.vector.tensor_copy(ends_row[:, :, :], ps[0:1, ENDS:ENDS + 2 * HALF].rearrange("o (k i) -> o k i", k=2)))
                scan(into[0:1, slot, 1:HALF + 1], lows_row[0:1, 0, :], ends_row[0:1, 0, :], into[0:1, slot, 0:1], False)
                link(scan(into_back[0:1, 0:HALF], lows_row[0:1, 1, :], ends_row[0:1, 1, :], -BIG, True))
                nc.vector.tensor_copy(into[0:1, (slot + 1) % 3, 0:1], into[0:1, slot, HALF:HALF + 1]).then_inc(into_set, 1)

            def find_shift(n, slot, link, first):
                dve.wait_ge(into_turned, n + 1)
                link(nc.vector.tensor_copy(carry[:, :], ps[0:HALF, CARRY:CARRY + 2]))
                scan(ahead, cut[:, slot, :], val, carry[:, 0:1], False)
                link(scan(back, cut_next[:, slot, :], val, carry[:, 1:2], True))
                link(nc.vector.tensor_tensor(back[:, :], back[:, :], ahead[:, :], ALU.max))
                nc.vector.tensor_tensor(val[:, :], val[:, :], back[:, :], ALU.subtract).then_inc(shifted, 1)
                if not first:
                    before = into[0:1, slot, 0:1]
                    link(nc.vector.scalar_tensor_tensor(raised[:, :], back[0:1, 0:1], cut[0:1, slot, 0:1], before,
                                                        ALU.add, ALU.max))
                    nc.vector.tensor_tensor(delta[:, :], before, raised[:, :], ALU.subtract).then_inc(delta_set, 1)

            def keep_probs(n, slot, link, first):
                dve.wait_ge(prob_turned, n + 1)
                if not first:
                    nc.vector.tensor_tensor(log_factor[:, :], ps[:, DELTA:DELTA + 1], last_lane[:, :], ALU.mult
                                            ).then_inc(log_set, 1)
                nc.vector.tensor_copy(scaled_rows[:, slot, :, DIM], ps[:, PROBS:PROBS + HALF]).then_inc(prob_set, 1)

            shift_steps = (scan_items, scan_ends, find_shift, keep_probs)

            def span(b, turn, slot, link, at=None, shift=True, sums=True):
                n, uses = b + 2, turn + (slot + 2) // 3 + 1

                def shift_step(k):
                    if shift:
                        shift_steps[k](b + 1, (slot + 1) % 3, link, not sums)

                for g in range(len(GROUPS)):
                    if g == 3:
                        shift_step(g)
                    if sums:
                        add_sums(b, slot, g, at)
                    if g < 3:
                        shift_step(g)
                    if sums and g == 2:
                        dve.wait_ge(scaled, (b + 1) * HALF)
                        set_index(b + 3, turn + 2, slot)
                    if g == len(GROUPS) - 1:
                        find_lows(n, uses, (slot + 2) % 3)
                    pick(n, uses, (slot + 2) % 3, g)
                if sums:
                    dve.wait_ge(factor_set, b + 1)
                    dve.wait_ge(sum_added, (b + 1) * HALF)
                    here = acc_rows[:, bass.ds(at[HALF - 1], W65)]
                    link(nc.vector.tensor_scalar(here, here, factor[:, 0:1], None, ALU.mult))

            nc.vector.memset(acc[:, :, :], 0.0).then_inc(setup, 1)
            nc.vector.memset(into[:, :, :], -BIG).then_inc(setup, 1)
            nc.vector.memset(into_back[:, :], -BIG).then_inc(setup, 1)
            dve.wait_ge(setup, 3)
            for slot in range(3):
                set_index(slot, 1, slot)
            dve.wait_ge(tables_in, 48)
            for n in range(3):
                for i in range(HALF):
                    build(n, n, i)
            dve.wait_ge(hot_set, 3 * HALF)
            span(-2, -1, 1, None, shift=False, sums=False)
            span(-1, -1, 2, link_on(dve, first_steps), sums=False)
            with dve.Fori(0, TURNS) as turn:
                def load_blocks(first, count):
                    return nc.values_load_multi_w_load_instructions(
                        c.block_row[0:1, bass.ds(turn * (3 * HALF) + first, count)], engines=DVE_ONLY, min_val=0,
                        max_val=(BLOCKS - 1) * W65, skip_runtime_bounds_check_because="the item map clamps the block")[1]

                for slot in range(3):
                    if slot != 1:
                        at = load_blocks(slot * HALF, (2 - slot // 2) * HALF)
                    steps = TurnCount(dve, steps_done, turn * 3 + slot, STEPS)
                    dve.wait_ge(hot_set, (turn * 3 + slot + 3) * HALF)
                    span(turn * 3 + slot, turn, slot, lambda i: steps.wait(steps.mark(i)),
                         at[slot % 2 * HALF:][:HALF])
                    steps.close()


def attention_update(nc, x, acc, h):
    with Stage(nc) as st:
        recip = st.sb("recip", [P, BLOCKS], F32)
        dve_done = st.sem("dve_done")
        block = st.block()

        @block.vector
        def _(dve):
            link = link_on(dve, dve_done)
            link(nc.vector.tensor_scalar(recip[:, :], acc[:, :, DIM], TINY, None, ALU.max))
            link(nc.vector.reciprocal(recip[:, :], recip[:, :]))
            link(nc.vector.tensor_tensor(h[:, :, :], acc[:, :, 0:DIM], recip[:, :, None].to_broadcast([P, BLOCKS, DIM]),
                                         ALU.mult))
            link(nc.vector.tensor_tensor(h[:, :, :], h[:, :, :], x[:, :, :], ALU.add))


def store_nodes(nc, x, out):
    with Stage(nc) as st:
        stored = st.sem("stored")
        block = st.block()
        full = NODES // P

        @block.sync
        def _(sp):
            sp.dma_start(out[0:full * P, :].rearrange("(b p) d -> p b d", p=P), x[:, 0:full, :]).then_inc(stored, 16)
            sp.dma_start(out[full * P:NODES, :], x[0:NODES - full * P, full, :]).then_inc(stored, 16)
            sp.wait_ge(stored, 32)


def graph_layers(nc, x_in, src, dst, edge_type, mean_weight, mean_bias, rel_weight, rel_root, rel_bias,
                 res_weight, res_bias, beta, out):
    with ExitStack() as ctx:
        Stage.made = 0
        c = Consts(nc, ctx)
        s = Scratch(nc)
        x = ctx.enter_context(nc.sbuf_tensor("x", [P, BLOCKS, DIM], F32))
        make_consts(nc, c)
        copy_edges(nc, s, src, dst, edge_type)
        sort_edges(nc, s, c, src, dst, edge_type)
        item_tables(nc, s, c)
        tile_tables(nc, s, c)
        load_nodes(nc, x, x_in)
        mean_layer(nc, s, c, x, mean_weight, mean_bias)
        max_layer(nc, s, c, x)
        relational_layer(nc, s, c, x, rel_weight, rel_root, rel_bias, res_weight, res_bias)
        attention_layer(nc, s, c, x, beta)
        store_nodes(nc, x, out)


_INS = ["x", "src", "dst", "edge_type_65", "L0_gnn_weight", "L0_gnn_bias", "L2_gnn_W", "L2_gnn_root", "L2_gnn_bias",
        "L2_gnn_res_W", "L2_gnn_res_b", "L3_gnn_beta"]


def kernel(**inputs):
    import concourse.bacc as bacc
    from concourse.bass_utils import run_bass_kernel_spmd

    nc = bacc.Bacc("TRN2", target_bir_lowering=False, num_devices=1)
    arrays, args = {}, []
    for name in _INS:
        a = np.ascontiguousarray(inputs[name])
        arrays[f"in_{name}"] = a
        args.append(nc.dram_tensor(f"in_{name}", a.shape, mybir.dt.from_np(a.dtype), kind="ExternalInput").ap())
    out = nc.dram_tensor("out_x", (NODES, DIM), F32, kind="ExternalOutput").ap()
    graph_layers(nc, *args, out)
    return run_bass_kernel_spmd(nc, [arrays], core_ids=[0]).results[0]["out_x"]
```
